# Optimizing a Trainium2 kernel written in Bass

```python
import numpy as np
import jax
import jax.numpy as jnp

def _softmax(x, axis=-1):
    return jax.nn.softmax(x, axis=axis)

def _gelu(x):
    return jax.nn.gelu(x, approximate=True)

def _silu(x):
    return jax.nn.silu(x)

def _sigmoid(x):
    return jax.nn.sigmoid(x)

def _layernorm(x, axis=-1, eps=1e-05):
    m = jnp.mean(x, axis=axis, keepdims=True)
    v = jnp.var(x, axis=axis, keepdims=True)
    return (x - m) / jnp.sqrt(v + eps)

def _scatter_add(tgt, idx, src, axis=0):
    return tgt.at[idx].add(src)

def _segment_sum(src, seg, n):
    return jax.ops.segment_sum(src, seg, n)
kernel_name = 'mk_adaln_ffn_d2_seqx_r8_9e7c70'

def setup_inputs(seed: int=0):
    np.random.seed(seed)
    _w = jnp.asarray

    def _rec_inputs():
        import jax
        import jax.numpy as jnp
        _rk = jax.random.key(seed)
        x = -7.109e-05 + 0.9999 * jax.random.normal(jax.random.fold_in(_rk, 1), (32, 32, 256), jnp.float32)
        _lenS = 32 - jax.random.randint(jax.random.fold_in(_rk, 7), (32,), 0, max(1, 32 // 4) + 1, jnp.int32)
        _lenS2 = 32 - jax.random.randint(jax.random.fold_in(_rk, 8), (32,), 0, max(1, 32 // 4) + 1, jnp.int32)
        itok_B_1_198 = jax.random.randint(jax.random.fold_in(_rk, 11), (32,), 1, 199, jnp.int32)
        itok_B_0_7 = jax.random.randint(jax.random.fold_in(_rk, 12), (32,), 0, 8, jnp.int32)
        return (x, itok_B_1_198, itok_B_0_7)
    x, itok_B_1_198, itok_B_0_7 = _rec_inputs()

    def _L0_cond_setup():
        import jax, jax.numpy as jnp
        import numpy as np
        B, C, T = (128, 32, 256)
        S, D = (200, 32)
        key = jax.random.key(seed)
        k1, k2, k3 = jax.random.split(key, 3)
        x = jax.random.normal(k1, (B, C, T), dtype=jnp.float32)
        conditions = jax.random.randint(k2, (B,), 0, S, dtype=jnp.int64)
        weights = jax.random.normal(k3, (S, C, D), dtype=jnp.float32) / jnp.sqrt(jnp.float32(C))
        return {'x': x, 'conditions': conditions, 'weights': weights}
    _L0_cond_all = _L0_cond_setup()
    _L0_cond_in = {k: v for k, v in _L0_cond_all.items() if k in ('weights',)}
    del _L0_cond_all

    def _L0_ffn_setup():
        import jax, jax.numpy as jnp
        import numpy as np
        D = 256
        H = 16
        KV = 4
        DH = 128
        RD = 64
        E = 8
        TOPK = 2
        I = 128
        EPS = 1e-06
        THETA = 1000000.0

        def rmsnorm(h, w, eps=EPS):
            dt = h.dtype
            h32 = h.astype(jnp.float32)
            var = jnp.mean(h32 * h32, axis=-1, keepdims=True)
            return (w * (h32 * jax.lax.rsqrt(var + eps))).astype(dt)

        def rotate_half(t):
            half = t.shape[-1] // 2
            return jnp.concatenate([-t[..., half:], t[..., :half]], axis=-1)
        key = jax.random.key(seed)
        ks = jax.random.split(key, 16)
        s = lambda k, shape, sc: jax.random.normal(k, shape, dtype=jnp.float32) * sc
        B, S = (1, 256)
        return {'x': s(ks[0], (B, S, D), 1.0), 'ln1_w': jnp.ones((D,), jnp.float32), 'ln2_w': jnp.ones((D,), jnp.float32), 'wq': s(ks[1], (D, H * DH), 0.02), 'wk': s(ks[2], (D, KV * DH), 0.02), 'wv': s(ks[3], (D, KV * DH), 0.02), 'wo': s(ks[4], (H * DH, D), 0.02), 'qnorm_w': jnp.ones((H * DH,), jnp.float32), 'knorm_w': jnp.ones((KV * DH,), jnp.float32), 'router_w': s(ks[5], (D, E), 0.02), 'router_bias': s(ks[6], (E,), 0.1), 'wg': s(ks[7], (E, D, I), 0.02), 'wu': s(ks[8], (E, D, I), 0.02), 'wd': s(ks[9], (E, I, D), 0.02)}
    _L0_ffn_all = _L0_ffn_setup()
    _L0_ffn_in = {k: v for k, v in _L0_ffn_all.items() if k in ('ln1_w', 'ln2_w', 'wq', 'wk', 'wv', 'wo', 'qnorm_w', 'knorm_w', 'router_w', 'router_bias', 'wg', 'wu', 'wd')}
    del _L0_ffn_all

    def _L1_cond_setup():
        import jax, jax.numpy as jnp
        import numpy as np
        B, C, D, T, N_SUBJECTS = (128, 32, 32, 256, 8)
        key = jax.random.key(seed)
        kx, ks, kw = jax.random.split(key, 3)
        x = jax.random.normal(kx, (B, C, T), dtype=jnp.float32)
        subjects = jax.random.randint(ks, (B,), 0, N_SUBJECTS, dtype=jnp.int64)
        weights = jax.random.normal(kw, (N_SUBJECTS, C, D), dtype=jnp.float32) * (1.0 / C ** 0.5)
        return {'x': x, 'subjects': subjects, 'weights': weights}
    _L1_cond_all = _L1_cond_setup()
    _L1_cond_in = {k: v for k, v in _L1_cond_all.items() if k in ('weights',)}
    del _L1_cond_all

    def _L1_ffn_setup():
        import jax, jax.numpy as jnp
        import numpy as np
        TOP_K = 4
        key = jax.random.key(seed)
        ks = jax.random.split(key, 9)
        B, T, D, H, NE = (2, 128, 256, 176, 16)
        s = 0.02
        return {'x': jax.random.normal(ks[0], (B, T, D), jnp.float32), 'gate_w': jax.random.normal(ks[1], (NE, D), jnp.float32) * s, 'gate_b': jax.random.normal(ks[2], (NE,), jnp.float32) * s, 'w1_shared': jax.random.normal(ks[3], (D, H), jnp.float32) * s, 'w2_shared': jax.random.normal(ks[4], (H, D), jnp.float32) * s, 'w3_shared': jax.random.normal(ks[5], (D, H), jnp.float32) * s, 'w1_routed': jax.random.normal(ks[6], (NE, D, H), jnp.float32) * s, 'w2_routed': jax.random.normal(ks[7], (NE, H, D), jnp.float32) * s, 'w3_routed': jax.random.normal(ks[8], (NE, D, H), jnp.float32) * s}
    _L1_ffn_all = _L1_ffn_setup()
    _L1_ffn_in = {k: v for k, v in _L1_ffn_all.items() if k in ('gate_w', 'gate_b', 'w1_shared', 'w2_shared', 'w3_shared', 'w1_routed', 'w2_routed', 'w3_routed')}
    del _L1_ffn_all
    return {'x': x, 'itok_B_1_198': itok_B_1_198, 'itok_B_0_7': itok_B_0_7, 'L0_cond_weights': _L0_cond_in['weights'], 'L0_ffn_ln1_w': _L0_ffn_in['ln1_w'], 'L0_ffn_ln2_w': _L0_ffn_in['ln2_w'], 'L0_ffn_wq': _L0_ffn_in['wq'], 'L0_ffn_wk': _L0_ffn_in['wk'], 'L0_ffn_wv': _L0_ffn_in['wv'], 'L0_ffn_wo': _L0_ffn_in['wo'], 'L0_ffn_qnorm_w': _L0_ffn_in['qnorm_w'], 'L0_ffn_knorm_w': _L0_ffn_in['knorm_w'], 'L0_ffn_router_w': _L0_ffn_in['router_w'], 'L0_ffn_router_bias': _L0_ffn_in['router_bias'], 'L0_ffn_wg': _L0_ffn_in['wg'], 'L0_ffn_wu': _L0_ffn_in['wu'], 'L0_ffn_wd': _L0_ffn_in['wd'], 'L1_cond_weights': _L1_cond_in['weights'], 'L1_ffn_gate_w': _L1_ffn_in['gate_w'], 'L1_ffn_gate_b': _L1_ffn_in['gate_b'], 'L1_ffn_w1_shared': _L1_ffn_in['w1_shared'], 'L1_ffn_w2_shared': _L1_ffn_in['w2_shared'], 'L1_ffn_w3_shared': _L1_ffn_in['w3_shared'], 'L1_ffn_w1_routed': _L1_ffn_in['w1_routed'], 'L1_ffn_w2_routed': _L1_ffn_in['w2_routed'], 'L1_ffn_w3_routed': _L1_ffn_in['w3_routed']}

def reference(x, itok_B_1_198, itok_B_0_7, L0_cond_weights, L0_ffn_ln1_w, L0_ffn_ln2_w, L0_ffn_wq, L0_ffn_wk, L0_ffn_wv, L0_ffn_wo, L0_ffn_qnorm_w, L0_ffn_knorm_w, L0_ffn_router_w, L0_ffn_router_bias, L0_ffn_wg, L0_ffn_wu, L0_ffn_wd, L1_cond_weights, L1_ffn_gate_w, L1_ffn_gate_b, L1_ffn_w1_shared, L1_ffn_w2_shared, L1_ffn_w3_shared, L1_ffn_w1_routed, L1_ffn_w2_routed, L1_ffn_w3_routed):
    import jax
    import jax.numpy as jnp

    def _L0_cond_ref(x, conditions, weights):
        import jax, jax.numpy as jnp
        import numpy as np
        B, C, T = (128, 32, 256)
        S, D = (200, 32)
        w = weights[conditions]
        return jnp.einsum('bct,bcd->bdt', x, w)

    def _L0_ffn_ref(x, ln1_w, ln2_w, wq, wk, wv, wo, qnorm_w, knorm_w, router_w, router_bias, wg, wu, wd):
        import jax, jax.numpy as jnp
        import numpy as np
        D = 256
        H = 16
        KV = 4
        DH = 128
        RD = 64
        E = 8
        TOPK = 2
        I = 128
        EPS = 1e-06
        THETA = 1000000.0

        def rmsnorm(h, w, eps=EPS):
            dt = h.dtype
            h32 = h.astype(jnp.float32)
            var = jnp.mean(h32 * h32, axis=-1, keepdims=True)
            return (w * (h32 * jax.lax.rsqrt(var + eps))).astype(dt)

        def rotate_half(t):
            half = t.shape[-1] // 2
            return jnp.concatenate([-t[..., half:], t[..., :half]], axis=-1)
        B, S, _ = x.shape
        res = x
        h = rmsnorm(x, ln1_w)
        q = h @ wq
        k = h @ wk
        v = h @ wv
        q = rmsnorm(q, qnorm_w)
        k = rmsnorm(k, knorm_w)
        q = q.reshape(B, S, H, DH).transpose(0, 2, 1, 3)
        k = k.reshape(B, S, KV, DH).transpose(0, 2, 1, 3)
        v = v.reshape(B, S, KV, DH).transpose(0, 2, 1, 3)
        pos = jnp.arange(S, dtype=jnp.float32)
        inv_freq = 1.0 / THETA ** (jnp.arange(0, RD, 2, dtype=jnp.float32) / RD)
        ang = pos[:, None] * inv_freq[None, :]
        emb = jnp.concatenate([ang, ang], axis=-1)
        cos, sin = (jnp.cos(emb), jnp.sin(emb))

        def rope(t):
            rot, pas = (t[..., :RD], t[..., RD:])
            rot = rot * cos + rotate_half(rot) * sin
            return jnp.concatenate([rot, pas], axis=-1)
        q, k = (rope(q), rope(k))
        rep = H // KV
        k = jnp.repeat(k, rep, axis=1)
        v = jnp.repeat(v, rep, axis=1)
        scores = jnp.einsum('bhqd,bhkd->bhqk', q, k) / np.sqrt(DH)
        causal = jnp.tril(jnp.ones((S, S), dtype=bool))
        scores = jnp.where(causal, scores, jnp.finfo(jnp.float32).min)
        attn = jax.nn.softmax(scores.astype(jnp.float32), axis=-1).astype(q.dtype)
        o = jnp.einsum('bhqk,bhkd->bhqd', attn, v)
        o = o.transpose(0, 2, 1, 3).reshape(B, S, H * DH) @ wo
        x1 = res + o
        h2 = rmsnorm(x1, ln2_w)
        t = h2.reshape(-1, D)
        T = t.shape[0]
        logits = t.astype(jnp.float32) @ router_w
        sig = jax.nn.sigmoid(logits)
        _, topi = jax.lax.top_k(sig + router_bias, TOPK)
        aff = jnp.take_along_axis(sig, topi, axis=-1)
        aff = aff / jnp.sum(aff, axis=-1, keepdims=True)
        combine = jnp.zeros((T, E), jnp.float32).at[jnp.arange(T)[:, None], topi].set(aff)
        gate = jnp.einsum('td,edi->tei', t, wg)
        up = jnp.einsum('td,edi->tei', t, wu)
        act = jax.nn.silu(gate) * up
        moe = jnp.einsum('te,tei,eid->td', combine.astype(t.dtype), act, wd)
        return x1 + moe.reshape(B, S, D)

    def _L1_cond_ref(x, subjects, weights):
        import jax, jax.numpy as jnp
        import numpy as np
        B, C, D, T, N_SUBJECTS = (128, 32, 32, 256, 8)
        w = weights[subjects]
        out = jnp.einsum('bct,bcd->bdt', x, w)
        return out

    def _L1_ffn_ref(x, gate_w, gate_b, w1_shared, w2_shared, w3_shared, w1_routed, w2_routed, w3_routed):
        import jax, jax.numpy as jnp
        import numpy as np
        TOP_K = 4
        n_experts = w1_routed.shape[0]
        logits = jnp.einsum('ed,btd->bte', gate_w, x)
        scores = jax.nn.sigmoid(logits) + gate_b
        weights, indices = jax.lax.top_k(scores, TOP_K)
        weights = weights / weights.sum(-1, keepdims=True)
        shared_out = jax.nn.silu(x @ w1_shared) * (x @ w3_shared) @ w2_shared
        one_hot = jax.nn.one_hot(indices, n_experts, dtype=x.dtype)
        router_probs = (weights[..., None] * one_hot).sum(-2)
        h1 = jnp.einsum('btd,edc->btec', x, w1_routed)
        h2 = jnp.einsum('btd,edc->btec', x, w3_routed)
        h3 = jax.nn.silu(h1 * h2)
        experts_out = jnp.einsum('btec,ecd->bted', h3, w2_routed)
        routed_out = jnp.einsum('bted,bte->btd', experts_out, router_probs)
        return shared_out + routed_out
    x = x + _L0_ffn_ref(_L0_cond_ref(x, itok_B_1_198, L0_cond_weights), L0_ffn_ln1_w, L0_ffn_ln2_w, L0_ffn_wq, L0_ffn_wk, L0_ffn_wv, L0_ffn_wo, L0_ffn_qnorm_w, L0_ffn_knorm_w, L0_ffn_router_w, L0_ffn_router_bias, L0_ffn_wg, L0_ffn_wu, L0_ffn_wd)
    x = x + _L1_ffn_ref(_L1_cond_ref(x, itok_B_0_7, L1_cond_weights), L1_ffn_gate_w, L1_ffn_gate_b, L1_ffn_w1_shared, L1_ffn_w2_shared, L1_ffn_w3_shared, L1_ffn_w1_routed, L1_ffn_w2_routed, L1_ffn_w3_routed)
    return x

_drawn_inputs = setup_inputs


def setup_inputs(seed=0):
    import zlib

    import numpy as np

    out = dict(_drawn_inputs(seed))
    spreads = {'L0_ffn_ln1_w': (1.0, 0.538),
     'L0_ffn_ln2_w': (1.0, 0.6),
     'L0_ffn_qnorm_w': (1.0, 0.6),
     'L0_ffn_knorm_w': (1.0, 0.6)}
    factors = {'L0_ffn_router_w': 8.0,
     'L0_ffn_router_bias': 8.0,
     'L0_ffn_wg': 8.0,
     'L0_ffn_wu': 8.0,
     'L0_ffn_wd': 8.0,
     'L1_ffn_gate_w': 6.082,
     'L1_ffn_gate_b': 8.0,
     'L1_ffn_w1_routed': 5.3,
     'L1_ffn_w2_routed': 5.176,
     'L1_ffn_w3_routed': 5.276,
     'L1_ffn_w1_shared': 4.848,
     'L1_ffn_w2_shared': 4.086,
     'L1_ffn_w3_shared': 4.08}
    for name, (base, spread) in spreads.items():
        noise = np.random.default_rng([zlib.crc32(name.encode()), seed]).standard_normal(out[name].shape)
        drawn = base * np.exp(spread * noise) if base else spread * noise
        out[name] = jnp.asarray(drawn.astype(out[name].dtype))
    for name, factor in factors.items():
        out[name] = (out[name] * factor).astype(out[name].dtype)
    return out
```

```python
import concourse.bass as bass
from concourse import mybir
from contextlib import ExitStack

F32 = mybir.dt.float32
F32R = mybir.dt.float32r
BF16 = mybir.dt.bfloat16
I32 = mybir.dt.int32
ALU = mybir.AluOpType
ACT = mybir.ActivationFunctionType
AX = mybir.AxisListType

P = 128
BANK = 512



def adaln_moe_program(nc, x, idx0, idx1, cw0, ln1_w, ln2_w, wq, wk, wv, wo, qn_w, kn_w,
                      router_w, router_b, wg, wu, wd, cw1, gate_w, gate_b,
                      w1s, w2s, w3s, w1r, w2r, w3r,
                      c_ident, c_identb, c_mask, c_cos, c_sin, c_sel0, c_sel1, out):
    B, C, D = x.shape
    BT = P // C
    T = B // BT
    NT = B * C
    KD = D // P
    DH = 128
    H = wq.shape[1] // DH
    KV = wk.shape[1] // DH
    REP = H // KV
    HALF = 32
    E0 = router_w.shape[1]
    E1 = gate_w.shape[0]
    HID = w1r.shape[2]
    NR = E1 * HID // P
    NS = -(-HID // P)
    HREM = HID - P
    NH = NT // BANK
    EPS = 1e-6
    SCALE = float(DH) ** -0.5
    QK = H + KV
    NPIECE = (H + 2 * KV) * DH // BANK
    NWO = H * D // 1024
    TOPK0, TOPK1 = 2, 4

    x_v = x.rearrange("(t a) c d -> (a c) t d", a=BT)
    out_v = out.rearrange("(t a) c d -> (a c) t d", a=BT)

    top = ExitStack()
    with top:
        def sb(name, shape, dt=F32, ctx=top):
            return ctx.enter_context(nc.sbuf_tensor(name, shape, dt))

        def sem(name):
            return top.enter_context(nc.semaphore(name))

        bank = [top.enter_context(nc.psum_tensor(f"bank{i}", [P, BANK], F32)) for i in range(1)]
        qbanks = top.enter_context(nc.psum_tensor("qbanks", [P, 4, BANK], F32))
        bank += [top.enter_context(nc.psum_tensor(f"bank{i}", [P, BANK], F32)) for i in range(1, 4)]

        xin = sb("xin", [P, T, D])
        x1 = sb("x1", [P, T, D])
        wbd0 = sb("wbd0", [P, T, P])
        wbd1 = sb("wbd1", [P, T, P])
        ident = sb("ident", [P, P])
        identb = sb("identb", [P, P], BF16)
        idx = sb("idx", [1, 2, B], I32)
        lnw = sb("lnw", [P, 2, KD])
        rbias = sb("rbias", [P, E0])
        gbias = sb("gbias", [P, E1])
        ssq = sb("ssq", [P, T])
        rms = sb("rms", [P, T])
        mhalf = sb("mhalf", [P, T])
        rw = sb("rw", [P, KD, E0])
        rw_h = sb("rw_h", [P, KD, E0], F32R)
        rw_l = sb("rw_l", [P, KD, E0], F32R)
        gwr = sb("gwr", [E1, D])
        gw_h = sb("gw_h", [P, KD, E1], F32R)
        gw_l = sb("gw_l", [P, KD, E1], F32R)

        ph1 = ExitStack()
        wstage = sb("wstage", [P, 3, 1024], F32, ph1)
        wqkv_h = sb("wqkv_h", [P, NPIECE, KD, BANK], F32R, ph1)
        wqkv_l = sb("wqkv_l", [P, NPIECE, KD, BANK], F32R, ph1)
        wo_h = sb("wo_h", [P, H, D], F32R, ph1)
        wo_l = sb("wo_l", [P, H, D], F32R, ph1)
        mask = sb("mask", [P, C], F32, ph1)
        cosT = sb("cosT", [P, 2 * HALF], F32, ph1)
        sinT = sb("sinT", [P, 2 * HALF], F32, ph1)
        wa = sb("wa", [P, QK, DH], F32, ph1)
        wb = sb("wb", [P, QK, 2 * HALF], F32, ph1)
        hn = sb("hn", [P, D], F32, ph1)
        hT_h = sb("hT_h", [P, KD, P], F32R, ph1)
        hT_l = sb("hT_l", [P, KD, P], F32R, ph1)
        qk = sb("qk", [P, QK, DH], F32, ph1)
        rot = sb("rot", [P, QK, 2 * HALF], F32, ph1)
        junk = sb("junk", [P, H * DH], BF16, ph1)
        qkss = sb("qkss", [P, 2], F32, ph1)
        qkr = sb("qkr", [P, 2], F32, ph1)
        qT_h = sb("qT_h", [P, BT, KV, REP, C], F32R, ph1)
        qT_l = sb("qT_l", [P, BT, KV, REP, C], F32R, ph1)
        kT_h = sb("kT_h", [P, KV, BT, C], F32R, ph1)
        kT_l = sb("kT_l", [P, KV, BT, C], F32R, ph1)
        v_h = sb("v_h", [P, KV * DH], F32R, ph1)
        v_l = sb("v_l", [P, KV * DH], F32R, ph1)
        sm = sb("sm", [P, KV * BT, C], F32, ph1)
        smax = sb("smax", [P, KV * BT], F32, ph1)
        prob = sb("prob", [P, KV * BT, C], F32, ph1)
        psm = sb("psm", [P, KV * BT], F32, ph1)
        pT_h = sb("pT_h", [P, KV, P], F32R, ph1)
        pT_l = sb("pT_l", [P, KV, P], F32R, ph1)
        oT_h = sb("oT_h", [P, H, BT, C], F32R, ph1)
        oT_l = sb("oT_l", [P, H, BT, C], F32R, ph1)
        ph1.close()

        ph2 = ExitStack()
        wg_s = sb("wg_s", [P, E0, KD, P], F32, ph2)
        wu_s = sb("wu_s", [P, E0, KD, P], F32, ph2)
        wd_s = sb("wd_s", [P, E0, D], F32, ph2)
        w1_s = sb("w1_s", [P, KD, (NR + NS) * P], F32, ph2)
        w3_s = sb("w3_s", [P, KD, (NR + NS) * P], F32, ph2)
        w2_s = sb("w2_s", [P, NR + NS, D], F32, ph2)
        sel0 = sb("sel0", [P, E0, P], BF16, ph2)
        sel1 = sb("sel1", [P, NR + NS, P], BF16, ph2)
        featT_h = sb("featT_h", [P, KD, NT], F32R, ph2)
        featT_l = sb("featT_l", [P, KD, NT], F32R, ph2)
        outT = sb("outT", [P, KD, NT], F32, ph2)
        hn2 = outT[:, :, :].rearrange("p k n -> p (k n)").rearrange("p (t d) -> p t d", d=D)
        combT = sb("combT", [P, NT], BF16, ph2)
        wA_h = [sb(f"wA_h{i}", [P, KD, P], F32R, ph2) for i in range(2)]
        wA_l = [sb(f"wA_l{i}", [P, KD, P], F32R, ph2) for i in range(2)]
        wB_h = [sb(f"wB_h{i}", [P, KD, P], F32R, ph2) for i in range(2)]
        wB_l = [sb(f"wB_l{i}", [P, KD, P], F32R, ph2) for i in range(2)]
        wC_h = [sb(f"wC_h{i}", [P, D], F32R, ph2) for i in range(2)]
        wC_l = [sb(f"wC_l{i}", [P, D], F32R, ph2) for i in range(2)]
        gate_s = sb("gate_s", [P, BANK], F32, ph2)
        prod = sb("prod", [P, 2, BANK], F32, ph2)
        act = sb("act", [P, 2, BANK], F32, ph2)
        act_h = sb("act_h", [P, 4, BANK], F32R, ph2)
        act_l = sb("act_l", [P, 4, BANK], F32R, ph2)
        EM = max(E0, E1)
        sig = sb("sig", [P, T * EM], F32, ph2)
        score = sb("score", [P, T * EM], F32, ph2)
        top8 = sb("top8", [P, T, 8], F32, ph2)
        gt = sb("gt", [P, T * EM], F32, ph2)
        eq = sb("eq", [P, T * EM], F32, ph2)
        scanA = sb("scanA", [P, T, 2 * EM], F32, ph2)
        scanB = sb("scanB", [P, T, 2 * EM], F32, ph2)
        rows = sb("rows", [P, 2, T], F32, ph2)
        comb = sb("comb", [P, T * EM], F32, ph2)
        comb3 = sb("comb3", [P, T, 3 * EM + 2], BF16, ph2)
        ph2.close()

        s_x = sem("x_loaded")
        s_idx = sem("idx_loaded")
        s_cst = sem("consts_loaded")
        s_cst2 = sem("router_loaded")
        s_sel = sem("sel_loaded")
        s_wst = [sem(f"stage_loaded{i}") for i in range(3)]
        s_wbd0 = sem("cond0_loaded")
        s_wbd1 = sem("cond1_loaded")
        s_zero = sem("wbd_zeroed")
        s_wh = sem("stage_high")
        s_wl = sem("stage_low")
        s_wtab = sem("rope_tables")
        s_c0 = sem("cond0_rows")
        s_res = sem("cond0_copied")
        s_ssq = sem("squares_summed")
        s_ms = sem("mean_squares")
        s_rms = sem("rms_ready")
        s_hn = sem("hn_ready")
        s_hT = sem("hT_transposed")
        s_hTh = sem("hT_high")
        s_hTl = sem("hT_low")
        s_k = sem("k_ready")
        s_v = sem("v_ready")
        s_q = sem("q_ready")
        s_kss = sem("k_squares")
        s_qss = sem("q_squares")
        s_kms = sem("k_mean")
        s_qms = sem("q_mean")
        s_kr = sem("k_rms")
        s_qr = sem("q_rms")
        s_kpost = sem("k_scaled")
        s_qpost = sem("q_scaled")
        s_krot = sem("k_rotated")
        s_qrot = sem("q_rotated")
        s_vh = sem("v_high")
        s_vl = sem("v_low")
        s_tr = sem("qk_transposed")
        s_trh = sem("qkT_high")
        s_trl = sem("qkT_low")
        s_sc = sem("scores_ready")
        s_sm = sem("scores_masked")
        s_mx = sem("scores_max")
        s_sub = sem("scores_less_max")
        s_exp = sem("exp_done")
        s_sum2 = sem("exp_sums")
        s_sum = sem("exp_sums_inverted")
        s_p = sem("probs_ready")
        s_pT = sem("pT_transposed")
        s_pTh = sem("pT_high")
        s_pTl = sem("pT_low")
        s_o = sem("oT_ready")
        s_oh = sem("oT_high")
        s_ol = sem("oT_low")
        s_wo = sem("wo_done")
        s_x1 = sem("x1_ready")
        s_dve = sem("dve_chain")
        s_pool = sem("pool_chain")
        s_w0 = [sem(f"moe0_w_loaded{i}") for i in range(2)]
        s_w1 = [sem("moe1_w_loaded")]
        s_pad = sem("shared_padding_zeroed")
        s_hn2 = sem("hn2_ready")
        s_x2 = sem("x2_ready")
        s_fT = [sem(f"featT_transposed{i}") for i in range(2)]
        s_fTh = [sem(f"featT_high{i}") for i in range(2)]
        s_fTl = [sem(f"featT_low{i}") for i in range(2)]
        s_gwT = sem("gate_w_transposed")
        s_rwh = sem("router_w_high")
        s_rwl = sem("router_w_low")
        s_lg = [sem(f"logits{i}") for i in range(2)]
        s_sig = [sem(f"sigmoid{i}") for i in range(2)]
        s_cb3 = [sem(f"comb_parts{i}") for i in range(2)]
        s_cbT = [sem(f"combT_transposed{i}") for i in range(2)]
        s_cbc = [sem(f"combT_copied{i}") for i in range(2)]
        s_cz = sem("combT_zeroed")
        s_wsh = [sem(f"chunk_w_high{i}") for i in range(2)]
        s_wsl = [sem(f"chunk_w_low{i}") for i in range(2)]
        s_G = [sem(f"gate_ready{i}") for i in range(2)]
        s_U = [sem(f"up_ready{i}") for i in range(2)]
        s_BC = [sem(f"weight_rows_ready{i}") for i in range(2)]
        s_fst = [sem(f"first_ready{i}") for i in range(2)]
        s_prd = [sem(f"product_ready{i}") for i in range(2)]
        s_sil = [sem(f"silu_ready{i}") for i in range(2)]
        s_act = [sem(f"act_ready{i}") for i in range(2)]
        s_ah = [sem(f"act_high{i}") for i in range(2)]
        s_al = [sem(f"act_low{i}") for i in range(2)]
        s_D = [sem(f"down_done{i}") for i in range(2)]
        s_mx0 = [sem(f"mixture_copied{i}") for i in range(2)]
        s_xs = sem("residual_summed")
        s_bk = [sem(f"rows_back{i}") for i in range(2)]
        s_fin = sem("out_rows_ready")
        s_out = sem("out_stored")

        block = top.enter_context(nc.Block())

        qv = qbanks[:, :, :].rearrange("p b n -> p (b n)")
        bT, bK, bV, bP = bank[0], bank[1], bank[2], bank[3]
        tr_bank = [bP, bK, bV, bP, bK]
        NTR = len(tr_bank)

        moes = [dict(sems=s_w0, runs=[(0, E0, True)], E=E0, K=TOPK0, sel=sel0),
                dict(sems=s_w1, runs=[(0, NR, False), (NR, NS, True)], E=E1, K=TOPK1, sel=sel1)]

        def chunk_weights(m, c):
            if m == 0:
                return (wg_s[:, bass.ds(c, 1), :, :].rearrange("p a k n -> p (a k) n"),
                        wu_s[:, bass.ds(c, 1), :, :].rearrange("p a k n -> p (a k) n"),
                        wd_s[:, bass.ds(c, 1), :].rearrange("p a n -> p (a n)"))
            return (w1_s[:, :, bass.ds(c * P, P)], w3_s[:, :, bass.ds(c * P, P)],
                    w2_s[:, bass.ds(c, 1), :].rearrange("p a n -> p (a n)"))

        @block.sync
        def _(sp):
            sp.dma_start(idx[:, 0, :], idx0.rearrange("(a n) -> a n", a=1)).then_inc(s_idx, 16)
            sp.dma_start(idx[:, 1, :], idx1.rearrange("(a n) -> a n", a=1)).then_inc(s_idx, 16)
            sp.dma_start(xin[:], x_v).then_inc(s_x, 16)

            def piece(n):
                if n < NPIECE:
                    src = [wk, wv][n] if n < 2 else wq[:, (n - 2) * BANK:(n - 1) * BANK]
                    return src.rearrange("(k p) n -> p k n", p=P), "p (k n) -> p k n", dict(k=KD)
                h = (n - NPIECE) * 4
                return (wo[h * DH:(h + 4) * DH, :].rearrange("(h p) n -> p h n", p=P),
                        "p (h n) -> p h n", dict(h=4))

            def load_piece(n):
                if n >= 3:
                    sp.wait_ge(s_wl, n - 2)
                src, how, kw = piece(n)
                sp.dma_start(wstage[:, n % 3, :].rearrange(how, **kw), src).then_inc(s_wst[n % 3], 16)

            for n in range(3):
                load_piece(n)
            sp.wait_ge(s_idx, 32)
            sp.wait_ge(s_zero, 2)
            with sp.Fori(0, T) as t:
                for a in range(BT):
                    r = sp.value_load(idx[0:1, 0, bass.ds(t * BT + a, 1)], min_val=0,
                                      max_val=cw0.shape[0] - 1)
                    sp.dma_start(wbd0[a * C:(a + 1) * C, bass.ds(t, 1), a * C:(a + 1) * C],
                                 cw0[bass.ds(r, 1), :, :].rearrange("a c d -> c a d")).then_inc(s_wbd0, 16)
            sp.dma_start(ident[:], c_ident).then_inc(s_cst, 16)
            sp.dma_start(identb[:], c_identb.bitcast(BF16)).then_inc(s_cst, 16)
            sp.dma_start(mask[:], c_mask).then_inc(s_cst, 16)
            sp.dma_start(cosT[:], c_cos).then_inc(s_cst, 16)
            sp.dma_start(sinT[:], c_sin).then_inc(s_cst, 16)
            sp.dma_start(wa[:, 0:H, :].rearrange("p h d -> p (h d)"),
                         qn_w.rearrange("(a n) -> a n", a=1).broadcast_to([P, H * DH])).then_inc(s_cst, 16)
            sp.dma_start(wa[:, H:QK, :].rearrange("p h d -> p (h d)"),
                         kn_w.rearrange("(a n) -> a n", a=1).broadcast_to([P, KV * DH])).then_inc(s_cst, 16)
            sp.dma_start(lnw[:, 0, :], ln1_w.rearrange("(k p) -> p k", p=P), allow_slow_non_contiguous=True).then_inc(s_cst, 16)
            sp.dma_start(lnw[:, 1, :], ln2_w.rearrange("(k p) -> p k", p=P), allow_slow_non_contiguous=True).then_inc(s_cst, 16)
            for n in range(3, NPIECE + NWO):
                load_piece(n)
            with sp.Fori(0, T) as t:
                for a in range(BT):
                    r = sp.value_load(idx[0:1, 1, bass.ds(t * BT + a, 1)], min_val=0,
                                      max_val=cw1.shape[0] - 1)
                    sp.dma_start(wbd1[a * C:(a + 1) * C, bass.ds(t, 1), a * C:(a + 1) * C],
                                 cw1[bass.ds(r, 1), :, :].rearrange("a c d -> c a d")).then_inc(s_wbd1, 16)
            sp.dma_start(rw[:], router_w.rearrange("(k p) e -> p k e", p=P)).then_inc(s_cst2, 16)
            sp.dma_start(gwr[:], gate_w).then_inc(s_cst2, 16)
            sp.dma_start(rbias[:], router_b.rearrange("(a n) -> a n", a=1).broadcast_to([P, E0])).then_inc(s_cst2, 16)
            sp.dma_start(gbias[:], gate_b.rearrange("(a n) -> a n", a=1).broadcast_to([P, E1])).then_inc(s_cst2, 16)

            sp.wait_ge(s_x1, T)
            sp.wait_ge(s_ssq, 2 * T)
            half = E0 // 2
            for lo, s in ((0, s_w0[0]), (half, s_w0[1])):
                e = slice(lo, lo + half)
                sp.dma_start(wg_s[:, e], wg[e].rearrange("e (k p) i -> p e k i", p=P)).then_inc(s, 16)
                sp.dma_start(wu_s[:, e], wu[e].rearrange("e (k p) i -> p e k i", p=P)).then_inc(s, 16)
                sp.dma_start(wd_s[:, e], wd[e].rearrange("e i d -> i e d")).then_inc(s, 16)
            sp.wait_ge(s_cz, 3)
            sp.dma_start(sel0[0:c_sel0.shape[0]], c_sel0.bitcast(BF16)).then_inc(s_sel, 16)
            sp.dma_start(sel1[0:c_sel1.shape[0]], c_sel1.bitcast(BF16)).then_inc(s_sel, 16)
            nr = NR * P
            for src, shr, dst, s in ((w1r, w1s, w1_s, s_w1[0]), (w3r, w3s, w3_s, s_w1[0])):
                for k in range(KD):
                    sp.dma_start(dst[:, k, 0:nr].rearrange("p (e c) -> p e c", e=E1),
                                 src[:, k * P:(k + 1) * P, :].rearrange("e p c -> p e c")).then_inc(s, 16)
                sp.dma_start(dst[:, :, nr:nr + HID], shr.rearrange("(k p) c -> p k c", p=P)).then_inc(s, 16)
            sp.dma_start(w2_s[:, 0:NR, :],
                         w2r.rearrange("e c d -> (e c) d").rearrange("(n p) d -> p n d", p=P)).then_inc(s_w1[0], 16)
            sp.dma_start(w2_s[:, NR, :], w2s[0:P, :]).then_inc(s_w1[0], 16)
            sp.wait_ge(s_pad, 3)
            sp.dma_start(w2_s[0:HREM, NR + 1, :], w2s[P:HID, :]).then_inc(s_w1[0], 16)

            for t in range(T):
                sp.wait_ge(s_fin, t + 1)
                sp.dma_start(out_v[:, t, :], xin[:, t, :]).then_inc(s_out, 16)
            sp.wait_ge(s_out, 16 * T)

        @block.tensor
        def _(pe):
            def passes(dst, lh, ll, rh, rl, start, stop):
                pe.matmul(dst, lh, rh, start=start, stop=False)
                pe.matmul(dst, lh, rl, start=False, stop=False)
                return pe.matmul(dst, ll, rh, start=False, stop=stop)

            pe.wait_ge(s_x, 16)
            pe.wait_ge(s_wbd0, 16 * B)
            for t in range(T):
                pe.matmul(qbanks[:, t // 2, (t % 2) * D:(t % 2 + 1) * D], wbd0[:, t, :], xin[:, t, :],
                          start=True, stop=True).then_inc(s_c0, 1)
            pe.wait_ge(s_cst, 16 * 9)

            def project(t):
                pe.wait_ge(s_hn, t + 1)
                for k in range(KD):
                    last = pe.transpose(bT[:, k * P:(k + 1) * P], hn[:, k * P:(k + 1) * P], ident[:])
                last.then_inc(s_hT, 1)

            def columns(dst, n):
                for k in range(KD):
                    last = passes(dst, hT_h[:, k, :], hT_l[:, k, :], wqkv_h[:, n, k, :], wqkv_l[:, n, k, :],
                                  k == 0, k == KD - 1)
                return last

            def attend(t):
                pe.wait_ge(s_p, t + 1)
                for g in range(KV):
                    last = pe.transpose(bP[:, g * P:(g + 1) * P],
                                        prob[:, g * BT:(g + 1) * BT, :].rearrange("p a c -> p (a c)"), ident[:])
                last.then_inc(s_pT, 1)

            def values(t):
                pe.wait_ge(s_pTl, t + 1)
                for a in range(BT):
                    r = slice(a * C, (a + 1) * C)
                    for g in range(KV):
                        last = passes(qbanks[:, a, g * P:(g + 1) * P], v_h[r, g * DH:(g + 1) * DH],
                                      v_l[r, g * DH:(g + 1) * DH], pT_h[r, g, :], pT_l[r, g, :], True, True)
                    last.then_inc(s_o, 1)

            def output(t):
                for h in range(H):
                    last = passes(bT[:, 0:D], oT_h[:, h, :, :].rearrange("p a c -> p (a c)"),
                                  oT_l[:, h, :, :].rearrange("p a c -> p (a c)"),
                                  wo_h[:, h, :], wo_l[:, h, :], h == 0, h == H - 1)
                last.then_inc(s_wo, 1)

            def scores(t):
                pe.wait_ge(s_krot, t + 1)
                for n in range(NTR):
                    if n == 1:
                        pe.wait_ge(s_qrot, t + 1)
                    if n == 2:
                        pe.wait_ge(s_vl, t + 1)
                    if n >= 3:
                        pe.wait_ge(s_trl, NTR * t + n - 2)
                    for i in range(4):
                        h = H + i if n == 0 else (n - 1) * REP + i
                        last = pe.transpose(tr_bank[n][:, i * P:(i + 1) * P], qk[:, h, :], ident[:])
                    last.then_inc(s_tr, 1)
                pe.wait_ge(s_trl, NTR * t + NTR)
                for g in range(KV):
                    for a in range(BT):
                        u = (g * BT + a) * C
                        ql = [z[:, a, g, :, :].rearrange("p r c -> p (r c)") for z in (qT_h, qT_l)]
                        last = passes(bV[:, u:u + C], ql[0], ql[1], kT_h[:, g, a, :], kT_l[:, g, a, :], True, True)
                last.then_inc(s_sc, 1)

            def tile(t, first):
                project(t)
                if not first:
                    attend(t - 1)
                    pe.wait_ge(s_qpost, t)
                    values(t - 1)
                pe.wait_ge(s_hTl, t + 1)
                columns(bK[:], 0).then_inc(s_k, 1)
                columns(bV[:], 1).then_inc(s_v, 1)
                for n in range(4):
                    if not first:
                        pe.wait_ge(s_ol, 4 * t + n - 3)
                    last = columns(qbanks[:, n, :], 2 + n)
                last.then_inc(s_q, 1)
                if not first:
                    output(t - 1)
                scores(t)

            pe.wait_ge(s_res, 4)
            pe.wait_ge(s_wl, NPIECE)
            tile(0, True)
            pe.wait_ge(s_wl, NPIECE + NWO)
            with pe.Fori(1, T) as t:
                tile(t, False)
            attend(T - 1)
            values(T - 1)
            pe.wait_ge(s_ol, 4 * T)
            output(T - 1)

            pe.wait_ge(s_cst2, 16 * 4)
            for k in range(KD):
                last = pe.transpose(bK[:, k * E1:(k + 1) * E1], gwr[:, k * P:(k + 1) * P], ident[0:E1, 0:E1])
            last.then_inc(s_gwT, 1)
            pe.wait_ge(s_rwl, 2)

            def features0():
                pe.wait_ge(s_x1, T)
                for t in range(T):
                    pe.wait_ge(s_hn2, t + 1)
                    if t >= 4:
                        pe.wait_ge(s_fTl[0], t - 3)
                    b = qbanks[:, t % 4, 0:KD * P].rearrange("p (k n) -> p k n", k=KD)
                    for k in range(KD):
                        last = pe.transpose(b[:, k, :], hn2[:, t, k * P:(k + 1) * P], ident[:])
                    last.then_inc(s_fT[0], 1)

            def features1():
                pe.wait_ge(s_wbd1, 16 * B)
                for t in range(T):
                    pe.wait_ge(s_x2, t + 1)
                    if t >= 4:
                        pe.wait_ge(s_fTl[1], t - 3)
                    b = qbanks[:, t % 4, 0:KD * P].rearrange("p (k n) -> p k n", k=KD)
                    for k in range(KD):
                        last = pe.matmul(b[:, k, :], x1[:, t, k * P:(k + 1) * P], wbd1[:, t, :],
                                         start=True, stop=True)
                    last.then_inc(s_fT[1], 1)

            def logits(m, E, w_h, w_l):
                for t in range(T):
                    pe.wait_ge(s_fTl[m], t + 1)
                    r = slice(t * P, (t + 1) * P)
                    for k in range(KD):
                        last = passes(bV[:, t * E:(t + 1) * E], featT_h[:, k, r], featT_l[:, k, r],
                                      w_h[:, k, :], w_l[:, k, :], k == 0, k == KD - 1)
                last.then_inc(s_lg[m], 1)

            def weight_rows(m, E):
                pe.wait_ge(s_cb3[m], 1)
                n = 3 * E + 2 * m
                cb = bP[:, :].bitcast(BF16)
                for t in range(T):
                    last = pe.transpose(cb[0:n, t * P:(t + 1) * P], comb3[:, t, 0:n], identb[:])
                last.then_inc(s_cbT[m], 1)
                pe.wait_ge(s_cbc[m], 1)

            def mixture(m):
                sel = moes[m]["sel"]
                def down(q, n, start, stop):
                    j, hf = n // 2, n % 2
                    pe.wait_ge(s_al[m], 4 * q + n + 1)
                    for d in range(KD):
                        cs = slice(d * P, (d + 1) * P)
                        last = passes(qbanks[:, d * NH + hf, :], wC_h[j][:, cs], wC_l[j][:, cs],
                                      act_h[:, n, :], act_l[:, n, :], start, stop)
                    last.then_inc(s_D[m], 1)

                def pair(q, first):
                    for n in range(4):
                        j, hf = n // 2, n % 2
                        s = 4 * q + n
                        r = slice(hf * BANK, (hf + 1) * BANK)
                        if hf == 0:
                            pe.wait_ge(s_wsl[m], 2 * q + j + 1)
                        if not (first and n == 0):
                            pe.wait_ge(s_fst[m], s)
                        for k in range(KD):
                            last = passes(bT[:], wA_h[j][:, k, :], wA_l[j][:, k, :], featT_h[:, k, r],
                                          featT_l[:, k, r], k == 0, k == KD - 1)
                        last.then_inc(s_G[m], 1)
                        if not (first and n == 0):
                            pe.wait_ge(s_prd[m], s)
                        for k in range(KD):
                            last = passes(bK[:], wB_h[j][:, k, :], wB_l[j][:, k, :], featT_h[:, k, r],
                                          featT_l[:, k, r], k == 0, k == KD - 1)
                        last.then_inc(s_U[m], 1)
                        if not (first and n < 2):
                            pe.wait_ge(s_act[m], s - 1)
                        pe.matmul([bV, bP][n % 2][:], sel[:, bass.ds(2 * q + j, 1), :].rearrange("p a n -> p (a n)"),
                                  combT[:, r], start=True, stop=True).then_inc(s_BC[m], 1)
                        if n >= 2:
                            down(q, n - 2, first, False)
                        elif not first:
                            down(q - 1, n + 2, False, False)

                q_all = sum(n for _, n, _ in moes[m]["runs"]) // 2
                pair(0, True)
                with pe.Fori(1, q_all) as q:
                    pair(q, False)
                down(q_all - 1, 2, False, True)
                down(q_all - 1, 3, False, True)

            def back(m):
                pe.wait_ge(s_mx0[m], 4)
                for t in range(T):
                    if t >= 4:
                        pe.wait_ge(s_x2 if m == 0 else s_fin, t - 3)
                    b = bank[t % 4]
                    for k in range(KD):
                        last = pe.transpose(b[:, k * P:(k + 1) * P], outT[:, k, t * P:(t + 1) * P], ident[:])
                    last.then_inc(s_bk[m], 1)

            features0()
            logits(0, E0, rw_h, rw_l)
            weight_rows(0, E0)
            pe.wait_ge(s_sel, 32)
            mixture(0)
            back(0)
            features1()
            logits(1, E1, gw_h, gw_l)
            weight_rows(1, E1)
            mixture(1)
            back(1)

        @block.scalar
        def _(act_e):
            for n in range(NPIECE + NWO):
                act_e.wait_ge(s_wst[n % 3], 16 * (n // 3 + 1))
                dst = (wqkv_h[:, n, :, :].rearrange("p k n -> p (k n)") if n < NPIECE else
                       wo_h[:, 4 * (n - NPIECE):4 * (n - NPIECE) + 4, :].rearrange("p h n -> p (h n)"))
                nc.scalar.activation(dst, wstage[:, n % 3, :], ACT.Copy).then_inc(s_wh, 1)
                if n == 3:
                    for t in range(T):
                        act_e.wait_ge(s_res, t // 2 + 1)
                        if t:
                            act_e.wait_ge(s_ssq, t)
                        nc.scalar.activation(junk[:, 0:D], x1[:, t, :], ACT.Square,
                                             accum_out=ssq[:, t:t + 1]).then_inc(s_ssq, 1)
            act_e.wait_ge(s_cst, 16 * 9)
            def values_high(t):
                act_e.wait_ge(s_pT, t + 1)
                nc.scalar.activation(pT_h[:, :, :].rearrange("p g n -> p (g n)"), bP[:], ACT.Copy).then_inc(s_pTh, 1)
                for a in range(BT):
                    act_e.wait_ge(s_o, BT * t + a + 1)
                    nc.scalar.activation(oT_h[:, :, a, :], qbanks[:, a, :].rearrange("p (h c) -> p h c", c=C),
                                         ACT.Copy).then_inc(s_oh, 1)

            def tile(t, first):
                act_e.wait_ge(s_hT, t + 1)
                for k in range(KD):
                    last = nc.scalar.activation(hT_h[:, k, :], bT[:, k * P:(k + 1) * P], ACT.Copy,
                                                scale=lnw[:, 0, k:k + 1])
                last.then_inc(s_hTh, 1)
                if not first:
                    values_high(t - 1)
                act_e.wait_ge(s_k, t + 1)
                if not first:
                    act_e.wait_ge(s_kms, t)
                    act_e.wait_ge(s_qss, t)
                    act_e.wait_ge(s_ssq, T + t - 1)
                nc.scalar.activation(junk[:, 0:BANK], bK[:], ACT.Square, accum_out=qkss[:, 1:2]).then_inc(s_kss, 1)
                act_e.wait_ge(s_v, t + 1)
                nc.scalar.activation(v_h[:], bV[:], ACT.Copy).then_inc(s_vh, 1)
                act_e.wait_ge(s_q, t + 1)
                act_e.wait_ge(s_kss, t + 1)
                if not first:
                    act_e.wait_ge(s_qms, t)
                nc.scalar.activation(junk[:], qv, ACT.Square, accum_out=qkss[:, 0:1]).then_inc(s_qss, 1)
                if not first:
                    act_e.wait_ge(s_x1, t)
                    act_e.wait_ge(s_qss, t + 1)
                    nc.scalar.activation(junk[:, 0:D], x1[:, bass.ds(t - 1, 1), :].rearrange("p a d -> p (a d)"),
                                         ACT.Square, accum_out=ssq[:, bass.ds(t - 1, 1)]).then_inc(s_ssq, 1)
                for n in range(NTR):
                    act_e.wait_ge(s_tr, NTR * t + n + 1)
                    src = tr_bank[n][:, :]
                    if n == 0:
                        nc.scalar.activation(kT_h[:, :, :, :].rearrange("p g a c -> p (g a c)"), src,
                                             ACT.Copy).then_inc(s_trh, 1)
                    else:
                        nc.scalar.activation(qT_h[:, :, n - 1, :, :].rearrange("p a r c -> p r a c"),
                                             src.rearrange("p (r a c) -> p r a c", r=REP, a=BT),
                                             ACT.Copy).then_inc(s_trh, 1)
                act_e.wait_ge(s_sub, t + 1)
                nc.scalar.activation(prob[:, :, :], sm[:, :, :], ACT.Exp, scale=SCALE).then_inc(s_exp, 1)

            act_e.wait_ge(s_rms, 1)
            tile(0, True)
            with act_e.Fori(1, T) as t:
                tile(t, False)
            values_high(T - 1)
            act_e.wait_ge(s_x1, T)
            nc.scalar.activation(junk[:, 0:D], x1[:, T - 1, :], ACT.Square,
                                 accum_out=ssq[:, T - 1:T]).then_inc(s_ssq, 1)
            act_e.wait_ge(s_cst2, 16 * 4)
            nc.scalar.activation(rw_h[:], rw[:], ACT.Copy).then_inc(s_rwh, 1)
            act_e.wait_ge(s_gwT, 1)
            nc.scalar.activation(gw_h[:], bK[:, 0:KD * E1].rearrange("p (k e) -> p k e", e=E1),
                                 ACT.Copy).then_inc(s_rwh, 1)

            def features_high(m):
                for t in range(T):
                    act_e.wait_ge(s_fT[m], t + 1)
                    b = qbanks[:, t % 4, 0:KD * P].rearrange("p (k n) -> p k n", k=KD)
                    r = slice(t * P, (t + 1) * P)
                    if m == 0:
                        for k in range(KD):
                            last = nc.scalar.activation(featT_h[:, k, r], b[:, k, :], ACT.Copy,
                                                        scale=lnw[:, 1, k:k + 1])
                        last.then_inc(s_fTh[m], 1)
                    else:
                        nc.scalar.activation(featT_h[:, :, r], b, ACT.Copy).then_inc(s_fTh[m], 1)

            def router(m, E):
                act_e.wait_ge(s_lg[m], 1)
                nc.scalar.activation(sig[:, 0:T * E], bV[:, 0:T * E], ACT.Sigmoid).then_inc(s_sig[m], 1)
                n = 3 * E + 2 * m
                act_e.wait_ge(s_cz, 1)
                act_e.wait_ge(s_cbT[m], 1)
                nc.scalar.activation(combT[0:n, :], bP[0:n, :].bitcast(BF16), ACT.Copy).then_inc(s_cbc[m], 1)

            def run_mixture(m):
                q_all = sum(n for _, n, _ in moes[m]["runs"]) // 2
                act_e.wait_ge(moes[m]["sems"][0], 16 * (3 if m == 0 else 9))
                if m == 1:
                    act_e.wait_ge(s_pad, 3)

                def split_weights(c, j, later):
                    if later:
                        act_e.wait_ge(s_U[m], 2 * c - 2)
                        act_e.wait_ge(s_wsl[m], c - 1)
                    wa_s, wb_s, wc_s = chunk_weights(m, c)
                    nc.scalar.activation(wA_h[j][:], wa_s, ACT.Copy)
                    nc.scalar.activation(wB_h[j][:], wb_s, ACT.Copy)
                    if later:
                        act_e.wait_ge(s_D[m], 2 * c - 2)
                    nc.scalar.activation(wC_h[j][:], wc_s, ACT.Copy).then_inc(s_wsh[m], 1)

                def high(q, n, later):
                    act_e.wait_ge(s_act[m], 4 * q + n + 1)
                    if later:
                        act_e.wait_ge(s_D[m], 4 * q + n - 3)
                    nc.scalar.activation(act_h[:, n, :], act[:, n % 2, :], ACT.Copy).then_inc(s_ah[m], 1)

                def pair(q, first, second, gated, more):
                    for n in range(4):
                        s = 4 * q + n
                        act_e.wait_ge(s_G[m], s + 1)
                        if not (first and n == 0):
                            act_e.wait_ge(s_prd[m], s)
                        nc.scalar.activation(gate_s[:], bT[:], ACT.Silu if gated else ACT.Copy).then_inc(s_fst[m], 1)
                        if n:
                            high(q, n - 1, not first)
                        elif not first:
                            high(q - 1, 3, not second)
                        if not gated:
                            act_e.wait_ge(s_prd[m], s + 1)
                            nc.scalar.activation(prod[:, 1, :], prod[:, 0, :], ACT.Silu).then_inc(s_sil[m], 1)
                        if n == 1 and not first:
                            split_weights(2 * q + 1, 1, True)
                        if n == 3 and more:
                            split_weights(2 * q + 2, 0, True)

                split_weights(0, 0, False)
                split_weights(1, 1, False)
                if m == 0:
                    act_e.wait_ge(moes[m]["sems"][1], 16 * 3)
                runs = [(lo // 2, (lo + n) // 2, g) for lo, n, g in moes[m]["runs"]]
                for lo, hi, gated in runs:
                    if lo == 0:
                        pair(0, True, False, gated, True)
                        pair(1, False, True, gated, True)
                        lo = 2
                    end = hi - 1 if hi == q_all else hi
                    if end > lo:
                        with act_e.Fori(lo, end) as q:
                            pair(q, False, False, gated, True)
                    if hi == q_all:
                        pair(q_all - 1, False, False, gated, False)
                high(q_all - 1, 3, True)
                act_e.wait_ge(s_D[m], 4 * q_all)
                for i in range(2):
                    nc.scalar.activation(outT[:, 0, i * BANK:(i + 1) * BANK], qbanks[:, i, :],
                                         ACT.Copy).then_inc(s_mx0[m], 1)

            features_high(0)
            router(0, E0)
            run_mixture(0)
            features_high(1)
            router(1, E1)
            run_mixture(1)

        @block.gpsimd
        def _(pool):
            nc.gpsimd.memset(wbd0[:], 0.0).then_inc(s_zero, 1)
            nc.gpsimd.memset(mhalf[:], -0.5).then_inc(s_zero, 1)
            nc.gpsimd.memset(wbd1[:], 0.0).then_inc(s_zero, 1)
            for n in range(NPIECE + NWO):
                pool.wait_ge(s_wh, n + 1)
                hi, lo = ((z[:, n, :, :].rearrange("p k n -> p (k n)") for z in (wqkv_h, wqkv_l)) if n < NPIECE
                          else (z[:, 4 * (n - NPIECE):4 * (n - NPIECE) + 4, :].rearrange("p h n -> p (h n)")
                                for z in (wo_h, wo_l)))
                nc.gpsimd.tensor_tensor(lo, wstage[:, n % 3, :], hi.bitcast(F32), ALU.subtract).then_inc(s_wl, 1)
                if n == 1:
                    pool.wait_ge(s_cst, 16 * 9)
                    for lo_d, hi_d in ((0, HALF), (HALF, 0)):
                        nc.gpsimd.tensor_tensor(wb[:, :, lo_d:lo_d + HALF], wa[:, :, hi_d:hi_d + HALF],
                                                sinT[:, lo_d:lo_d + HALF].unsqueeze(1).broadcast_to([P, QK, HALF]),
                                                ALU.mult).then_inc(s_pool, 1)
                    pool.wait_ge(s_pool, 2)
                    nc.gpsimd.tensor_tensor(wa[:, :, 0:2 * HALF], wa[:, :, 0:2 * HALF],
                                            cosT[:, :].unsqueeze(1).broadcast_to([P, QK, 2 * HALF]),
                                            ALU.mult).then_inc(s_wtab, 1)
                if n == 3:
                    pool.wait_ge(s_ms, 1)
                    nc.gpsimd.tensor_tensor(rms[:], rms[:], mhalf[:], ALU.pow).then_inc(s_rms, 1)

            def rope(t):
                pool.wait_ge(s_kms, t + 1)
                nc.gpsimd.tensor_tensor(qkr[:, 1:2], qkr[:, 1:2], mhalf[:, 0:1], ALU.pow).then_inc(s_kr, 1)
                pool.wait_ge(s_kpost, t + 1)
                nc.gpsimd.tensor_tensor(qk[:, H:QK, 0:2 * HALF], qk[:, H:QK, 0:2 * HALF], rot[:, H:QK, :],
                                        ALU.add).then_inc(s_krot, 1)
                pool.wait_ge(s_qms, t + 1)
                nc.gpsimd.tensor_tensor(qkr[:, 0:1], qkr[:, 0:1], mhalf[:, 0:1], ALU.pow).then_inc(s_qr, 1)
                pool.wait_ge(s_qpost, t + 1)
                nc.gpsimd.tensor_tensor(qk[:, 0:H, 0:2 * HALF], qk[:, 0:H, 0:2 * HALF], rot[:, 0:H, :],
                                        ALU.add).then_inc(s_qrot, 1)
                pool.wait_ge(s_mx, t + 1)
                nc.gpsimd.tensor_tensor(sm[:], sm[:], smax[:].unsqueeze(2).broadcast_to([P, KV * BT, C]),
                                        ALU.subtract).then_inc(s_sub, 1)
                pool.wait_ge(s_sum, t + 1)
                nc.gpsimd.tensor_tensor(prob[:], prob[:], psm[:].unsqueeze(2).broadcast_to([P, KV * BT, C]),
                                        ALU.mult).then_inc(s_p, 1)

            with pool.Fori(0, T) as t:
                rope(t)
            pool.wait_ge(s_x1, T)
            pool.wait_ge(s_ssq, 2 * T)
            nc.gpsimd.memset(combT[:], 0.0).then_inc(s_cz, 1)
            nc.gpsimd.memset(sel0[:], 0.0).then_inc(s_cz, 1)
            nc.gpsimd.memset(sel1[:], 0.0).then_inc(s_cz, 1)
            nr = NR * P
            nc.gpsimd.memset(w1_s[:, :, nr + HID:], 0.0).then_inc(s_pad, 1)
            nc.gpsimd.memset(w3_s[:, :, nr + HID:], 0.0).then_inc(s_pad, 1)
            nc.gpsimd.memset(w2_s[:, NR + 1, :], 0.0).then_inc(s_pad, 1)
            pool.wait_ge(s_ms, 2)
            nc.gpsimd.tensor_tensor(rms[:], rms[:], mhalf[:], ALU.pow).then_inc(s_rms, 1)
            for t in range(T):
                nc.gpsimd.tensor_tensor(xin[:, t, :], xin[:, t, :], x1[:, t, :], ALU.add).then_inc(s_xs, 1)

            def run_mixture(m):
                q_all = sum(n for _, n, _ in moes[m]["runs"]) // 2

                def split_weights(c, j, later):
                    pool.wait_ge(s_wsh[m], c + 1)
                    wa_s, wb_s, wc_s = chunk_weights(m, c)
                    nc.gpsimd.tensor_tensor(wA_l[j][:], wa_s, wA_h[j][:].bitcast(F32), ALU.subtract)
                    nc.gpsimd.tensor_tensor(wB_l[j][:], wb_s, wB_h[j][:].bitcast(F32), ALU.subtract)
                    nc.gpsimd.tensor_tensor(wC_l[j][:], wc_s, wC_h[j][:].bitcast(F32),
                                            ALU.subtract).then_inc(s_wsl[m], 1)

                def low(q, n):
                    pool.wait_ge(s_ah[m], 4 * q + n + 1)
                    nc.gpsimd.tensor_tensor(act_l[:, n, :], act[:, n % 2, :], act_h[:, n, :].bitcast(F32),
                                            ALU.subtract).then_inc(s_al[m], 1)

                def pair(q, first, more):
                    if not first:
                        low(q - 1, 3)
                    low(q, 0)
                    if not first:
                        split_weights(2 * q + 1, 1, True)
                    low(q, 1)
                    low(q, 2)
                    if more:
                        split_weights(2 * q + 2, 0, True)

                split_weights(0, 0, False)
                split_weights(1, 1, False)
                pair(0, True, True)
                with pool.Fori(1, q_all - 1) as q:
                    pair(q, False, True)
                pair(q_all - 1, False, False)
                low(q_all - 1, 3)

            run_mixture(0)
            run_mixture(1)

        @block.vector
        def _(dve):
            chain = [0]

            def then(ins):
                chain[0] += 1
                ins.then_inc(s_dve, 1)
                dve.wait_ge(s_dve, chain[0])

            V = nc.vector
            for i in range(T // 2):
                dve.wait_ge(s_c0, 2 * i + 2)
                V.tensor_copy(x1[:, 2 * i:2 * i + 2, :].rearrange("p t d -> p (t d)"), qbanks[:, i, :]).then_inc(s_res, 1)
            dve.wait_ge(s_ssq, T)
            V.tensor_scalar(rms[:], ssq[:], 1.0 / D, EPS, ALU.mult, ALU.add).then_inc(s_ms, 1)
            dve.wait_ge(s_rms, 1)
            V.tensor_scalar(hn[:], x1[:, 0, :], rms[:, 0:1], None, ALU.mult).then_inc(s_hn, 1)
            dve.wait_ge(s_wtab, 1)

            def scaled_heads(r, src, h0, h1):
                n = (h1 - h0)
                V.scalar_tensor_tensor(qk[:, h0:h1, :].rearrange("p h d -> p (h d)"), src, r,
                                       wa[:, h0:h1, :].rearrange("p h d -> p (h d)"), ALU.mult, ALU.mult)
                sv = src.rearrange("p (h d) -> p h d", d=DH)
                for lo, hi in ((0, HALF), (HALF, 0)):
                    last = V.scalar_tensor_tensor(rot[:, h0:h1, lo:lo + HALF], sv[:, :, hi:hi + HALF], r,
                                                  wb[:, h0:h1, lo:lo + HALF], ALU.mult, ALU.mult)
                return last

            def values_low(t):
                dve.wait_ge(s_pTh, t + 1)
                V.tensor_tensor(pT_l[:, :, :].rearrange("p g n -> p (g n)"), bP[:],
                                pT_h[:, :, :].rearrange("p g n -> p (g n)").bitcast(F32),
                                ALU.subtract).then_inc(s_pTl, 1)
                for a in range(BT):
                    dve.wait_ge(s_oh, BT * t + a + 1)
                    V.tensor_tensor(oT_l[:, :, a, :], qbanks[:, a, :].rearrange("p (h c) -> p h c", c=C),
                                    oT_h[:, :, a, :].bitcast(F32), ALU.subtract).then_inc(s_ol, 1)

            def add_rows(t, tr):
                dve.wait_ge(s_wo, t + 1)
                V.tensor_tensor(tr, tr, bT[:, 0:D], ALU.add).then_inc(s_x1, 1)

            def tile(t, first):
                dve.wait_ge(s_hTh, t + 1)
                for k in range(KD):
                    last = V.scalar_tensor_tensor(hT_l[:, k, :], bT[:, k * P:(k + 1) * P], lnw[:, 0, k:k + 1],
                                                  hT_h[:, k, :].bitcast(F32), ALU.mult, ALU.subtract)
                last.then_inc(s_hTl, 1)
                if not first:
                    values_low(t - 1)
                dve.wait_ge(s_kss, t + 1)
                V.tensor_scalar(qkr[:, 1:2], qkss[:, 1:2], 1.0 / (KV * DH), EPS, ALU.mult, ALU.add).then_inc(s_kms, 1)
                dve.wait_ge(s_kr, t + 1)
                scaled_heads(qkr[:, 1:2], bK[:], H, QK).then_inc(s_kpost, 1)
                dve.wait_ge(s_vh, t + 1)
                V.tensor_tensor(v_l[:], bV[:], v_h[:].bitcast(F32), ALU.subtract).then_inc(s_vl, 1)
                dve.wait_ge(s_qss, t + 1)
                V.tensor_scalar(qkr[:, 0:1], qkss[:, 0:1], 1.0 / (H * DH), EPS, ALU.mult, ALU.add).then_inc(s_qms, 1)
                dve.wait_ge(s_qr, t + 1)
                scaled_heads(qkr[:, 0:1], qv, 0, H).then_inc(s_qpost, 1)
                if not first:
                    add_rows(t - 1, x1[:, bass.ds(t - 1, 1), :].rearrange("p a d -> p (a d)"))
                for n in range(NTR):
                    dve.wait_ge(s_trh, NTR * t + n + 1)
                    src = tr_bank[n][:, :]
                    if n == 0:
                        V.tensor_tensor(kT_l[:, :, :, :].rearrange("p g a c -> p (g a c)"), src,
                                        kT_h[:, :, :, :].rearrange("p g a c -> p (g a c)").bitcast(F32),
                                        ALU.subtract).then_inc(s_trl, 1)
                    else:
                        V.tensor_tensor(qT_l[:, :, n - 1, :, :].rearrange("p a r c -> p r a c"),
                                        src.rearrange("p (r a c) -> p r a c", r=REP, a=BT),
                                        qT_h[:, :, n - 1, :, :].rearrange("p a r c -> p r a c").bitcast(F32),
                                        ALU.subtract).then_inc(s_trl, 1)
                dve.wait_ge(s_sc, t + 1)
                V.tensor_tensor(sm[:], bV[:, :].rearrange("p (u c) -> p u c", c=C),
                                mask[:].unsqueeze(1).broadcast_to([P, KV * BT, C]), ALU.add).then_inc(s_sm, 1)
                dve.wait_ge(s_sm, t + 1)
                V.tensor_reduce(smax[:], sm[:], AX.X, ALU.max).then_inc(s_mx, 1)
                dve.wait_ge(s_exp, t + 1)
                V.tensor_reduce(psm[:], prob[:], AX.X, ALU.add).then_inc(s_sum2, 1)
                dve.wait_ge(s_sum2, t + 1)
                V.reciprocal(psm[:], psm[:]).then_inc(s_sum, 1)

            def next_rows(t, tr, r):
                V.tensor_scalar(hn[:], tr, r, None, ALU.mult).then_inc(s_hn, 1)

            tile(0, True)
            next_rows(1, x1[:, 1, :], rms[:, 1:2])
            with dve.Fori(1, T - 1) as t:
                tile(t, False)
                next_rows(t + 1, x1[:, bass.ds(t + 1, 1), :].rearrange("p a d -> p (a d)"),
                          rms[:, bass.ds(t + 1, 1)])
            tile(T - 1, False)
            values_low(T - 1)
            add_rows(T - 1, x1[:, T - 1, :])

            dve.wait_ge(s_rwh, 1)
            V.tensor_tensor(rw_l[:], rw[:], rw_h[:].bitcast(F32), ALU.subtract).then_inc(s_rwl, 1)
            dve.wait_ge(s_rwh, 2)
            V.tensor_tensor(gw_l[:], bK[:, 0:KD * E1].rearrange("p (k e) -> p k e", e=E1),
                            gw_h[:].bitcast(F32), ALU.subtract).then_inc(s_rwl, 1)
            dve.wait_ge(s_ssq, 2 * T)
            V.tensor_scalar(rms[:], ssq[:], 1.0 / D, EPS, ALU.mult, ALU.add).then_inc(s_ms, 1)
            dve.wait_ge(s_rms, 2)
            for t in range(T):
                V.tensor_scalar(hn2[:, t, :], x1[:, t, :], rms[:, t:t + 1], None, ALU.mult).then_inc(s_hn2, 1)

            def features_low(m):
                for t in range(T):
                    dve.wait_ge(s_fTh[m], t + 1)
                    b = qbanks[:, t % 4, 0:KD * P].rearrange("p (k n) -> p k n", k=KD)
                    r = slice(t * P, (t + 1) * P)
                    if m == 0:
                        for k in range(KD):
                            last = V.scalar_tensor_tensor(featT_l[:, k, r], b[:, k, :], lnw[:, 1, k:k + 1],
                                                          featT_h[:, k, r].bitcast(F32), ALU.mult, ALU.subtract)
                        last.then_inc(s_fTl[m], 1)
                    else:
                        V.tensor_tensor(featT_l[:, :, r], b, featT_h[:, :, r].bitcast(F32),
                                        ALU.subtract).then_inc(s_fTl[m], 1)

            def router(m, E, K, bias):
                def v3(z):
                    return z[:, 0:T * E].rearrange("p (t e) -> p t e", e=E)

                def row(z):
                    return z.unsqueeze(2).broadcast_to([P, T, E])

                V.memset(scanA[:], 0.0)
                then(V.memset(scanB[:], 0.0))
                V.memset(comb3[:, :, 3 * E:3 * E + 2], 1.0)
                dve.wait_ge(s_sig[m], 1)
                then(V.tensor_tensor(v3(score), v3(sig), bias[:].unsqueeze(1).broadcast_to([P, T, E]), ALU.add))
                for t in range(T):
                    last = V.max(top8[:, t, :], score[:, t * E:(t + 1) * E])
                then(last)
                kth = top8[:, :, K - 1:K].broadcast_to([P, T, E])
                V.tensor_tensor(v3(eq), v3(score), kth, ALU.is_equal)
                then(V.tensor_tensor(v3(gt), v3(score), kth, ALU.is_gt))
                then(V.tensor_reduce(rows[:, 0, :], v3(gt), AX.X, ALU.add))
                then(V.tensor_scalar(rows[:, 0, :], rows[:, 0, :], -1.0, float(K), ALU.mult, ALU.add))
                then(V.tensor_copy(scanA[:, :, EM:EM + E], v3(eq)))
                src, dst, step = scanA, scanB, 1
                while step < E:
                    then(V.tensor_tensor(dst[:, :, EM:EM + E], src[:, :, EM:EM + E],
                                         src[:, :, EM - step:EM - step + E], ALU.add))
                    src, dst, step = dst, src, 2 * step
                then(V.tensor_tensor(v3(comb), src[:, :, EM:EM + E], row(rows[:, 0, :]), ALU.is_le))
                then(V.tensor_tensor(v3(comb), v3(comb), v3(eq), ALU.mult))
                then(V.tensor_tensor(v3(comb), v3(comb), v3(gt), ALU.add))
                then(V.tensor_tensor(v3(comb), v3(comb), v3(score if m else sig), ALU.mult))
                then(V.tensor_reduce(rows[:, 1, :], v3(comb), AX.X, ALU.add))
                then(V.reciprocal(rows[:, 1, :], rows[:, 1, :]))
                then(V.tensor_tensor(v3(comb), v3(comb), row(rows[:, 1, :]), ALU.mult))
                then(V.tensor_copy(comb3[:, :, 0:E], v3(comb)))
                then(V.tensor_tensor(v3(comb), v3(comb), comb3[:, :, 0:E], ALU.subtract))
                then(V.tensor_copy(comb3[:, :, E:2 * E], v3(comb)))
                V.tensor_tensor(comb3[:, :, 2 * E:3 * E], v3(comb), comb3[:, :, E:2 * E],
                                ALU.subtract).then_inc(s_cb3[m], 1)

            def run_mixture(m):
                q_all = sum(n for _, n, _ in moes[m]["runs"]) // 2

                def pair(q, first, gated):
                    for n in range(4):
                        s = 4 * q + n
                        dve.wait_ge(s_fst[m], s + 1)
                        dve.wait_ge(s_U[m], s + 1)
                        if not (first and n == 0):
                            dve.wait_ge(s_act[m], s)
                        V.tensor_tensor(prod[:, 0, :], gate_s[:], bK[:], ALU.mult).then_inc(s_prd[m], 1)
                        dve.wait_ge(s_BC[m], s + 1)
                        if gated:
                            dve.wait_ge(s_prd[m], s + 1)
                        else:
                            dve.wait_ge(s_sil[m], s + 1)
                        if not (first and n < 2):
                            dve.wait_ge(s_al[m], s - 1)
                        V.tensor_tensor(act[:, n % 2, :], prod[:, 0 if gated else 1, :], [bV, bP][n % 2][:],
                                        ALU.mult).then_inc(s_act[m], 1)

                pair(0, True, moes[m]["runs"][0][2])
                for lo, n, gated in moes[m]["runs"]:
                    lo, hi = max(lo // 2, 1), (lo + n) // 2
                    if hi - lo > 1:
                        with dve.Fori(lo, hi) as q:
                            pair(q, False, gated)
                    else:
                        pair(lo, False, gated)
                dve.wait_ge(s_D[m], 4 * q_all)
                for i in range(2):
                    V.tensor_copy(outT[:, 1, i * BANK:(i + 1) * BANK], qbanks[:, 2 + i, :]).then_inc(s_mx0[m], 1)

            features_low(0)
            router(0, E0, TOPK0, rbias)
            run_mixture(0)
            dve.wait_ge(s_xs, T)
            for t in range(T):
                dve.wait_ge(s_bk[0], t + 1)
                V.tensor_tensor(x1[:, t, :], xin[:, t, :], bank[t % 4][:, 0:D], ALU.add).then_inc(s_x2, 1)
            features_low(1)
            router(1, E1, TOPK1, gbias)
            run_mixture(1)
            for t in range(T):
                dve.wait_ge(s_bk[1], t + 1)
                V.tensor_tensor(xin[:, t, :], x1[:, t, :], bank[t % 4][:, 0:D], ALU.add).then_inc(s_fin, 1)


_INS = ["x", "itok_B_1_198", "itok_B_0_7", "L0_cond_weights", "L0_ffn_ln1_w", "L0_ffn_ln2_w", "L0_ffn_wq",
        "L0_ffn_wk", "L0_ffn_wv", "L0_ffn_wo", "L0_ffn_qnorm_w", "L0_ffn_knorm_w", "L0_ffn_router_w",
        "L0_ffn_router_bias", "L0_ffn_wg", "L0_ffn_wu", "L0_ffn_wd", "L1_cond_weights", "L1_ffn_gate_w",
        "L1_ffn_gate_b", "L1_ffn_w1_shared", "L1_ffn_w2_shared", "L1_ffn_w3_shared", "L1_ffn_w1_routed",
        "L1_ffn_w2_routed", "L1_ffn_w3_routed"]


def shape_constants():
    import numpy as np
    one = 0x3F80
    p = np.arange(128)
    pos = (p % 32).astype(np.float32)
    inv = (1.0 / np.float32(1000000.0) ** (np.arange(0, 64, 2, dtype=np.float32) / np.float32(64))).astype(np.float32)
    ang = pos[:, None] * inv[None, :]
    cos, sin = np.cos(ang), np.sin(ang)
    mask = np.where(np.arange(32)[None, :] <= pos[:, None], 0.0, -3.0e38).astype(np.float32)
    sel0 = np.zeros((24, 8, 128), np.uint16)
    for e in range(8):
        sel0[[e, 8 + e, 16 + e], e, :] = one
    sel1 = np.zeros((50, 24, 128), np.uint16)
    for c in range(22):
        e = (c * 128 + p) // 176
        for part in range(3):
            sel1[16 * part + e, c, p] = one
    sel1[48, 22:24, :] = one
    return {"c_ident": np.eye(128, dtype=np.float32), "c_identb": np.eye(128, dtype=np.uint16) * np.uint16(one),
            "c_mask": mask, "c_cos": np.concatenate([cos, cos], 1).astype(np.float32),
            "c_sin": np.concatenate([-sin, sin], 1).astype(np.float32),
            "c_sel0": sel0, "c_sel1": sel1}


def kernel(**inputs):
    import numpy as _np
    import concourse.bacc as _bacc
    from concourse import mybir as _mybir
    from concourse.bass_utils import run_bass_kernel_spmd as _run

    nc = _bacc.Bacc("TRN2", target_bir_lowering=False, num_devices=1)
    arrays, args = {}, []
    for name in _INS:
        arrays[f"in_{name}"] = _np.ascontiguousarray(inputs[name])
    for name, a in shape_constants().items():
        arrays[f"in_{name}"] = a
    for name, a in arrays.items():
        args.append(nc.dram_tensor(name, a.shape, _mybir.dt.from_np(a.dtype), kind="ExternalInput").ap())
    args.append(nc.dram_tensor("out_rows", arrays["in_x"].shape, F32, kind="ExternalOutput").ap())
    adaln_moe_program(nc, *args)
    r = _run(nc, [arrays], core_ids=[0])
    return r.results[0]["out_rows"]
```

```python
import concourse.bass as bass
from concourse import mybir
from contextlib import ExitStack

F32 = mybir.dt.float32
F32R = mybir.dt.float32r
BF16 = mybir.dt.bfloat16
I32 = mybir.dt.int32
U32 = mybir.dt.uint32
ALU = mybir.AluOpType
ACT = mybir.ActivationFunctionType
AX = mybir.AxisListType

P = 128
BANK = 512



def adaln_moe_program(nc, x, idx0, idx1, cw0, ln1_w, ln2_w, wq, wk, wv, wo, qn_w, kn_w,
                      router_w, router_b, wg, wu, wd, cw1, gate_wT, gate_b,
                      w1s, w2s, w3s, w1r, w2r, w3r,
                      c_ident, c_identb, c_mask, c_cos, c_sin, c_rowno, c_sel0, c_sel1, out):
    B, C, D = x.shape
    BT = P // C
    T = B // BT
    NT = B * C
    KD = D // P
    DH = 128
    H = wq.shape[1] // DH
    KV = wk.shape[1] // DH
    REP = H // KV
    HALF = 32
    E0 = router_w.shape[1]
    E1 = gate_wT.shape[1]
    HID = w1r.shape[2]
    NR = E1 * HID // P
    NS = -(-HID // P)
    HREM = HID - P
    NH = NT // BANK
    EPS = 1e-6
    SCALE = float(DH) ** -0.5
    QK = H + KV
    NPIECE = (H + 2 * KV) * DH // BANK
    NWO = H * D // 1024
    TOPK0, TOPK1 = 2, 4

    x_v = x.rearrange("(t a) c d -> (a c) t d", a=BT)
    out_v = out.rearrange("(t a) c d -> (a c) t d", a=BT)

    top = ExitStack()
    with top:
        def sb(name, shape, dt=F32, ctx=top):
            return ctx.enter_context(nc.sbuf_tensor(name, shape, dt))

        def sem(name):
            return top.enter_context(nc.semaphore(name))

        bank = [top.enter_context(nc.psum_tensor(f"bank{i}", [P, BANK], F32)) for i in range(4)]
        qbanks = top.enter_context(nc.psum_tensor("qbanks", [P, 4, BANK], F32))

        xin = sb("xin", [P, T, D])
        x1 = sb("x1", [P, T + 1, D])
        wbd1 = sb("wbd1", [P, T, P])
        ident = sb("ident", [P, P])
        identb = sb("identb", [P, P], BF16)
        lnw = sb("lnw", [P, 2, KD])
        rbias = sb("rbias", [P, E0])
        gbias = sb("gbias", [P, E1])
        ssq = sb("ssq", [P, T])
        rms = sb("rms", [P, T + 1])
        mhalf = sb("mhalf", [P, T])
        rw = sb("rw", [P, KD, E0])
        rw_h = sb("rw_h", [P, KD, E0], F32R)
        rw_l = sb("rw_l", [P, KD, E0], F32R)
        gw = sb("gw", [P, KD, E1])
        gw_h = sb("gw_h", [P, KD, E1], F32R)
        gw_l = sb("gw_l", [P, KD, E1], F32R)

        ph1 = ExitStack()
        wstage = sb("wstage", [P, 3, 1024], F32, ph1)
        wqkv_h = sb("wqkv_h", [P, NPIECE, KD, BANK], F32R, ph1)
        wqkv_l = sb("wqkv_l", [P, NPIECE, KD, BANK], F32R, ph1)
        wo_h = sb("wo_h", [P, H, D], F32R, ph1)
        wo_l = sb("wo_l", [P, H, D], F32R, ph1)
        mask = sb("mask", [P, C], F32, ph1)
        cosT = sb("cosT", [P, 2 * HALF], F32, ph1)
        sinT = sb("sinT", [P, 2 * HALF], F32, ph1)
        wa = sb("wa", [P, QK, DH], F32, ph1)
        wb = sb("wb", [P, QK, 2 * HALF], F32, ph1)
        hn = sb("hn", [P, D], F32, ph1)
        hT_h = sb("hT_h", [P, KD, P], F32R, ph1)
        hT_l = sb("hT_l", [P, KD, P], F32R, ph1)
        qk = sb("qk", [P, QK, DH], F32, ph1)
        rot = sb("rot", [P, QK, 2 * HALF], F32, ph1)
        junk = sb("junk", [P, 5, BANK], BF16, ph1)
        junkx = sb("junkx", [P, D], BF16, ph1)
        qkss = sb("qkss", [P, 5], F32, ph1)
        qkr = sb("qkr", [P, 3], F32, ph1)
        qT = sb("qT", [P, BT, KV, REP, C], F32, ph1)
        kT = sb("kT", [P, KV, BT, C], F32, ph1)
        v = [sb(f"v{i}", [P, KV * DH], F32, ph1) for i in range(2)]
        sm = sb("sm", [P, KV * BT, C], F32, ph1)
        smax = sb("smax", [P, KV * BT], F32, ph1)
        prob = sb("prob", [P, KV * BT, C], F32, ph1)
        psm = sb("psm", [P, KV * BT], F32, ph1)
        pT = sb("pT", [P, KV, BT, P], F32, ph1)
        oT_h = sb("oT_h", [P, H, BT, C], F32R, ph1)
        ph0 = ExitStack()
        wbd0 = sb("wbd0", [P, T, P], F32, ph0)
        idx = sb("idx", [P, 2, T], I32, ph0)
        rowno = sb("rowno", [P, 1], F32, ph0)
        cidx = sb("cidx", [P, 2, T], I32, ph0)
        crows = sb("crows", [P, 2, T, C], F32, ph0)
        ph0.close()
        oT_l = sb("oT_l", [P, H, BT, C], F32R, ph1)
        ph1.close()

        ph2 = ExitStack()
        wg_s = sb("wg_s", [P, E0, KD, P], F32, ph2)
        wu_s = sb("wu_s", [P, E0, KD, P], F32, ph2)
        wd_s = sb("wd_s", [P, E0, D], F32, ph2)
        w1_s = sb("w1_s", [P, KD, (NR + NS) * P], F32, ph2)
        w3_s = sb("w3_s", [P, KD, (NR + NS) * P], F32, ph2)
        w2_s = sb("w2_s", [P, NR + NS, D], F32, ph2)
        sel0 = sb("sel0", [P, E0, P], BF16, ph2)
        sel1 = sb("sel1", [P, NR + NS, P], BF16, ph2)
        featT_h = sb("featT_h", [P, KD, NT], F32R, ph2)
        featT_l = sb("featT_l", [P, KD, NT], F32R, ph2)
        outT = sb("outT", [P, KD, NT], F32, ph2)
        hn2 = outT[:, :, :].rearrange("p k n -> p (k n)").rearrange("p (t d) -> p t d", d=D)
        combT = sb("combT", [P, NT], BF16, ph2)
        wA_h = [sb(f"wA_h{i}", [P, KD, P], F32R, ph2) for i in range(2)]
        wA_l = [sb(f"wA_l{i}", [P, KD, P], F32R, ph2) for i in range(2)]
        wB_h = [sb(f"wB_h{i}", [P, KD, P], F32R, ph2) for i in range(2)]
        wB_l = [sb(f"wB_l{i}", [P, KD, P], F32R, ph2) for i in range(2)]
        wC_h = [sb(f"wC_h{i}", [P, D], F32R, ph2) for i in range(2)]
        wC_l = [sb(f"wC_l{i}", [P, D], F32R, ph2) for i in range(2)]
        gate_s = sb("gate_s", [P, BANK], F32, ph2)
        prod = sb("prod", [P, 2, BANK], F32, ph2)
        act = sb("act", [P, 2, BANK], F32, ph2)
        act_h = sb("act_h", [P, 4, BANK], F32R, ph2)
        act_l = sb("act_l", [P, 4, BANK], F32R, ph2)
        EM = max(E0, E1)
        sig = sb("sig", [P, T * EM], F32, ph2)
        score = sb("score", [P, T * EM], F32, ph2)
        top8 = sb("top8", [P, T, 8], F32, ph2)
        gt = sb("gt", [P, T * EM], F32, ph2)
        eq = sb("eq", [P, T * EM], F32, ph2)
        scanA = sb("scanA", [P, T, 2 * EM], F32, ph2)
        scanB = sb("scanB", [P, T, 2 * EM], F32, ph2)
        rows = sb("rows", [P, 2, T], F32, ph2)
        comb = sb("comb", [P, T * EM], F32, ph2)
        comb3 = sb("comb3", [P, T, 3 * EM + 2], BF16, ph2)
        ph2.close()

        s_x = sem("x_loaded")
        s_idx = sem("idx_loaded")
        s_cst = sem("consts_loaded")
        s_cst2 = sem("router_loaded")
        s_sel = sem("sel_loaded")
        s_wst = [sem(f"stage_loaded{i}") for i in range(3)]
        s_cidx = sem("cond_rows_numbered")
        s_crow = [sem(f"cond_rows_loaded{i}") for i in range(2)]
        s_wbd = [sem(f"cond_blocks_placed{i}") for i in range(2)]
        s_zero = sem("wbd_zeroed")
        s_wh = sem("stage_high")
        s_wl = sem("stage_low")
        s_wlo = sem("stage_low_wo")
        s_wtab = sem("rope_tables")
        s_c0 = sem("cond0_rows")
        s_res = sem("cond0_copied")
        s_ssq = sem("squares_summed")
        s_ms = sem("mean_squares")
        s_rms = sem("rms_ready")
        s_hn = sem("hn_ready")
        s_hT = sem("hT_transposed")
        s_hTh = sem("hT_high")
        s_hTl = sem("hT_low")
        s_k = sem("k_ready")
        s_v = sem("v_ready")
        s_q = sem("q_ready")
        s_kss = sem("k_squares")
        s_qss = sem("q_squares")
        s_kms = sem("k_mean")
        s_qsum = sem("q_squares_summed")
        s_qms = sem("q_mean")
        s_kr = sem("k_rms")
        s_qr = sem("q_rms")
        s_kpost = sem("k_scaled")
        s_qpost = sem("q_scaled")
        s_krot = sem("k_rotated")
        s_qrot = sem("q_rotated")
        s_vc = sem("v_copied")
        s_tr = sem("qk_transposed")
        s_trA = sem("qT_even_copied")
        s_trD = sem("kT_qT_odd_copied")
        s_sc = sem("scores_ready")
        s_sm = sem("scores_masked")
        s_mx = sem("scores_max")
        s_sub = sem("scores_less_max")
        s_exp = sem("exp_done")
        s_sum2 = sem("exp_sums")
        s_sum = sem("exp_sums_inverted")
        s_p = sem("probs_ready")
        s_pT = sem("pT_transposed")
        s_pTA = sem("pT_batches01")
        s_pTD = sem("pT_batches23")
        s_pTz = sem("pT_zeroed")
        s_o = sem("oT_ready")
        s_oh = sem("oT_high")
        s_ol = sem("oT_low")
        s_wo = sem("wo_done")
        s_x1 = sem("x1_ready")
        s_dve = sem("dve_chain")
        s_pool = sem("pool_chain")
        s_w0 = [sem(f"moe0_w_loaded{i}") for i in range(2)]
        s_w1 = [sem("moe1_w_loaded")]
        s_pad = sem("shared_padding_zeroed")
        s_hn2 = sem("hn2_ready")
        s_x2 = sem("x2_ready")
        s_fT = [sem(f"featT_transposed{i}") for i in range(2)]
        s_fTh = [sem(f"featT_high{i}") for i in range(2)]
        s_fTl = [sem(f"featT_low{i}") for i in range(2)]
        s_rwh = sem("router_w_high")
        s_rwl = sem("router_w_low")
        s_lg = [sem(f"logits{i}") for i in range(2)]
        s_sig = [sem(f"sigmoid{i}") for i in range(2)]
        s_cb3 = [sem(f"comb_parts{i}") for i in range(2)]
        s_cbT = [sem(f"combT_transposed{i}") for i in range(2)]
        s_cbc = [sem(f"combT_copied{i}") for i in range(2)]
        s_cz = sem("combT_zeroed")
        s_wsh = [sem(f"chunk_wab_high{i}") for i in range(2)]
        s_wsl = [sem(f"chunk_wab_low{i}") for i in range(2)]
        s_wch = [sem(f"chunk_wc_high{i}") for i in range(2)]
        s_wcl = [sem(f"chunk_wc_low{i}") for i in range(2)]
        s_G = [sem(f"gate_ready{i}") for i in range(2)]
        s_U = [sem(f"up_ready{i}") for i in range(2)]
        s_BC = [sem(f"weight_rows_ready{i}") for i in range(2)]
        s_fst = [sem(f"first_ready{i}") for i in range(2)]
        s_prd = [sem(f"product_ready{i}") for i in range(2)]
        s_sil = [sem(f"silu_ready{i}") for i in range(2)]
        s_act = [sem(f"act_ready{i}") for i in range(2)]
        s_ah = [sem(f"act_high{i}") for i in range(2)]
        s_al = [sem(f"act_low{i}") for i in range(2)]
        s_D = [sem(f"down_done{i}") for i in range(2)]
        s_mx0 = [sem(f"mixture_copied{i}") for i in range(2)]
        s_xs = sem("residual_summed")
        s_bk = [sem(f"rows_back{i}") for i in range(2)]
        s_fin = sem("out_rows_ready")
        s_out = sem("out_stored")

        block = top.enter_context(nc.Block())

        qv = qbanks[:, :, :].rearrange("p b n -> p (b n)")
        bT, bK, bV, bP = bank[0], bank[1], bank[2], bank[3]
        X0, X1, X2, X3 = bank
        tr_bank = [X0, X1, X0, qbanks[:, 3, :], X0]
        o_bank = [X0, X1, X2, X3]
        NTR = len(tr_bank)
        FRONT = 10

        moes = [dict(sems=s_w0, runs=[(0, E0, True)], E=E0, K=TOPK0, sel=sel0),
                dict(sems=s_w1, runs=[(0, NR, False), (NR, NS, True)], E=E1, K=TOPK1, sel=sel1)]

        def chunk_weights(m, c):
            if m == 0:
                return (wg_s[:, bass.ds(c, 1), :, :].rearrange("p a k n -> p (a k) n"),
                        wu_s[:, bass.ds(c, 1), :, :].rearrange("p a k n -> p (a k) n"),
                        wd_s[:, bass.ds(c, 1), :].rearrange("p a n -> p (a n)"))
            return (w1_s[:, :, bass.ds(c * P, P)], w3_s[:, :, bass.ds(c * P, P)],
                    w2_s[:, bass.ds(c, 1), :].rearrange("p a n -> p (a n)"))

        @block.sync
        def _(sp):
            sp.dma_start(idx[:, 0, :], idx0).then_inc(s_idx, 16)
            sp.dma_start(idx[:, 1, :], idx1).then_inc(s_idx, 16)
            sp.dma_start(rowno[:], c_rowno).then_inc(s_idx, 16)
            sp.dma_start(xin[:], x_v).then_inc(s_x, 16)

            def piece(n):
                if n < NPIECE:
                    src = [wk, wv][n] if n < 2 else wq[:, (n - 2) * BANK:(n - 1) * BANK]
                    return src.rearrange("(k p) n -> p k n", p=P), "p (k n) -> p k n", dict(k=KD)
                h = (n - NPIECE) * 4
                return (wo[h * DH:(h + 4) * DH, :].rearrange("(h p) n -> p h n", p=P),
                        "p (h n) -> p h n", dict(h=4))

            def load_piece(n):
                if 3 <= n < NPIECE + 3:
                    sp.wait_ge(s_wl, n - 2)
                elif n >= 3:
                    sp.wait_ge(s_wlo, n - 2 - NPIECE)
                src, how, kw = piece(n)
                sp.dma_start(wstage[:, n % 3, :].rearrange(how, **kw), src).then_inc(s_wst[n % 3], 16)

            for n in range(3):
                load_piece(n)
            sp.dma_start(ident[:], c_ident).then_inc(s_cst, 16)
            sp.dma_start(identb[:], c_identb.bitcast(BF16)).then_inc(s_cst, 16)
            sp.dma_start(mask[:], c_mask).then_inc(s_cst, 16)
            sp.dma_start(cosT[:], c_cos).then_inc(s_cst, 16)
            sp.dma_start(sinT[:], c_sin).then_inc(s_cst, 16)
            sp.dma_start(wa[:, 0:H, :].rearrange("p h d -> p (h d)"),
                         qn_w.rearrange("(a n) -> a n", a=1).broadcast_to([P, H * DH])).then_inc(s_cst, 16)
            sp.dma_start(wa[:, H:QK, :].rearrange("p h d -> p (h d)"),
                         kn_w.rearrange("(a n) -> a n", a=1).broadcast_to([P, KV * DH])).then_inc(s_cst, 16)
            sp.dma_start(lnw[:, 0, :], ln1_w).then_inc(s_cst, 16)
            sp.dma_start(lnw[:, 1, :], ln2_w).then_inc(s_cst, 16)
            for n in range(3, NPIECE + NWO):
                load_piece(n)
            sp.dma_start(rw[:], router_w.rearrange("(k p) e -> p k e", p=P)).then_inc(s_cst2, 16)
            sp.dma_start(gw[:], gate_wT.rearrange("(k p) e -> p k e", p=P)).then_inc(s_cst2, 16)
            sp.dma_start(rbias[:], router_b.rearrange("(a n) -> a n", a=1).broadcast_to([P, E0])).then_inc(s_cst2, 16)
            sp.dma_start(gbias[:], gate_b.rearrange("(a n) -> a n", a=1).broadcast_to([P, E1])).then_inc(s_cst2, 16)

            sp.wait_ge(s_x1, T)
            sp.wait_ge(s_ssq, 2 * T)
            half = E0 // 2
            for lo, s in ((0, s_w0[0]), (half, s_w0[1])):
                e = slice(lo, lo + half)
                sp.dma_start(wg_s[:, e], wg[e].rearrange("e (k p) i -> p e k i", p=P)).then_inc(s, 16)
                sp.dma_start(wu_s[:, e], wu[e].rearrange("e (k p) i -> p e k i", p=P)).then_inc(s, 16)
                sp.dma_start(wd_s[:, e], wd[e].rearrange("e i d -> i e d")).then_inc(s, 16)
            sp.wait_ge(s_cz, 3)
            sp.dma_start(sel0[0:c_sel0.shape[0]], c_sel0.bitcast(BF16)).then_inc(s_sel, 16)
            sp.dma_start(sel1[0:c_sel1.shape[0]], c_sel1.bitcast(BF16)).then_inc(s_sel, 16)
            nr = NR * P
            for src, shr, dst, s in ((w1r, w1s, w1_s, s_w1[0]), (w3r, w3s, w3_s, s_w1[0])):
                for k in range(KD):
                    sp.dma_start(dst[:, k, 0:nr].rearrange("p (e c) -> p e c", e=E1),
                                 src[:, k * P:(k + 1) * P, :].rearrange("e p c -> p e c")).then_inc(s, 16)
                sp.dma_start(dst[:, :, nr:nr + HID], shr.rearrange("(k p) c -> p k c", p=P)).then_inc(s, 16)
            sp.dma_start(w2_s[:, 0:NR, :],
                         w2r.rearrange("e c d -> (e c) d").rearrange("(n p) d -> p n d", p=P)).then_inc(s_w1[0], 16)
            sp.dma_start(w2_s[:, NR, :], w2s[0:P, :]).then_inc(s_w1[0], 16)
            sp.wait_ge(s_pad, 3)
            sp.dma_start(w2_s[0:HREM, NR + 1, :], w2s[P:HID, :]).then_inc(s_w1[0], 16)

            for t in range(T):
                sp.wait_ge(s_fin, t + 1)
                sp.dma_start(out_v[:, t, :], xin[:, t, :]).then_inc(s_out, 16)
            sp.wait_ge(s_out, 16 * T)

        @block.tensor
        def _(pe):
            def passes(dst, lh, ll, rh, rl, start, stop):
                pe.matmul(dst, lh, rh, start=start, stop=False)
                pe.matmul(dst, lh, rl, start=False, stop=False)
                return pe.matmul(dst, ll, rh, start=False, stop=stop)

            pe.wait_ge(s_x, 16)
            pe.wait_ge(s_wbd[0], BT)
            for t in range(T):
                pe.matmul(qbanks[:, t // 2, (t % 2) * D:(t % 2 + 1) * D], wbd0[:, t, :], xin[:, t, :],
                          start=True, stop=True).then_inc(s_c0, 1)
            pe.wait_ge(s_cst, 16 * 9)

            def columns(dst, n):
                for k in range(KD):
                    last = passes(dst, hT_h[:, k, :], hT_l[:, k, :], wqkv_h[:, n, k, :], wqkv_l[:, n, k, :],
                                  k == 0, k == KD - 1)
                return last

            def rows_T(t):
                pe.wait_ge(s_hn, t + 1)
                for k in range(KD):
                    last = pe.transpose(X2[:, k * P:(k + 1) * P], hn[:, k * P:(k + 1) * P], ident[:])
                last.then_inc(s_hT, 1)

            def heads_T(n):
                for i in range(4):
                    h = H + i if n == 0 else (n - 1) * REP + i
                    last = pe.transpose(tr_bank[n][:, i * P:(i + 1) * P], qk[:, h, :], ident[:])
                last.then_inc(s_tr, 1)

            def scores(g):
                for a in range(BT):
                    u = (g * BT + a) * C
                    last = pe.matmul(X1[:, u:u + C], qT[:, a, g, :, :].rearrange("p r c -> p (r c)"), kT[:, g, a, :],
                                     start=True, stop=True)
                if g == KV - 1:
                    last.then_inc(s_sc, 1)

            def probs_T():
                for g in range(KV):
                    last = pe.transpose(X1[:, g * P:(g + 1) * P],
                                        prob[:, g * BT:(g + 1) * BT, :].rearrange("p a c -> p (a c)"), ident[:])
                last.then_inc(s_pT, 1)

            def values(g, par):
                pe.matmul(o_bank[g][:], v[par][:, g * DH:(g + 1) * DH], pT[:, g, :, :].rearrange("p a n -> p (a n)"),
                          start=True, stop=True).then_inc(s_o, 1)

            def output(lo, hi):
                for h in range(lo, hi):
                    last = passes(X3[:, 0:D], oT_h[:, h, :, :].rearrange("p a c -> p (a c)"),
                                  oT_l[:, h, :, :].rearrange("p a c -> p (a c)"),
                                  wo_h[:, h, :], wo_l[:, h, :], h == 0, h == H - 1)
                if hi == H:
                    last.then_inc(s_wo, 1)

            def step(t, par, q=True, mid=True, wo=True, t0=False):
                if mid:
                    pe.wait_ge(s_krot, t)
                    if wo:
                        pe.wait_ge(s_ol, KV * t - 7)
                    heads_T(0)
                    pe.wait_ge(s_qrot, 2 * t - 1)
                    if wo:
                        pe.wait_ge(s_ol, KV * t - 6)
                    heads_T(1)
                if q:
                    pe.wait_ge(s_hTl, t + 1)
                    if mid and wo:
                        pe.wait_ge(s_ol, KV * t - 5)
                    if t0:
                        pe.wait_ge(s_wl, 1)
                    columns(X2[:], 0).then_inc(s_k, 1)
                if mid:
                    pe.wait_ge(s_trD, 3 * t - 2)
                    heads_T(2)
                if q:
                    if mid:
                        if wo:
                            pe.wait_ge(s_ol, KV * t - 4)
                        else:
                            pe.wait_ge(s_vc, t)
                    if t0:
                        pe.wait_ge(s_wl, 2)
                    columns(X3[:], 1).then_inc(s_v, 1)
                if mid:
                    pe.wait_ge(s_qrot, 2 * t)
                    heads_T(3)
                    pe.wait_ge(s_trA, 2 * t - 1)
                    scores(0)
                if q:
                    if t0:
                        pe.wait_ge(s_wl, 3)
                    columns(qbanks[:, 0, :], 2).then_inc(s_q, 1)
                if mid:
                    pe.wait_ge(s_trD, 3 * t - 1)
                    heads_T(4)
                    scores(1)
                if q:
                    if t0:
                        pe.wait_ge(s_wl, 4)
                    columns(qbanks[:, 1, :], 3).then_inc(s_q, 1)
                if mid:
                    pe.wait_ge(s_trA, 2 * t)
                    scores(2)
                    pe.wait_ge(s_trD, 3 * t)
                    scores(3)
                if q:
                    if t0:
                        pe.wait_ge(s_wl, 5)
                    columns(qbanks[:, 2, :], 4).then_inc(s_q, 1)
                    if t0:
                        pe.wait_ge(s_wl, 6)
                    columns(qbanks[:, 3, :], 5).then_inc(s_q, 1)
                    pe.wait_ge(s_kpost, t + 1)
                    rows_T(t + 1)
                if wo:
                    if q:
                        pe.wait_ge(s_vc, t + 1)
                    pe.wait_ge(s_ol, KV * t - 4)
                    output(0, FRONT)
                if mid:
                    pe.wait_ge(s_p, t)
                    probs_T()
                if wo:
                    output(FRONT, H)
                if mid:
                    pe.wait_ge(s_pTA, t)
                    pe.wait_ge(s_pTD, t)
                    values(0, 1 - par)
                    values(1, 1 - par)
                    if q:
                        pe.wait_ge(s_hTl, t + 2)
                    values(2, 1 - par)
                    if wo:
                        pe.wait_ge(s_x1, t - 1)
                    else:
                        pe.wait_ge(s_vc, t + 1)
                    values(3, 1 - par)

            rows_T(0)
            pe.wait_ge(s_res, 4)
            step(0, 0, mid=False, wo=False, t0=True)
            step(1, 1, wo=False)
            pe.wait_ge(s_wlo, NWO)
            with pe.Fori(1, T // 2) as i:
                step(2 * i, 0)
                step(2 * i + 1, 1)
            step(T, 0, q=False)
            step(T + 1, 1, q=False, mid=False)

            pe.wait_ge(s_rwl, 2)

            def features0():
                pe.wait_ge(s_x1, T)
                for t in range(T):
                    pe.wait_ge(s_hn2, t + 1)
                    if t >= 4:
                        pe.wait_ge(s_fTl[0], t - 3)
                    b = qbanks[:, t % 4, 0:KD * P].rearrange("p (k n) -> p k n", k=KD)
                    for k in range(KD):
                        last = pe.transpose(b[:, k, :], hn2[:, t, k * P:(k + 1) * P], ident[:])
                    last.then_inc(s_fT[0], 1)

            def features1():
                pe.wait_ge(s_wbd[1], BT)
                for t in range(T):
                    pe.wait_ge(s_x2, t + 1)
                    if t >= 4:
                        pe.wait_ge(s_fTl[1], t - 3)
                    b = qbanks[:, t % 4, 0:KD * P].rearrange("p (k n) -> p k n", k=KD)
                    for k in range(KD):
                        last = pe.matmul(b[:, k, :], x1[:, t, k * P:(k + 1) * P], wbd1[:, t, :],
                                         start=True, stop=True)
                    last.then_inc(s_fT[1], 1)

            def logits(m, E, w_h, w_l):
                for t in range(T):
                    pe.wait_ge(s_fTl[m], t + 1)
                    r = slice(t * P, (t + 1) * P)
                    for k in range(KD):
                        last = passes(bV[:, t * E:(t + 1) * E], featT_h[:, k, r], featT_l[:, k, r],
                                      w_h[:, k, :], w_l[:, k, :], k == 0, k == KD - 1)
                last.then_inc(s_lg[m], 1)

            def weight_rows(m, E):
                pe.wait_ge(s_cb3[m], 1)
                n = 3 * E + 2 * m
                cb = bP[:, :].bitcast(BF16)
                for t in range(T):
                    last = pe.transpose(cb[0:n, t * P:(t + 1) * P], comb3[:, t, 0:n], identb[:])
                last.then_inc(s_cbT[m], 1)
                pe.wait_ge(s_cbc[m], 1)

            def mixture(m):
                sel = moes[m]["sel"]
                def down(q, n, start, stop):
                    j, hf = n // 2, n % 2
                    pe.wait_ge(s_al[m], 4 * q + n + 1)
                    if hf == 0:
                        pe.wait_ge(s_wcl[m], 2 * q + j + 1)
                    for d in range(KD):
                        cs = slice(d * P, (d + 1) * P)
                        last = passes(qbanks[:, d * NH + hf, :], wC_h[j][:, cs], wC_l[j][:, cs],
                                      act_h[:, n, :], act_l[:, n, :], start, stop)
                    last.then_inc(s_D[m], 1)

                def pair(q, first):
                    for n in range(4):
                        j, hf = n // 2, n % 2
                        s = 4 * q + n
                        r = slice(hf * BANK, (hf + 1) * BANK)
                        if hf == 0:
                            pe.wait_ge(s_wsl[m], 2 * q + j + 1)
                        if not (first and n == 0):
                            pe.wait_ge(s_fst[m], s)
                        for k in range(KD):
                            last = passes(bT[:], wA_h[j][:, k, :], wA_l[j][:, k, :], featT_h[:, k, r],
                                          featT_l[:, k, r], k == 0, k == KD - 1)
                        last.then_inc(s_G[m], 1)
                        if not (first and n == 0):
                            pe.wait_ge(s_prd[m], s)
                        for k in range(KD):
                            last = passes(bK[:], wB_h[j][:, k, :], wB_l[j][:, k, :], featT_h[:, k, r],
                                          featT_l[:, k, r], k == 0, k == KD - 1)
                        last.then_inc(s_U[m], 1)
                        if not (first and n < 2):
                            pe.wait_ge(s_act[m], s - 1)
                        pe.matmul([bV, bP][n % 2][:], sel[:, bass.ds(2 * q + j, 1), :].rearrange("p a n -> p (a n)"),
                                  combT[:, r], start=True, stop=True).then_inc(s_BC[m], 1)
                        if n >= 2:
                            down(q, n - 2, first, False)
                        elif not first:
                            down(q - 1, n + 2, False, False)

                q_all = sum(n for _, n, _ in moes[m]["runs"]) // 2
                pair(0, True)
                with pe.Fori(1, q_all) as q:
                    pair(q, False)
                down(q_all - 1, 2, False, True)
                down(q_all - 1, 3, False, True)

            def back(m):
                pe.wait_ge(s_mx0[m], 4)
                for t in range(T):
                    if t >= 4:
                        pe.wait_ge(s_x2 if m == 0 else s_fin, t - 3)
                    b = bank[t % 4]
                    for k in range(KD):
                        last = pe.transpose(b[:, k * P:(k + 1) * P], outT[:, k, t * P:(t + 1) * P], ident[:])
                    last.then_inc(s_bk[m], 1)

            features0()
            logits(0, E0, rw_h, rw_l)
            weight_rows(0, E0)
            pe.wait_ge(s_sel, 32)
            mixture(0)
            back(0)
            features1()
            logits(1, E1, gw_h, gw_l)
            weight_rows(1, E1)
            mixture(1)
            back(1)

        @block.scalar
        def _(act_e):
            for n in range(NPIECE + NWO):
                act_e.wait_ge(s_wst[n % 3], 16 * (n // 3 + 1))
                dst = (wqkv_h[:, n, :, :].rearrange("p k n -> p (k n)") if n < NPIECE else
                       wo_h[:, 4 * (n - NPIECE):4 * (n - NPIECE) + 4, :].rearrange("p h n -> p (h n)"))
                nc.scalar.activation(dst, wstage[:, n % 3, :], ACT.Copy).then_inc(s_wh, 1)
                if n == 3:
                    for t in range(T):
                        act_e.wait_ge(s_res, t // 2 + 1)
                        if t:
                            act_e.wait_ge(s_ssq, t)
                        nc.scalar.activation(junkx[:], x1[:, t, :], ACT.Square,
                                             accum_out=ssq[:, t:t + 1]).then_inc(s_ssq, 1)
            act_e.wait_ge(s_cst, 16 * 9)

            def heads_copy(t, n):
                act_e.wait_ge(s_tr, NTR * t - 4 + n)
                nc.scalar.activation(qT[:, :, n - 1, :, :].rearrange("p a r c -> p r a c"),
                                     tr_bank[n][:, :].rearrange("p (r a c) -> p r a c", r=REP, a=BT),
                                     ACT.Copy).then_inc(s_trA, 1)

            def rows_high(t):
                act_e.wait_ge(s_hT, t + 1)
                for k in range(KD):
                    last = nc.scalar.activation(hT_h[:, k, :], X2[:, k * P:(k + 1) * P], ACT.Copy,
                                                scale=lnw[:, 0, k:k + 1])
                last.then_inc(s_hTh, 1)

            def q_squares(t, n, mid):
                act_e.wait_ge(s_q, 4 * t + n + 1)
                if mid and n == 0:
                    act_e.wait_ge(s_qsum, t)
                nc.scalar.activation(junk[:, n, :], qbanks[:, n, :], ACT.Square,
                                     accum_out=qkss[:, n:n + 1]).then_inc(s_qss, 1)

            def step(t, par, q=True, mid=True, wo=True):
                if mid:
                    heads_copy(t, 1)
                if q:
                    act_e.wait_ge(s_k, t + 1)
                    if mid:
                        act_e.wait_ge(s_kms, t)
                    nc.scalar.activation(junk[:, 4, :], X2[:], ACT.Square, accum_out=qkss[:, 4:5]).then_inc(s_kss, 1)
                    act_e.wait_ge(s_v, t + 1)
                    nc.scalar.activation(v[par][:], X3[:], ACT.Copy).then_inc(s_vc, 1)
                if mid:
                    heads_copy(t, 3)
                if q:
                    for n in range(3):
                        q_squares(t, n, mid)
                if mid:
                    act_e.wait_ge(s_sub, t)
                    nc.scalar.activation(prob[:, :, :], sm[:, :, :], ACT.Exp, scale=SCALE).then_inc(s_exp, 1)
                if q:
                    q_squares(t, 3, mid)
                    rows_high(t + 1)
                if mid:
                    act_e.wait_ge(s_pT, t)
                    for a in range(2):
                        r = slice(a * C, (a + 1) * C)
                        last = nc.scalar.activation(pT[r, :, a, :], X1[r, :].rearrange("p (g n) -> p g n", g=KV), ACT.Copy)
                    last.then_inc(s_pTA, 1)
                if wo:
                    act_e.wait_ge(s_x1, t - 1)
                    act_e.wait_ge(s_ssq, t + T - 2)
                    u = bass.ds(t - 2, 1)
                    nc.scalar.activation(junkx[:], x1[:, u, :].rearrange("p a d -> p (a d)"),
                                         ACT.Square, accum_out=ssq[:, u]).then_inc(s_ssq, 1)
                if mid:
                    for g in range(KV):
                        act_e.wait_ge(s_o, KV * t - 3 + g)
                        nc.scalar.activation(oT_h[:, g * REP:(g + 1) * REP, :, :],
                                             o_bank[g][:, :].rearrange("p (a r c) -> p r a c", a=BT, c=C),
                                             ACT.Copy).then_inc(s_oh, 1)

            act_e.wait_ge(s_pTz, 1)
            act_e.wait_ge(s_rms, 1)
            rows_high(0)
            step(0, 0, mid=False, wo=False)
            step(1, 1, wo=False)
            with act_e.Fori(1, T // 2) as i:
                step(2 * i, 0)
                step(2 * i + 1, 1)
            step(T, 0, q=False)
            step(T + 1, 1, q=False, mid=False)
            act_e.wait_ge(s_cst2, 16 * 4)
            nc.scalar.activation(rw_h[:], rw[:], ACT.Copy).then_inc(s_rwh, 1)
            nc.scalar.activation(gw_h[:], gw[:], ACT.Copy).then_inc(s_rwh, 1)

            def features_high(m):
                for t in range(T):
                    act_e.wait_ge(s_fT[m], t + 1)
                    b = qbanks[:, t % 4, 0:KD * P].rearrange("p (k n) -> p k n", k=KD)
                    r = slice(t * P, (t + 1) * P)
                    if m == 0:
                        for k in range(KD):
                            last = nc.scalar.activation(featT_h[:, k, r], b[:, k, :], ACT.Copy,
                                                        scale=lnw[:, 1, k:k + 1])
                        last.then_inc(s_fTh[m], 1)
                    else:
                        nc.scalar.activation(featT_h[:, :, r], b, ACT.Copy).then_inc(s_fTh[m], 1)

            def router(m, E):
                act_e.wait_ge(s_lg[m], 1)
                nc.scalar.activation(sig[:, 0:T * E], bV[:, 0:T * E], ACT.Sigmoid).then_inc(s_sig[m], 1)
                n = 3 * E + 2 * m
                act_e.wait_ge(s_cz, 1)
                act_e.wait_ge(s_cbT[m], 1)
                nc.scalar.activation(combT[0:n, :], bP[0:n, :].bitcast(BF16), ACT.Copy).then_inc(s_cbc[m], 1)

            def run_mixture(m):
                q_all = sum(n for _, n, _ in moes[m]["runs"]) // 2
                act_e.wait_ge(moes[m]["sems"][0], 16 * (3 if m == 0 else 9))
                if m == 1:
                    act_e.wait_ge(s_pad, 3)

                def split_ab(c, j, later):
                    if later:
                        act_e.wait_ge(s_U[m], 2 * c - 2)
                        act_e.wait_ge(s_wsl[m], c - 1)
                    wa_s, wb_s, _ = chunk_weights(m, c)
                    nc.scalar.activation(wA_h[j][:], wa_s, ACT.Copy)
                    nc.scalar.activation(wB_h[j][:], wb_s, ACT.Copy).then_inc(s_wsh[m], 1)

                def split_c(c, j, later):
                    if later:
                        act_e.wait_ge(s_D[m], 2 * c - 2)
                        act_e.wait_ge(s_wcl[m], c - 1)
                    nc.scalar.activation(wC_h[j][:], chunk_weights(m, c)[2], ACT.Copy).then_inc(s_wch[m], 1)

                def high(q, n, later):
                    act_e.wait_ge(s_act[m], 4 * q + n + 1)
                    if later:
                        act_e.wait_ge(s_D[m], 4 * q + n - 3)
                    nc.scalar.activation(act_h[:, n, :], act[:, n % 2, :], ACT.Copy).then_inc(s_ah[m], 1)

                def pair(q, first, second, gated, more):
                    for n in range(4):
                        s = 4 * q + n
                        act_e.wait_ge(s_G[m], s + 1)
                        if not (first and n == 0):
                            act_e.wait_ge(s_prd[m], s)
                        nc.scalar.activation(gate_s[:], bT[:], ACT.Silu if gated else ACT.Copy).then_inc(s_fst[m], 1)
                        if n:
                            high(q, n - 1, not first)
                        elif not first:
                            high(q - 1, 3, not second)
                        if not gated:
                            act_e.wait_ge(s_prd[m], s + 1)
                            nc.scalar.activation(prod[:, 1, :], prod[:, 0, :], ACT.Silu).then_inc(s_sil[m], 1)
                        if n == 0:
                            split_ab(2 * q + 1, 1, not first)
                        if n == 1:
                            split_c(2 * q, 0, not first)
                        if n == 2 and more:
                            split_ab(2 * q + 2, 0, True)
                        if n == 3:
                            split_c(2 * q + 1, 1, not first)

                split_ab(0, 0, False)
                if m == 0:
                    act_e.wait_ge(moes[m]["sems"][1], 16 * 3)
                runs = [(lo // 2, (lo + n) // 2, g) for lo, n, g in moes[m]["runs"]]
                for lo, hi, gated in runs:
                    if lo == 0:
                        pair(0, True, False, gated, True)
                        pair(1, False, True, gated, True)
                        lo = 2
                    end = hi - 1 if hi == q_all else hi
                    if end > lo:
                        with act_e.Fori(lo, end) as q:
                            pair(q, False, False, gated, True)
                    if hi == q_all:
                        pair(q_all - 1, False, False, gated, False)
                high(q_all - 1, 3, True)
                act_e.wait_ge(s_D[m], 4 * q_all)
                for i in range(2):
                    nc.scalar.activation(outT[:, 0, i * BANK:(i + 1) * BANK], qbanks[:, i, :],
                                         ACT.Copy).then_inc(s_mx0[m], 1)

            features_high(0)
            router(0, E0)
            run_mixture(0)
            features_high(1)
            router(1, E1)
            run_mixture(1)

        @block.gpsimd
        def _(pool):
            nc.gpsimd.memset(mhalf[:], -0.5).then_inc(s_zero, 1)
            pool.wait_ge(s_cidx, 1)

            def gather(m, table):
                for t in range(T):
                    nc.gpsimd.indirect_dma_start(
                        crows[:, m, t, :], None, table.rearrange("s c d -> (s c) d"),
                        bass.IndirectOffsetOnAxis(ap=cidx[:, m, t:t + 1].bitcast(U32), axis=0),
                    ).then_inc(s_crow[m], 16)

            gather(0, cw0)
            nc.gpsimd.memset(wbd0[:], 0.0).then_inc(s_zero, 1)
            nc.gpsimd.memset(wbd1[:], 0.0).then_inc(s_zero, 1)
            nc.gpsimd.memset(x1[:, T, :], 0.0).then_inc(s_zero, 1)
            nc.gpsimd.memset(rms[:, T:T + 1], 0.0).then_inc(s_zero, 1)
            nc.gpsimd.memset(pT[:], 0.0).then_inc(s_pTz, 1)
            gather(1, cw1)
            pool.wait_ge(s_cst, 16 * 9)
            for lo_d, hi_d in ((0, HALF), (HALF, 0)):
                nc.gpsimd.tensor_tensor(wb[:, :, lo_d:lo_d + HALF], wa[:, :, hi_d:hi_d + HALF],
                                        sinT[:, lo_d:lo_d + HALF].unsqueeze(1).broadcast_to([P, QK, HALF]),
                                        ALU.mult).then_inc(s_pool, 1)
            pool.wait_ge(s_pool, 2)
            nc.gpsimd.tensor_tensor(wa[:, :, 0:2 * HALF], wa[:, :, 0:2 * HALF],
                                    cosT[:, :].unsqueeze(1).broadcast_to([P, QK, 2 * HALF]),
                                    ALU.mult).then_inc(s_wtab, 1)
            pool.wait_ge(s_ms, 1)
            nc.gpsimd.tensor_tensor(rms[:, 0:T], rms[:, 0:T], mhalf[:], ALU.pow).then_inc(s_rms, 1)
            for n in range(NPIECE, NPIECE + NWO):
                pool.wait_ge(s_wh, n + 1)
                r = slice(4 * (n - NPIECE), 4 * (n - NPIECE) + 4)
                nc.gpsimd.tensor_tensor(wo_l[:, r, :].rearrange("p h n -> p (h n)"), wstage[:, n % 3, :],
                                        wo_h[:, r, :].rearrange("p h n -> p (h n)").bitcast(F32),
                                        ALU.subtract).then_inc(s_wlo, 1)

            def step(t, par, q=True, mid=True):
                if q:
                    pool.wait_ge(s_kms, t + 1)
                    nc.gpsimd.tensor_tensor(qkr[:, 1:2], qkr[:, 1:2], mhalf[:, 0:1], ALU.pow).then_inc(s_kr, 1)
                    pool.wait_ge(s_kpost, t + 1)
                    nc.gpsimd.tensor_tensor(qk[:, H:QK, 0:2 * HALF], qk[:, H:QK, 0:2 * HALF], rot[:, H:QK, :],
                                            ALU.add).then_inc(s_krot, 1)
                if mid:
                    pool.wait_ge(s_mx, t)
                    nc.gpsimd.tensor_tensor(sm[:], sm[:], smax[:].unsqueeze(2).broadcast_to([P, KV * BT, C]),
                                            ALU.subtract).then_inc(s_sub, 1)
                if mid:
                    pool.wait_ge(s_sum, t)
                    nc.gpsimd.tensor_tensor(prob[:], prob[:], psm[:].unsqueeze(2).broadcast_to([P, KV * BT, C]),
                                            ALU.mult).then_inc(s_p, 1)
                if q:
                    pool.wait_ge(s_qms, t + 1)
                    nc.gpsimd.tensor_tensor(qkr[:, 0:1], qkr[:, 0:1], mhalf[:, 0:1], ALU.pow).then_inc(s_qr, 1)
                if q:
                    for i in range(2):
                        r = slice(i * H // 2, (i + 1) * H // 2)
                        pool.wait_ge(s_qpost, 2 * t + i + 1)
                        nc.gpsimd.tensor_tensor(qk[:, r, 0:2 * HALF], qk[:, r, 0:2 * HALF], rot[:, r, :],
                                                ALU.add).then_inc(s_qrot, 1)

            step(0, 0, mid=False)
            step(1, 1)
            with pool.Fori(1, T // 2) as i:
                step(2 * i, 0)
                step(2 * i + 1, 1)
            step(T, 0, q=False)
            pool.wait_ge(s_x1, T)
            pool.wait_ge(s_ssq, 2 * T)
            nc.gpsimd.memset(combT[:], 0.0).then_inc(s_cz, 1)
            nc.gpsimd.memset(sel0[:], 0.0).then_inc(s_cz, 1)
            nc.gpsimd.memset(sel1[:], 0.0).then_inc(s_cz, 1)
            nr = NR * P
            nc.gpsimd.memset(w1_s[:, :, nr + HID:], 0.0).then_inc(s_pad, 1)
            nc.gpsimd.memset(w3_s[:, :, nr + HID:], 0.0).then_inc(s_pad, 1)
            nc.gpsimd.memset(w2_s[:, NR + 1, :], 0.0).then_inc(s_pad, 1)
            pool.wait_ge(s_ms, 2)
            nc.gpsimd.tensor_tensor(rms[:, 0:T], rms[:, 0:T], mhalf[:], ALU.pow).then_inc(s_rms, 1)
            for t in range(T):
                nc.gpsimd.tensor_tensor(xin[:, t, :], xin[:, t, :], x1[:, t, :], ALU.add).then_inc(s_xs, 1)

            def run_mixture(m):
                q_all = sum(n for _, n, _ in moes[m]["runs"]) // 2

                def split_ab(c, j):
                    pool.wait_ge(s_wsh[m], c + 1)
                    wa_s, wb_s, _ = chunk_weights(m, c)
                    nc.gpsimd.tensor_tensor(wA_l[j][:], wa_s, wA_h[j][:].bitcast(F32), ALU.subtract)
                    nc.gpsimd.tensor_tensor(wB_l[j][:], wb_s, wB_h[j][:].bitcast(F32),
                                            ALU.subtract).then_inc(s_wsl[m], 1)

                def split_c(c, j):
                    pool.wait_ge(s_wch[m], c + 1)
                    nc.gpsimd.tensor_tensor(wC_l[j][:], chunk_weights(m, c)[2], wC_h[j][:].bitcast(F32),
                                            ALU.subtract).then_inc(s_wcl[m], 1)

                def low(q, n):
                    pool.wait_ge(s_ah[m], 4 * q + n + 1)
                    nc.gpsimd.tensor_tensor(act_l[:, n, :], act[:, n % 2, :], act_h[:, n, :].bitcast(F32),
                                            ALU.subtract).then_inc(s_al[m], 1)

                def pair(q, first, more):
                    if not first:
                        low(q - 1, 3)
                    split_ab(2 * q + 1, 1)
                    low(q, 0)
                    split_c(2 * q, 0)
                    low(q, 1)
                    if more:
                        split_ab(2 * q + 2, 0)
                    low(q, 2)
                    split_c(2 * q + 1, 1)

                split_ab(0, 0)
                pair(0, True, True)
                with pool.Fori(1, q_all - 1) as q:
                    pair(q, False, True)
                pair(q_all - 1, False, False)
                low(q_all - 1, 3)

            run_mixture(0)
            run_mixture(1)

        @block.vector
        def _(dve):
            chain = [0]

            def then(ins):
                chain[0] += 1
                ins.then_inc(s_dve, 1)
                dve.wait_ge(s_dve, chain[0])

            V = nc.vector
            dve.wait_ge(s_idx, 16 * 3)
            V.tensor_scalar(cidx[:], idx[:], float(C), rowno[:, 0:1], ALU.mult, ALU.add).then_inc(s_cidx, 1)

            def low_piece(n):
                dve.wait_ge(s_wh, n + 1)
                V.tensor_tensor(wqkv_l[:, n, :, :].rearrange("p k n -> p (k n)"), wstage[:, n % 3, :],
                                wqkv_h[:, n, :, :].rearrange("p k n -> p (k n)").bitcast(F32),
                                ALU.subtract).then_inc(s_wl, 1)

            def place(m, wbd):
                dve.wait_ge(s_crow[m], 16 * T)
                for a in range(BT):
                    r = slice(a * C, (a + 1) * C)
                    V.tensor_copy(wbd[r, :, r], crows[r, m, :, :]).then_inc(s_wbd[m], 1)

            for n in range(3):
                low_piece(n)
            dve.wait_ge(s_zero, 5)
            place(0, wbd0)
            low_piece(3)
            for i in range(T // 2):
                dve.wait_ge(s_c0, 2 * i + 2)
                V.tensor_copy(x1[:, 2 * i:2 * i + 2, :].rearrange("p t d -> p (t d)"), qbanks[:, i, :]).then_inc(s_res, 1)
            low_piece(4)
            dve.wait_ge(s_ssq, T)
            V.tensor_scalar(rms[:, 0:T], ssq[:], 1.0 / D, EPS, ALU.mult, ALU.add).then_inc(s_ms, 1)
            low_piece(5)
            place(1, wbd1)
            dve.wait_ge(s_rms, 1)
            V.tensor_scalar(hn[:], x1[:, 0, :], rms[:, 0:1], None, ALU.mult).then_inc(s_hn, 1)
            dve.wait_ge(s_wtab, 1)

            def scaled_heads(r, src, h0, h1):
                V.scalar_tensor_tensor(qk[:, h0:h1, :].rearrange("p h d -> p (h d)"), src, r,
                                       wa[:, h0:h1, :].rearrange("p h d -> p (h d)"), ALU.mult, ALU.mult)
                sv = src.rearrange("p (h d) -> p h d", d=DH)
                for lo, hi in ((0, HALF), (HALF, 0)):
                    last = V.scalar_tensor_tensor(rot[:, h0:h1, lo:lo + HALF], sv[:, :, hi:hi + HALF], r,
                                                  wb[:, h0:h1, lo:lo + HALF], ALU.mult, ALU.mult)
                return last

            def heads_copy(t, n):
                dve.wait_ge(s_tr, NTR * t - 4 + n)
                if n == 0:
                    V.tensor_copy(kT[:, :, :, :].rearrange("p g a c -> p (g a c)"), X0[:]).then_inc(s_trD, 1)
                else:
                    V.tensor_copy(qT[:, :, n - 1, :, :].rearrange("p a r c -> p r a c"),
                                  tr_bank[n][:, :].rearrange("p (r a c) -> p r a c", r=REP, a=BT)).then_inc(s_trD, 1)

            def rows_low(t):
                dve.wait_ge(s_hTh, t + 1)
                for k in range(KD):
                    last = V.scalar_tensor_tensor(hT_l[:, k, :], X2[:, k * P:(k + 1) * P], lnw[:, 0, k:k + 1],
                                                  hT_h[:, k, :].bitcast(F32), ALU.mult, ALU.subtract)
                last.then_inc(s_hTl, 1)

            def step(t, par, q=True, mid=True, wo=True):
                if mid:
                    heads_copy(t, 0)
                if q:
                    dve.wait_ge(s_kss, t + 1)
                    V.tensor_scalar(qkr[:, 1:2], qkss[:, 4:5], 1.0 / (KV * DH), EPS, ALU.mult, ALU.add).then_inc(s_kms, 1)
                if mid:
                    heads_copy(t, 2)
                if q:
                    dve.wait_ge(s_kr, t + 1)
                    scaled_heads(qkr[:, 1:2], X2[:], H, QK).then_inc(s_kpost, 1)
                if mid:
                    heads_copy(t, 4)
                if q:
                    dve.wait_ge(s_hT, t + 1)
                    u = bass.ds(t + 1, 1)
                    V.tensor_scalar(hn[:], x1[:, u, :].rearrange("p a d -> p (a d)"), rms[:, u], None,
                                    ALU.mult).then_inc(s_hn, 1)
                if mid:
                    dve.wait_ge(s_sc, t)
                    V.tensor_tensor(sm[:], X1[:, :].rearrange("p (u c) -> p u c", c=C),
                                    mask[:].unsqueeze(1).broadcast_to([P, KV * BT, C]), ALU.add).then_inc(s_sm, 1)
                    dve.wait_ge(s_sm, t)
                    V.tensor_reduce(smax[:], sm[:], AX.X, ALU.max).then_inc(s_mx, 1)
                    dve.wait_ge(s_exp, t)
                    V.tensor_reduce(psm[:], prob[:], AX.X, ALU.add).then_inc(s_sum2, 1)
                    dve.wait_ge(s_sum2, t)
                    V.reciprocal(psm[:], psm[:]).then_inc(s_sum, 1)
                if q:
                    dve.wait_ge(s_qss, 4 * t + 4)
                    V.tensor_reduce(qkr[:, 2:3], qkss[:, 0:4], AX.X, ALU.add).then_inc(s_qsum, 1)
                    dve.wait_ge(s_qsum, t + 1)
                    V.tensor_scalar(qkr[:, 0:1], qkr[:, 2:3], 1.0 / (H * DH), EPS, ALU.mult, ALU.add).then_inc(s_qms, 1)
                    rows_low(t + 1)
                    dve.wait_ge(s_qr, t + 1)
                    scaled_heads(qkr[:, 0:1], qv[:, 0:2 * BANK], 0, H // 2).then_inc(s_qpost, 1)
                if mid:
                    dve.wait_ge(s_pT, t)
                    for a in range(2, BT):
                        r = slice(a * C, (a + 1) * C)
                        last = V.tensor_copy(pT[r, :, a, :], X1[r, :].rearrange("p (g n) -> p g n", g=KV))
                    last.then_inc(s_pTD, 1)
                if q:
                    scaled_heads(qkr[:, 0:1], qv[:, 2 * BANK:], H // 2, H).then_inc(s_qpost, 1)
                if wo:
                    dve.wait_ge(s_wo, t - 1)
                    u = x1[:, bass.ds(t - 2, 1), :].rearrange("p a d -> p (a d)")
                    V.tensor_tensor(u, u, X3[:, 0:D], ALU.add).then_inc(s_x1, 1)
                if mid:
                    for g in range(KV):
                        dve.wait_ge(s_oh, KV * t - 3 + g)
                        h = slice(g * REP, (g + 1) * REP)
                        V.tensor_tensor(oT_l[:, h, :, :], o_bank[g][:, :].rearrange("p (a r c) -> p r a c", a=BT, c=C),
                                        oT_h[:, h, :, :].bitcast(F32), ALU.subtract).then_inc(s_ol, 1)

            dve.wait_ge(s_pTz, 1)
            rows_low(0)
            step(0, 0, mid=False, wo=False)
            step(1, 1, wo=False)
            with dve.Fori(1, T // 2) as i:
                step(2 * i, 0)
                step(2 * i + 1, 1)
            step(T, 0, q=False)
            step(T + 1, 1, q=False, mid=False)

            dve.wait_ge(s_rwh, 1)
            V.tensor_tensor(rw_l[:], rw[:], rw_h[:].bitcast(F32), ALU.subtract).then_inc(s_rwl, 1)
            dve.wait_ge(s_rwh, 2)
            V.tensor_tensor(gw_l[:], gw[:], gw_h[:].bitcast(F32), ALU.subtract).then_inc(s_rwl, 1)
            dve.wait_ge(s_ssq, 2 * T)
            V.tensor_scalar(rms[:, 0:T], ssq[:], 1.0 / D, EPS, ALU.mult, ALU.add).then_inc(s_ms, 1)
            dve.wait_ge(s_rms, 2)
            for t in range(T):
                V.tensor_scalar(hn2[:, t, :], x1[:, t, :], rms[:, t:t + 1], None, ALU.mult).then_inc(s_hn2, 1)

            def features_low(m):
                for t in range(T):
                    dve.wait_ge(s_fTh[m], t + 1)
                    b = qbanks[:, t % 4, 0:KD * P].rearrange("p (k n) -> p k n", k=KD)
                    r = slice(t * P, (t + 1) * P)
                    if m == 0:
                        for k in range(KD):
                            last = V.scalar_tensor_tensor(featT_l[:, k, r], b[:, k, :], lnw[:, 1, k:k + 1],
                                                          featT_h[:, k, r].bitcast(F32), ALU.mult, ALU.subtract)
                        last.then_inc(s_fTl[m], 1)
                    else:
                        V.tensor_tensor(featT_l[:, :, r], b, featT_h[:, :, r].bitcast(F32),
                                        ALU.subtract).then_inc(s_fTl[m], 1)

            def router(m, E, K, bias):
                def v3(z):
                    return z[:, 0:T * E].rearrange("p (t e) -> p t e", e=E)

                def row(z):
                    return z.unsqueeze(2).broadcast_to([P, T, E])

                V.memset(scanA[:], 0.0)
                then(V.memset(scanB[:], 0.0))
                V.memset(comb3[:, :, 3 * E:3 * E + 2], 1.0)
                dve.wait_ge(s_sig[m], 1)
                then(V.tensor_tensor(v3(score), v3(sig), bias[:].unsqueeze(1).broadcast_to([P, T, E]), ALU.add))
                for t in range(T):
                    last = V.max(top8[:, t, :], score[:, t * E:(t + 1) * E])
                then(last)
                kth = top8[:, :, K - 1:K].broadcast_to([P, T, E])
                V.tensor_tensor(v3(eq), v3(score), kth, ALU.is_equal)
                then(V.tensor_tensor(v3(gt), v3(score), kth, ALU.is_gt))
                then(V.tensor_reduce(rows[:, 0, :], v3(gt), AX.X, ALU.add))
                then(V.tensor_scalar(rows[:, 0, :], rows[:, 0, :], -1.0, float(K), ALU.mult, ALU.add))
                then(V.tensor_copy(scanA[:, :, EM:EM + E], v3(eq)))
                src, dst, step = scanA, scanB, 1
                while step < E:
                    then(V.tensor_tensor(dst[:, :, EM:EM + E], src[:, :, EM:EM + E],
                                         src[:, :, EM - step:EM - step + E], ALU.add))
                    src, dst, step = dst, src, 2 * step
                then(V.tensor_tensor(v3(comb), src[:, :, EM:EM + E], row(rows[:, 0, :]), ALU.is_le))
                then(V.tensor_tensor(v3(comb), v3(comb), v3(eq), ALU.mult))
                then(V.tensor_tensor(v3(comb), v3(comb), v3(gt), ALU.add))
                then(V.tensor_tensor(v3(comb), v3(comb), v3(score if m else sig), ALU.mult))
                then(V.tensor_reduce(rows[:, 1, :], v3(comb), AX.X, ALU.add))
                then(V.reciprocal(rows[:, 1, :], rows[:, 1, :]))
                then(V.tensor_tensor(v3(comb), v3(comb), row(rows[:, 1, :]), ALU.mult))
                then(V.tensor_copy(comb3[:, :, 0:E], v3(comb)))
                then(V.tensor_tensor(v3(comb), v3(comb), comb3[:, :, 0:E], ALU.subtract))
                then(V.tensor_copy(comb3[:, :, E:2 * E], v3(comb)))
                V.tensor_tensor(comb3[:, :, 2 * E:3 * E], v3(comb), comb3[:, :, E:2 * E],
                                ALU.subtract).then_inc(s_cb3[m], 1)

            def run_mixture(m):
                q_all = sum(n for _, n, _ in moes[m]["runs"]) // 2

                def pair(q, first, gated):
                    for n in range(4):
                        s = 4 * q + n
                        dve.wait_ge(s_fst[m], s + 1)
                        dve.wait_ge(s_U[m], s + 1)
                        if not (first and n == 0):
                            dve.wait_ge(s_act[m], s)
                        V.tensor_tensor(prod[:, 0, :], gate_s[:], bK[:], ALU.mult).then_inc(s_prd[m], 1)
                        dve.wait_ge(s_BC[m], s + 1)
                        if gated:
                            dve.wait_ge(s_prd[m], s + 1)
                        else:
                            dve.wait_ge(s_sil[m], s + 1)
                        if not (first and n < 2):
                            dve.wait_ge(s_al[m], s - 1)
                        V.tensor_tensor(act[:, n % 2, :], prod[:, 0 if gated else 1, :], [bV, bP][n % 2][:],
                                        ALU.mult).then_inc(s_act[m], 1)

                pair(0, True, moes[m]["runs"][0][2])
                for lo, n, gated in moes[m]["runs"]:
                    lo, hi = max(lo // 2, 1), (lo + n) // 2
                    if hi - lo > 1:
                        with dve.Fori(lo, hi) as q:
                            pair(q, False, gated)
                    else:
                        pair(lo, False, gated)
                dve.wait_ge(s_D[m], 4 * q_all)
                for i in range(2):
                    V.tensor_copy(outT[:, 1, i * BANK:(i + 1) * BANK], qbanks[:, 2 + i, :]).then_inc(s_mx0[m], 1)

            features_low(0)
            router(0, E0, TOPK0, rbias)
            run_mixture(0)
            dve.wait_ge(s_xs, T)
            for t in range(T):
                dve.wait_ge(s_bk[0], t + 1)
                V.tensor_tensor(x1[:, t, :], xin[:, t, :], bank[t % 4][:, 0:D], ALU.add).then_inc(s_x2, 1)
            features_low(1)
            router(1, E1, TOPK1, gbias)
            run_mixture(1)
            for t in range(T):
                dve.wait_ge(s_bk[1], t + 1)
                V.tensor_tensor(xin[:, t, :], x1[:, t, :], bank[t % 4][:, 0:D], ALU.add).then_inc(s_fin, 1)


_INS = ["x", "itok_B_1_198", "itok_B_0_7", "L0_cond_weights", "L0_ffn_ln1_w", "L0_ffn_ln2_w", "L0_ffn_wq",
        "L0_ffn_wk", "L0_ffn_wv", "L0_ffn_wo", "L0_ffn_qnorm_w", "L0_ffn_knorm_w", "L0_ffn_router_w",
        "L0_ffn_router_bias", "L0_ffn_wg", "L0_ffn_wu", "L0_ffn_wd", "L1_cond_weights", "L1_ffn_gate_w",
        "L1_ffn_gate_b", "L1_ffn_w1_shared", "L1_ffn_w2_shared", "L1_ffn_w3_shared", "L1_ffn_w1_routed",
        "L1_ffn_w2_routed", "L1_ffn_w3_routed"]


def shape_constants():
    import numpy as np
    one = 0x3F80
    p = np.arange(128)
    pos = (p % 32).astype(np.float32)
    inv = (1.0 / np.float32(1000000.0) ** (np.arange(0, 64, 2, dtype=np.float32) / np.float32(64))).astype(np.float32)
    ang = pos[:, None] * inv[None, :]
    cos, sin = np.cos(ang), np.sin(ang)
    mask = np.where(np.arange(32)[None, :] <= pos[:, None], 0.0, -3.0e38).astype(np.float32)
    sel0 = np.zeros((24, 8, 128), np.uint16)
    for e in range(8):
        sel0[[e, 8 + e, 16 + e], e, :] = one
    sel1 = np.zeros((50, 24, 128), np.uint16)
    for c in range(22):
        e = (c * 128 + p) // 176
        for part in range(3):
            sel1[16 * part + e, c, p] = one
    sel1[48, 22:24, :] = one
    return {"c_ident": np.eye(128, dtype=np.float32), "c_identb": np.eye(128, dtype=np.uint16) * np.uint16(one),
            "c_mask": mask, "c_cos": np.concatenate([cos, cos], 1).astype(np.float32),
            "c_sin": np.concatenate([-sin, sin], 1).astype(np.float32), "c_rowno": pos[:, None],
            "c_sel0": sel0, "c_sel1": sel1}


def kernel(**inputs):
    import numpy as _np
    import concourse.bacc as _bacc
    from concourse import mybir as _mybir
    from concourse.bass_utils import run_bass_kernel_spmd as _run

    nc = _bacc.Bacc("TRN2", target_bir_lowering=False, num_devices=1)
    arrays, args = {}, []
    laid = dict(inputs)
    for name in ("itok_B_1_198", "itok_B_0_7"):
        laid[name] = _np.repeat(inputs[name].reshape(8, 4).T, 32, axis=0)
    for name in ("L0_ffn_ln1_w", "L0_ffn_ln2_w"):
        laid[name] = inputs[name].reshape(2, 128).T
    laid["L1_ffn_gate_w"] = inputs["L1_ffn_gate_w"].T
    for name in _INS:
        arrays[f"in_{name}"] = _np.ascontiguousarray(laid[name])
    for name, a in shape_constants().items():
        arrays[f"in_{name}"] = a
    for name, a in arrays.items():
        args.append(nc.dram_tensor(name, a.shape, _mybir.dt.from_np(a.dtype), kind="ExternalInput").ap())
    args.append(nc.dram_tensor("out_rows", arrays["in_x"].shape, F32, kind="ExternalOutput").ap())
    adaln_moe_program(nc, *args)
    r = _run(nc, [arrays], core_ids=[0])
    return r.results[0]["out_rows"]
```

```python
import concourse.bass as bass
from concourse import mybir
from contextlib import ExitStack

F32 = mybir.dt.float32
F32R = mybir.dt.float32r
BF16 = mybir.dt.bfloat16
I32 = mybir.dt.int32
U32 = mybir.dt.uint32
ALU = mybir.AluOpType
ACT = mybir.ActivationFunctionType
AX = mybir.AxisListType

P = 128
BANK = 512



def adaln_moe_program(nc, x, idx01, cw0, lnw12, wq, wk, wv, wo, qn_w, kn_w,
                      router_w, router_b, wg, wu, wd, cw1, gate_wT, gate_b,
                      w1s, w2s, w3s, w1r, w2r, w3r,
                      c_ident, c_identb, c_mask, c_cos, c_sin, c_rowno, c_sel0, c_sel1, out):
    B, C, D = x.shape
    BT = P // C
    T = B // BT
    NT = B * C
    KD = D // P
    DH = 128
    H = wq.shape[1] // DH
    KV = wk.shape[1] // DH
    REP = H // KV
    HALF = 32
    E0 = router_w.shape[1]
    E1 = gate_wT.shape[1]
    HID = w1r.shape[2]
    NR = E1 * HID // P
    NS = -(-HID // P)
    HREM = HID - P
    NH = NT // BANK
    EPS = 1e-6
    SCALE = float(DH) ** -0.5
    QK = H + KV
    NPIECE = (H + 2 * KV) * DH // BANK
    NWO = H * D // 1024
    TOPK0, TOPK1 = 2, 4
    NONE = -3.25e38

    x_v = x.rearrange("(t a) c d -> (a c) t d", a=BT)
    out_v = out.rearrange("(t a) c d -> (a c) t d", a=BT)

    top = ExitStack()
    with top:
        def sb(name, shape, dt=F32, ctx=top):
            return ctx.enter_context(nc.sbuf_tensor(name, shape, dt))

        def sem(name):
            return top.enter_context(nc.semaphore(name))

        bank = [top.enter_context(nc.psum_tensor(f"bank{i}", [P, BANK], F32)) for i in range(4)]
        qbanks = top.enter_context(nc.psum_tensor("qbanks", [P, 4, BANK], F32))

        xin = sb("xin", [P, T, D])
        x1 = sb("x1", [P, T + 1, D])
        wbd1 = sb("wbd1", [P, T, P])
        ident = sb("ident", [P, P])
        identb = sb("identb", [P, P], BF16)
        lnw = sb("lnw", [P, 2, KD])
        rbias = sb("rbias", [P, E0])
        gbias = sb("gbias", [P, E1])
        ssq = sb("ssq", [P, T])
        rms = sb("rms", [P, T + 1])
        mhalf = sb("mhalf", [P, T])
        rw = sb("rw", [P, KD, E0])
        rw_h = sb("rw_h", [P, KD, E0], F32R)
        rw_l = sb("rw_l", [P, KD, E0], F32R)
        gw = sb("gw", [P, KD, E1])
        gw_h = sb("gw_h", [P, KD, E1], F32R)
        gw_l = sb("gw_l", [P, KD, E1], F32R)
        sigT = sb("sigT", [max(E0, E1), NT])

        idx = sb("idx", [P, 2, T], I32)
        rowno = sb("rowno", [P, 1])
        cidx = sb("cidx", [P, 2, T], I32)
        crows = sb("crows", [P, 2, T, C])

        ph1 = ExitStack()
        wqkv_h = sb("wqkv_h", [P, NPIECE, KD, BANK], F32R, ph1)
        raw = ExitStack()
        wqkv = sb("wqkv", [P, NPIECE, KD, BANK], F32, raw)
        raw.close()
        wqkv_l = sb("wqkv_l", [P, NPIECE, KD, BANK], F32R, ph1)
        wo_h = sb("wo_h", [P, H, D], F32R, ph1)
        raw = ExitStack()
        wo_raw = sb("wo_raw", [P, H, D], F32, raw)
        raw.close()
        wo_l = sb("wo_l", [P, H, D], F32R, ph1)
        wa = sb("wa", [P, QK, DH], F32, ph1)
        wb = sb("wb", [P, QK, 2 * HALF], F32, ph1)
        rot = sb("rot", [P, QK, 2 * HALF], F32, ph1)
        qk = sb("qk", [P, QK, DH], F32, ph1)
        mask = sb("mask", [P, KV * BT * C], BF16, ph1)
        cosT = sb("cosT", [P, 2 * HALF], F32, ph1)
        sinT = sb("sinT", [P, 2 * HALF], F32, ph1)
        hn = sb("hn", [P, D], F32, ph1)
        hT_h = sb("hT_h", [P, KD, P], F32R, ph1)
        hT_l = sb("hT_l", [P, KD, P], F32R, ph1)
        junk = sb("junk", [P, 5, BANK], BF16, ph1)
        junkx = sb("junkx", [P, D], BF16, ph1)
        qkss = sb("qkss", [P, 5], F32, ph1)
        qkr = sb("qkr", [P, 3], F32, ph1)
        qT = sb("qT", [P, BT, KV, REP, C], F32, ph1)
        kT = sb("kT", [P, KV, BT, C], F32, ph1)
        v_h = [sb(f"v_h{i}", [P, KV * DH], F32R, ph1) for i in range(2)]
        v_l = [sb(f"v_l{i}", [P, KV * DH], F32R, ph1) for i in range(2)]
        sm = sb("sm", [P, KV * BT, C], F32, ph1)
        smax = sb("smax", [P, KV * BT], F32, ph1)
        prob = sb("prob", [P, KV * BT, C], F32, ph1)
        psm = sb("psm", [P, KV * BT], F32, ph1)
        pT_h = sb("pT_h", [P, KV, BT, P], F32R, ph1)
        pT_l = sb("pT_l", [P, KV, BT, P], F32R, ph1)
        oT_h = sb("oT_h", [P, H, BT, C], F32R, ph1)
        ph0 = ExitStack()
        wbd0 = sb("wbd0", [P, T, P], F32, ph0)
        ph0.close()
        oT_l = sb("oT_l", [P, H, BT, C], F32R, ph1)
        ph1.close()

        ph2 = ExitStack()
        wg_s = sb("wg_s", [P, E0, KD, P], F32, ph2)
        wu_s = sb("wu_s", [P, E0, KD, P], F32, ph2)
        wd_s = sb("wd_s", [P, E0, D], F32, ph2)
        w1_s = sb("w1_s", [P, KD, (NR + NS) * P], F32, ph2)
        w3_s = sb("w3_s", [P, KD, (NR + NS) * P], F32, ph2)
        sel0 = sb("sel0", [P, E0, P], BF16, ph2)
        sel1 = sb("sel1", [P, NR + NS, P], BF16, ph2)
        outT = sb("outT", [P, KD, NT], F32, ph2)
        hn2 = outT[:, :, :].rearrange("p k n -> p (k n)").rearrange("p (t d) -> p t d", d=D)
        featT_h = sb("featT_h", [P, KD, NT], F32R, ph2)
        featT_l = sb("featT_l", [P, KD, NT], F32R, ph2)
        w2_s = sb("w2_s", [P, NR + NS, D], F32, ph2)
        combT = sb("combT", [P, NT], BF16, ph2)
        wA_h = [sb(f"wA_h{i}", [P, KD, P], F32R, ph2) for i in range(2)]
        wA_l = [sb(f"wA_l{i}", [P, KD, P], F32R, ph2) for i in range(2)]
        wB_h = [sb(f"wB_h{i}", [P, KD, P], F32R, ph2) for i in range(2)]
        wB_l = [sb(f"wB_l{i}", [P, KD, P], F32R, ph2) for i in range(2)]
        wC_h = [sb(f"wC_h{i}", [P, D], F32R, ph2) for i in range(2)]
        wC_l = [sb(f"wC_l{i}", [P, D], F32R, ph2) for i in range(2)]
        gate_s = sb("gate_s", [P, BANK], F32, ph2)
        prod = sb("prod", [P, 2, BANK], F32, ph2)
        act = sb("act", [P, 2, BANK], F32, ph2)
        act_h = sb("act_h", [P, 4, BANK], F32R, ph2)
        act_l = sb("act_l", [P, 4, BANK], F32R, ph2)
        EM = max(E0, E1)
        sig = sb("sig", [P, T * EM], F32, ph2)
        score = sb("score", [P, T * EM], F32, ph2)
        top8 = sb("top8", [P, T, 8], F32, ph2)
        rest = sb("rest", [P, T * EM], F32, ph2)
        total = sb("total", [P, T], F32, ph2)
        comb = sb("comb", [P, T * EM], F32, ph2)
        comb3 = sb("comb3", [P, T, 3 * EM + 2], BF16, ph2)
        ph2.close()

        s_x = [sem("x_tile0_loaded"), sem("x_rest_loaded")]
        s_idx = sem("idx_loaded")
        s_cst = sem("ident_lnw_loaded")
        s_tab = [sem("table_parts_k_loaded"), sem("table_parts_q_loaded")]
        s_msk = sem("mask_loaded")
        s_cst2 = sem("router_loaded")
        s_sel = sem("sel_loaded")
        s_wst = [sem(f"piece_loaded{i}") for i in range(NPIECE + NWO)]
        s_cidx = sem("cond_rows_numbered")
        s_crow = [sem(f"cond0_rows_loaded{i}") for i in range(3)]
        s_crow1 = sem("cond1_rows_loaded")
        s_wbd = [sem(f"cond_blocks_placed{i}") for i in range(2)]
        s_zero = sem("wbd0_and_pads_zeroed")
        s_zero1 = sem("wbd1_zeroed")
        s_wh = sem("piece_high")
        s_wl = sem("piece_low")
        s_c0 = sem("cond0_rows")
        s_res = sem("cond0_copied")
        s_ssq = sem("squares_summed")
        s_ms = sem("mean_squares")
        s_rms = sem("rms_ready")
        s_hn = sem("hn_ready")
        s_hT = sem("hT_transposed")
        s_hTh = sem("hT_high")
        s_hTl = sem("hT_low")
        s_k = sem("k_ready")
        s_v = sem("v_ready")
        s_q = sem("q_ready")
        s_kss = sem("k_squares")
        s_qss = sem("q_squares")
        s_kms = sem("k_mean")
        s_qsum = sem("q_squares_summed")
        s_qms = sem("q_mean")
        s_kr = sem("k_rms")
        s_qr = sem("q_rms")
        s_kpost = sem("k_scaled")
        s_qpost = sem("q_scaled")
        s_krot = sem("k_rotated")
        s_qrot = sem("q_rotated")
        s_vh = sem("v_high")
        s_vc = sem("v_split")
        s_tr = sem("qk_transposed")
        s_trA = sem("kT_q0_q2_copied")
        s_trD = sem("q1_q3_copied")
        s_sc = sem("scores_ready")
        s_mx = sem("scores_max")
        s_sub = sem("scores_less_max")
        s_exp = sem("exp_done")
        s_sum2 = sem("exp_sums")
        s_sum = sem("exp_sums_inverted")
        s_p = sem("probs_ready")
        s_pT = sem("pT_transposed")
        s_pTh = sem("pT_high")
        s_pTl = sem("pT_low")
        s_pTz = sem("pT_zeroed")
        s_o = sem("oT_ready")
        s_oh = sem("oT_high")
        s_ol = sem("oT_low")
        s_wo = sem("wo_done")
        s_x1 = sem("x1_ready")
        s_dve = sem("dve_chain")
        s_w0 = [sem(f"moe0_w_loaded{i}") for i in range(2)]
        s_w1 = [sem("moe1_w_loaded")]
        s_pad = sem("shared_padding_zeroed")
        s_hn2 = sem("hn2_ready")
        s_x2 = sem("x2_ready")
        s_fT = [sem(f"featT_transposed{i}") for i in range(2)]
        s_fTh = [sem(f"featT_high{i}") for i in range(2)]
        s_fTl = [sem(f"featT_low{i}") for i in range(2)]
        s_rwh = sem("router_w_high")
        s_rwl = sem("router_w_low")
        s_sgT = [sem(f"sigmoid_transposed{i}") for i in range(2)]
        s_lg = [sem(f"logits{i}") for i in range(2)]
        s_sig = [sem(f"sigmoid{i}") for i in range(2)]
        s_cb3 = [sem(f"comb_parts{i}") for i in range(2)]
        s_cbT = [sem(f"combT_transposed{i}") for i in range(2)]
        s_cz = sem("combT_zeroed")
        s_cbc = [sem(f"combT_first_rows_copied{i}") for i in range(2)]
        s_cbd = [sem(f"combT_last_rows_copied{i}") for i in range(2)]
        s_wsh = [sem(f"chunk_wab_high{i}") for i in range(2)]
        s_wsl = [sem(f"chunk_wab_low{i}") for i in range(2)]
        s_wch = [sem(f"chunk_wc_high{i}") for i in range(2)]
        s_wcl = [sem(f"chunk_wc_low{i}") for i in range(2)]
        s_G = [sem(f"gate_ready{i}") for i in range(2)]
        s_U = [sem(f"up_ready{i}") for i in range(2)]
        s_BC = [sem(f"weight_rows_ready{i}") for i in range(2)]
        s_fst = [sem(f"first_ready{i}") for i in range(2)]
        s_prd = [sem(f"product_ready{i}") for i in range(2)]
        s_sil = [sem(f"silu_ready{i}") for i in range(2)]
        s_act = [sem(f"act_ready{i}") for i in range(2)]
        s_ah = [sem(f"act_high{i}") for i in range(2)]
        s_al = [sem(f"act_low{i}") for i in range(2)]
        s_D = [sem(f"down_done{i}") for i in range(2)]
        s_mx0 = [[sem(f"mixture{m}_half{i}_copied") for i in range(2)] for m in range(2)]
        s_xs = sem("residual_summed")
        s_bk = [sem(f"rows_back{i}") for i in range(2)]
        s_fin = sem("out_rows_ready")
        s_out = sem("out_stored")

        block = top.enter_context(nc.Block())

        qv = qbanks[:, :, :].rearrange("p b n -> p (b n)")
        bT, bK, bV, bP = bank[0], bank[1], bank[2], bank[3]
        X0, X1, X2, X3 = bank
        tr_bank = [X0, X1, X0, qbanks[:, 3, :], X0]
        o_bank = [X0, X1, X2, X3]
        NTR = len(tr_bank)
        FRONT = H // REP
        CUTS = (FRONT, 2 * FRONT, 2 * FRONT + 2)
        LOWS = 2

        back_banks = [bT, bK, bP]

        def back_bank(t):
            return back_banks[t % 3][:, 0:D]

        moes = [dict(sems=s_w0, runs=[(0, E0, True)], E=E0, K=TOPK0, sel=sel0),
                dict(sems=s_w1, runs=[(0, NR, False), (NR, NS, True)], E=E1, K=TOPK1, sel=sel1)]

        def chunk_weights(m, c):
            if m == 0:
                return (wg_s[:, bass.ds(c, 1), :, :].rearrange("p a k n -> p (a k) n"),
                        wu_s[:, bass.ds(c, 1), :, :].rearrange("p a k n -> p (a k) n"),
                        wd_s[:, bass.ds(c, 1), :].rearrange("p a n -> p (a n)"))
            return (w1_s[:, :, bass.ds(c * P, P)], w3_s[:, :, bass.ds(c * P, P)],
                    w2_s[:, bass.ds(c, 1), :].rearrange("p a n -> p (a n)"))

        @block.sync
        def _(sp):
            sp.dma_start(idx[:], idx01).then_inc(s_idx, 16)
            sp.dma_start(xin[:, 0, :], x_v[:, 0, :]).then_inc(s_x[0], 16)

            def load_piece(n):
                if n < NPIECE:
                    src = [wk, wv][n] if n < 2 else wq[:, (n - 2) * BANK:(n - 1) * BANK]
                    sp.dma_start(wqkv[:, n, :, :], src.rearrange("(k p) n -> p k n", p=P)).then_inc(s_wst[n], 16)
                else:
                    h = (n - NPIECE) * 4
                    sp.dma_start(wo_raw[:, h:h + 4, :],
                                 wo[h * DH:(h + 4) * DH, :].rearrange("(h p) n -> p h n", p=P)).then_inc(s_wst[n], 16)

            def row_to_all(v):
                return v.rearrange("(a n) -> a n", a=1).broadcast_to([P, v.shape[0]])

            load_piece(0)
            sp.dma_start(ident[:], c_ident).then_inc(s_cst, 16)
            sp.dma_start(lnw[:], lnw12).then_inc(s_cst, 16)
            load_piece(1)
            sp.wait_ge(s_crow[0], 16)
            sp.dma_start(xin[:, 1:T, :], x_v[:, 1:T, :]).then_inc(s_x[1], 16)
            sp.dma_start(cosT[:], c_cos).then_inc(s_tab[0], 16)
            sp.dma_start(sinT[:], c_sin).then_inc(s_tab[0], 16)
            sp.dma_start(wa[:, H:QK, :].rearrange("p h d -> p (h d)"), row_to_all(kn_w)).then_inc(s_tab[0], 16)
            load_piece(2)
            sp.dma_start(wa[:, 0:H, :].rearrange("p h d -> p (h d)"), row_to_all(qn_w)).then_inc(s_tab[1], 16)
            sp.dma_start(mask[:], c_mask.bitcast(BF16)).then_inc(s_msk, 16)
            sp.dma_start(identb[:], c_identb.bitcast(BF16)).then_inc(s_msk, 16)
            for n in range(3, NPIECE + NWO):
                sp.wait_ge(s_wst[n - 2], 16)
                load_piece(n)
            sp.dma_start(rw[:], router_w.rearrange("(k p) e -> p k e", p=P)).then_inc(s_cst2, 16)
            sp.dma_start(gw[:], gate_wT.rearrange("(k p) e -> p k e", p=P)).then_inc(s_cst2, 16)
            sp.dma_start(rbias[:], row_to_all(router_b)).then_inc(s_cst2, 16)
            sp.dma_start(gbias[:], row_to_all(gate_b)).then_inc(s_cst2, 16)

            sp.wait_ge(s_q, 4 * T)
            half = E0 // 2
            for lo, s in ((0, s_w0[0]), (half, s_w0[1])):
                e = slice(lo, lo + half)
                sp.dma_start(wg_s[:, e], wg[e].rearrange("e (k p) i -> p e k i", p=P)).then_inc(s, 16)
                sp.dma_start(wu_s[:, e], wu[e].rearrange("e (k p) i -> p e k i", p=P)).then_inc(s, 16)
                sp.dma_start(wd_s[:, e], wd[e].rearrange("e i d -> i e d")).then_inc(s, 16)

            def load_units(src, shr, dst):
                nr = NR * P
                for k in range(KD):
                    sp.dma_start(dst[:, k, 0:nr].rearrange("p (e c) -> p e c", e=E1),
                                 src[:, k * P:(k + 1) * P, :].rearrange("e p c -> p e c")).then_inc(s_w1[0], 16)
                sp.dma_start(dst[:, :, nr:nr + HID], shr.rearrange("(k p) c -> p k c", p=P)).then_inc(s_w1[0], 16)

            load_units(w1r, w1s, w1_s)
            sp.wait_ge(s_x1, T)
            sp.dma_start(sel0[:], c_sel0.bitcast(BF16)).then_inc(s_sel, 16)
            sp.dma_start(sel1[:], c_sel1.bitcast(BF16)).then_inc(s_sel, 16)
            load_units(w3r, w3s, w3_s)
            sp.wait_ge(s_ssq, 2 * T)
            sp.dma_start(w2_s[:, 0:NR, :],
                         w2r.rearrange("e c d -> (e c) d").rearrange("(n p) d -> p n d", p=P)).then_inc(s_w1[0], 16)
            sp.dma_start(w2_s[:, NR, :], w2s[0:P, :]).then_inc(s_w1[0], 16)
            sp.wait_ge(s_pad, 3)
            sp.dma_start(w2_s[0:HREM, NR + 1, :], w2s[P:HID, :]).then_inc(s_w1[0], 16)

            for t in range(T):
                sp.wait_ge(s_fin, t + 1)
                sp.dma_start(out_v[:, t, :], xin[:, t, :]).then_inc(s_out, 16)
            sp.wait_ge(s_out, 16 * T)

        @block.tensor
        def _(pe):
            def passes(dst, lh, ll, rh, rl, start, stop):
                pe.matmul(dst, lh, rh, start=start, stop=False)
                pe.matmul(dst, lh, rl, start=False, stop=False)
                return pe.matmul(dst, ll, rh, start=False, stop=stop)

            def cond0(lo, hi):
                for t in range(lo, hi):
                    if t >= 4:
                        pe.wait_ge(s_res, t - 3)
                    pe.matmul(qbanks[:, t % 4, 0:D], wbd0[:, t, :], xin[:, t, :],
                              start=True, stop=True).then_inc(s_c0, 1)

            def columns(dst, n):
                for k in range(KD):
                    last = passes(dst, hT_h[:, k, :], hT_l[:, k, :], wqkv_h[:, n, k, :], wqkv_l[:, n, k, :],
                                  k == 0, k == KD - 1)
                return last

            def rows_T(t):
                pe.wait_ge(s_hn, t + 1)
                for k in range(KD):
                    last = pe.transpose(X2[:, k * P:(k + 1) * P], hn[:, k * P:(k + 1) * P], ident[:])
                last.then_inc(s_hT, 1)

            def heads_T(n):
                for i in range(4):
                    h = H + i if n == 0 else (n - 1) * REP + i
                    last = pe.transpose(tr_bank[n][:, i * P:(i + 1) * P], qk[:, h, :], ident[:])
                last.then_inc(s_tr, 1)

            def scores(g):
                if g == 0:
                    pe.matmul(X1[:], identb[:], mask[:], start=True, stop=False)
                for a in range(BT):
                    u = (g * BT + a) * C
                    last = pe.matmul(X1[:, u:u + C], qT[:, a, g, :, :].rearrange("p r c -> p (r c)"), kT[:, g, a, :],
                                     start=False, stop=g == KV - 1 and a == BT - 1)
                if g == KV - 1:
                    last.then_inc(s_sc, 1)

            def probs_T():
                for g in range(KV):
                    last = pe.transpose(X1[:, g * P:(g + 1) * P],
                                        prob[:, g * BT:(g + 1) * BT, :].rearrange("p a c -> p (a c)"), ident[:])
                last.then_inc(s_pT, 1)

            def values(g, par):
                passes(o_bank[g][:], v_h[par][:, g * DH:(g + 1) * DH], v_l[par][:, g * DH:(g + 1) * DH],
                       pT_h[:, g, :, :].rearrange("p a n -> p (a n)"), pT_l[:, g, :, :].rearrange("p a n -> p (a n)"),
                       True, True).then_inc(s_o, 1)

            def output(lo, hi):
                for h in range(lo, hi):
                    last = passes(X3[:, 0:D], oT_h[:, h, :, :].rearrange("p a c -> p (a c)"),
                                  oT_l[:, h, :, :].rearrange("p a c -> p (a c)"),
                                  wo_h[:, h, :], wo_l[:, h, :], h == 0, h == H - 1)
                if hi == H:
                    last.then_inc(s_wo, 1)

            def features0(t):
                pe.wait_ge(s_hn2, t + 1)
                if t >= 4:
                    pe.wait_ge(s_fTl[0], t - 3)
                b = qbanks[:, t % 4, 0:KD * P].rearrange("p (k n) -> p k n", k=KD)
                for k in range(KD):
                    last = pe.transpose(b[:, k, :], hn2[:, t, k * P:(k + 1) * P], ident[:])
                last.then_inc(s_fT[0], 1)

            def step(t, par, q=True, mid=True, wo=True, t0=False, end=False):
                if mid and not wo:
                    pe.wait_ge(s_hTl, t + 1)
                    columns(X2[:], 0).then_inc(s_k, 1)
                    pe.wait_ge(s_vc, t)
                    columns(X3[:], 1).then_inc(s_v, 1)
                if mid:
                    pe.wait_ge(s_krot, t)
                    if wo:
                        pe.wait_ge(s_ol, KV * t - 7)
                    heads_T(0)
                    pe.wait_ge(s_qrot, 2 * t - 1)
                    if wo:
                        pe.wait_ge(s_ol, KV * t - 6)
                    heads_T(1)
                if q and (wo or not mid):
                    pe.wait_ge(s_hTl, t + 1)
                    if wo:
                        pe.wait_ge(s_ol, KV * t - 5)
                    if t0:
                        pe.wait_ge(s_wl, 1)
                    columns(X2[:], 0).then_inc(s_k, 1)
                if end:
                    pe.wait_ge(s_ol, KV * t - 4)
                    output(0, CUTS[0])
                if mid:
                    pe.wait_ge(s_trA, 3 * t - 2)
                    heads_T(2)
                if q and (wo or not mid):
                    if wo:
                        pe.wait_ge(s_ol, KV * t - 4)
                    if t0:
                        pe.wait_ge(s_wl, 2)
                    columns(X3[:], 1).then_inc(s_v, 1)
                def q_columns(lo, hi):
                    for n in range(lo, hi):
                        if t0:
                            pe.wait_ge(s_wl, n + 3)
                        columns(qbanks[:, n, :], n + 2).then_inc(s_q, 1)

                if t0:
                    pe.wait_ge(s_x[1], 16)
                    pe.wait_ge(s_wbd[0], 2 * BT)
                    cond0(1, T // 2)
                    pe.wait_ge(s_wbd[0], 3 * BT)
                    cond0(T // 2, T)
                    pe.wait_ge(s_res, T)
                if mid:
                    pe.wait_ge(s_trA, 3 * t - 1)
                    scores(0)
                    if end:
                        output(CUTS[0], CUTS[1])
                    pe.wait_ge(s_qrot, 2 * t)
                    heads_T(3)
                if q and (wo or not mid):
                    q_columns(0, 1)
                if mid:
                    pe.wait_ge(s_trD, 2 * t - 1)
                    heads_T(4)
                    scores(1)
                if q and (wo or not mid):
                    q_columns(1, 2)
                if mid:
                    pe.wait_ge(s_trA, 3 * t)
                    scores(2)
                    pe.wait_ge(s_trD, 2 * t)
                    scores(3)
                if mid and not wo:
                    q_columns(0, 3)
                    pe.wait_ge(s_p, t)
                    probs_T()
                if q:
                    q_columns(3 if mid and not wo else 2, 4)
                    pe.wait_ge(s_kpost, t + 1)
                    rows_T(t + 1)
                if wo:
                    if q:
                        pe.wait_ge(s_vc, t + 1)
                    if not end:
                        pe.wait_ge(s_ol, KV * t - 4)
                        output(0, FRONT)
                if end:
                    for i in range(4):
                        features0(i)
                    output(CUTS[1], CUTS[2])
                if mid and wo:
                    pe.wait_ge(s_p, t)
                    probs_T()
                if wo:
                    output(CUTS[2] if end else FRONT, H)
                if mid:
                    pe.wait_ge(s_pTl, t)
                    values(0, 1 - par)
                    values(1, 1 - par)
                    if q:
                        pe.wait_ge(s_hTl, t + 2)
                    values(2, 1 - par)
                    if wo:
                        pe.wait_ge(s_x1, t - 1)
                    else:
                        pe.wait_ge(s_vc, t + 1)
                    values(3, 1 - par)

            pe.wait_ge(s_x[0], 16)
            pe.wait_ge(s_wbd[0], BT)
            cond0(0, 1)
            pe.wait_ge(s_cst, 16 * 2)
            rows_T(0)
            step(0, 0, mid=False, wo=False, t0=True)
            pe.wait_ge(s_msk, 16 * 2)
            step(1, 1, wo=False)
            pe.wait_ge(s_wl, NPIECE + NWO)
            with pe.Fori(1, T // 2) as i:
                step(2 * i, 0)
                step(2 * i + 1, 1)
            step(T, 0, q=False, end=True)

            def features1(t):
                pe.wait_ge(s_x2, t + 1)
                if t >= 4:
                    pe.wait_ge(s_fTl[1], t - 3)
                b = qbanks[:, t % 4, 0:KD * P].rearrange("p (k n) -> p k n", k=KD)
                for k in range(KD):
                    last = pe.matmul(b[:, k, :], x1[:, t, k * P:(k + 1) * P], wbd1[:, t, :],
                                     start=True, stop=True)
                last.then_inc(s_fT[1], 1)

            def logits(m, hf):
                E, w_h, w_l = [(E0, rw_h, rw_l), (E1, gw_h, gw_l)][m]
                pe.wait_ge(s_fTl[m], (hf + 1) * T // 2)
                r = slice(hf * BANK, (hf + 1) * BANK)
                for k in range(KD):
                    last = passes([bV, bP][hf][0:E, :], w_h[:, k, :], w_l[:, k, :],
                                  featT_h[:, k, r], featT_l[:, k, r], k == 0, k == KD - 1)
                last.then_inc(s_lg[m], 1)

            def sigmoid_T(m, hf):
                E = moes[m]["E"]
                pe.wait_ge(s_sig[m], hf + 1)
                for t in range(hf * T // 2, (hf + 1) * T // 2):
                    last = pe.transpose(bV[:, t * E:(t + 1) * E], sigT[0:E, t * P:(t + 1) * P], ident[0:E, 0:E])
                if hf:
                    last.then_inc(s_sgT[m], 1)

            def weight_rows(m, E):
                pe.wait_ge(s_cb3[m], 1)
                n = 3 * E + 2 * m
                for t in range(T):
                    cb = qbanks[:, t // 4, :].bitcast(BF16)
                    last = pe.transpose(cb[0:n, (t % 4) * P:(t % 4 + 1) * P], comb3[:, t, 0:n], identb[:])
                    if t % 4 == 3:
                        last.then_inc(s_cbT[m], 1)

            def mixture(m):
                sel, E = moes[m]["sel"], moes[m]["E"]
                def down(q, n, start, stop):
                    j, hf = n // 2, n % 2
                    pe.wait_ge(s_al[m], 4 * q + n + 1)
                    if hf == 0:
                        pe.wait_ge(s_wcl[m], 2 * q + j + 1)
                    for d in range(KD):
                        cs = slice(d * P, (d + 1) * P)
                        last = passes(qbanks[:, d * NH + hf, :], wC_h[j][:, cs], wC_l[j][:, cs],
                                      act_h[:, n, :], act_l[:, n, :], start, stop)
                    last.then_inc(s_D[m], 1)

                def gate(q, n, first):
                    if n % 2 == 0:
                        pe.wait_ge(s_wsl[m], 2 * q + n // 2 + 1)
                    if not (first and n == 0):
                        pe.wait_ge(s_fst[m], 4 * q + n)
                    half_product(bT, wA_h[n // 2], wA_l[n // 2], n % 2).then_inc(s_G[m], 1)

                def up(q, n, first):
                    if not (first and n == 0):
                        pe.wait_ge(s_prd[m], 4 * q + n)
                    half_product(bK, wB_h[n // 2], wB_l[n // 2], n % 2).then_inc(s_U[m], 1)

                def half_product(b, w_h, w_l, hf):
                    r = slice(hf * BANK, (hf + 1) * BANK)
                    for k in range(KD):
                        last = passes(b[:], w_h[:, k, :], w_l[:, k, :], featT_h[:, k, r], featT_l[:, k, r],
                                      k == 0, k == KD - 1)
                    return last

                def weights(q, n, first):
                    if not (first and n < 2):
                        pe.wait_ge(s_act[m], 4 * q + n - 1)
                    r = slice(n % 2 * BANK, (n % 2 + 1) * BANK)
                    pe.matmul([bV, bP][n % 2][:], sel[:, bass.ds(2 * q + n // 2, 1), :].rearrange("p a n -> p (a n)"),
                              combT[:, r], start=True, stop=True).then_inc(s_BC[m], 1)

                def pair(q):
                    for n in range(4):
                        gate(q, n, False)
                        up(q, n, False)
                        weights(q, n, False)
                        if n >= 2:
                            down(q, n - 2, False, False)
                        else:
                            down(q - 1, n + 2, False, False)

                q_all = sum(n for _, n, _ in moes[m]["runs"]) // 2
                gate(0, 0, True)
                if m == 0:
                    features0(T - 1)
                logits(m, 1)
                up(0, 0, True)
                sigmoid_T(m, 0)
                sigmoid_T(m, 1)
                gate(0, 1, True)
                up(0, 1, True)
                weight_rows(m, E)
                if m == 0:
                    pe.wait_ge(s_sel, 32)
                pe.wait_ge(s_cbc[m], 1)
                weights(0, 0, True)
                pe.wait_ge(s_cbd[m], 1)
                weights(0, 1, True)
                for n in range(2, 4):
                    gate(0, n, True)
                    up(0, n, True)
                    weights(0, n, True)
                    down(0, n - 2, True, False)
                with pe.Fori(1, q_all) as q:
                    pair(q)
                down(q_all - 1, 2, False, True)
                down(q_all - 1, 3, False, True)

            def back(m, t):
                if t % 4 == 0:
                    pe.wait_ge(s_mx0[m][t // 4], 2)
                if t >= 3:
                    pe.wait_ge(s_x2 if m == 0 else s_fin, t - 2)
                for k in range(KD):
                    last = pe.transpose(back_bank(t)[:, k * P:(k + 1) * P], outT[:, k, t * P:(t + 1) * P], ident[:])
                last.then_inc(s_bk[m], 1)

            features0(4)
            features0(5)
            pe.wait_ge(s_rwl, 2)
            pe.wait_ge(s_ol, KV * T - 1)
            logits(0, 0)
            pe.wait_ge(s_ol, KV * T)
            output(0, 4)
            features0(T - 2)
            output(4, H)
            mixture(0)
            for t in range(3):
                back(0, t)
            pe.wait_ge(s_wbd[1], BT)
            pe.wait_ge(s_mx0[0][1], 2)
            for t in range(T):
                features1(t)
                if t + 3 < T:
                    back(0, t + 3)
                if t == 5:
                    logits(1, 0)
            mixture(1)
            for t in range(T):
                back(1, t)

        @block.scalar
        def _(act_e):
            act_e.dma_start(rowno[:], c_rowno).then_inc(s_idx, 16)

            def piece_high(n):
                act_e.wait_ge(s_wst[n], 16)
                if n < NPIECE:
                    nc.scalar.activation(wqkv_h[:, n, :, :], wqkv[:, n, :, :], ACT.Copy).then_inc(s_wh, 1)
                else:
                    r = slice(4 * (n - NPIECE), 4 * (n - NPIECE) + 4)
                    nc.scalar.activation(wo_h[:, r, :], wo_raw[:, r, :], ACT.Copy).then_inc(s_wh, 1)

            def squares0(lo, hi):
                for t in range(lo, hi):
                    act_e.wait_ge(s_res, t + 1)
                    if t:
                        act_e.wait_ge(s_ssq, t)
                    nc.scalar.activation(junkx[:], x1[:, t, :], ACT.Square,
                                         accum_out=ssq[:, t:t + 1]).then_inc(s_ssq, 1)

            def heads_copy(t, n):
                act_e.wait_ge(s_tr, NTR * t - 4 + n)
                if n == 0:
                    nc.scalar.activation(kT[:, :, :, :].rearrange("p g a c -> p (g a c)"), X0[:],
                                         ACT.Copy).then_inc(s_trA, 1)
                else:
                    nc.scalar.activation(qT[:, :, n - 1, :, :].rearrange("p a r c -> p r a c"),
                                         tr_bank[n][:, :].rearrange("p (r a c) -> p r a c", r=REP, a=BT),
                                         ACT.Copy).then_inc(s_trA, 1)

            def rows_high(t):
                act_e.wait_ge(s_hT, t + 1)
                for k in range(KD):
                    last = nc.scalar.activation(hT_h[:, k, :], X2[:, k * P:(k + 1) * P], ACT.Copy,
                                                scale=lnw[:, 0, k:k + 1])
                last.then_inc(s_hTh, 1)

            def q_squares(t, n, mid):
                act_e.wait_ge(s_q, 4 * t + n + 1)
                if mid and n == 0:
                    act_e.wait_ge(s_qsum, t)
                nc.scalar.activation(junk[:, n, :], qbanks[:, n, :], ACT.Square,
                                     accum_out=qkss[:, n:n + 1]).then_inc(s_qss, 1)

            def kv(t, par, mid):
                act_e.wait_ge(s_k, t + 1)
                if mid:
                    act_e.wait_ge(s_kms, t)
                nc.scalar.activation(junk[:, 4, :], X2[:], ACT.Square, accum_out=qkss[:, 4:5]).then_inc(s_kss, 1)
                act_e.wait_ge(s_v, t + 1)
                nc.scalar.activation(v_h[par][:], X3[:], ACT.Copy).then_inc(s_vh, 1)

            def features_high(m, t):
                act_e.wait_ge(s_fT[m], t + 1)
                b = qbanks[:, t % 4, 0:KD * P].rearrange("p (k n) -> p k n", k=KD)
                r = slice(t * P, (t + 1) * P)
                if m == 0:
                    for k in range(KD):
                        last = nc.scalar.activation(featT_h[:, k, r], b[:, k, :], ACT.Copy,
                                                    scale=lnw[:, 1, k:k + 1])
                    last.then_inc(s_fTh[m], 1)
                else:
                    nc.scalar.activation(featT_h[:, :, r], b, ACT.Copy).then_inc(s_fTh[m], 1)

            def step(t, par, q=True, mid=True, wo=True, t0=False, end=False):
                if mid and not wo:
                    kv(t, par, mid)
                if mid:
                    heads_copy(t, 0)
                    heads_copy(t, 1)
                if q and (wo or not mid):
                    kv(t, par, mid)
                if t0:
                    squares0(1, T // 2)
                    piece_high(3)
                    squares0(T // 2, T)
                    piece_high(4)
                    piece_high(5)
                if mid:
                    heads_copy(t, 3)
                if q and (wo or not mid):
                    for n in range(2):
                        q_squares(t, n, mid)
                if mid:
                    act_e.wait_ge(s_sub, t)
                    nc.scalar.activation(prob[:, :, :], sm[:, :, :], ACT.Exp, scale=SCALE).then_inc(s_exp, 1)
                if end:
                    for i in range(4):
                        features_high(0, i)
                def probs_high():
                    act_e.wait_ge(s_pT, t)
                    for a in range(BT):
                        r = slice(a * C, (a + 1) * C)
                        nc.scalar.activation(pT_h[r, :, a, :], X1[r, :].rearrange("p (g n) -> p g n", g=KV),
                                             ACT.Copy).then_inc(s_pTh, 1)

                if mid and not wo:
                    for n in range(3):
                        q_squares(t, n, mid)
                    probs_high()
                elif q:
                    q_squares(t, 2, mid)
                if q:
                    q_squares(t, 3, mid)
                    rows_high(t + 1)
                if mid and wo:
                    probs_high()
                if mid:
                    for g in range(KV):
                        act_e.wait_ge(s_o, KV * t - 3 + g)
                        nc.scalar.activation(oT_h[:, g * REP:(g + 1) * REP, :, :],
                                             o_bank[g][:, :].rearrange("p (a r c) -> p r a c", a=BT, c=C),
                                             ACT.Copy).then_inc(s_oh, 1)
                if wo:
                    act_e.wait_ge(s_x1, t - 1)
                    act_e.wait_ge(s_ssq, t + T - 2)
                    u = bass.ds(t - 2, 1)
                    nc.scalar.activation(junkx[:], x1[:, u, :].rearrange("p a d -> p (a d)"),
                                         ACT.Square, accum_out=ssq[:, u]).then_inc(s_ssq, 1)

            piece_high(0)
            piece_high(1)
            squares0(0, 1)
            act_e.wait_ge(s_cst, 16 * 2)
            rows_high(0)
            piece_high(2)
            step(0, 0, mid=False, wo=False, t0=True)
            for n in range(NPIECE, NPIECE + NWO):
                piece_high(n)
            act_e.wait_ge(s_pTz, 2)
            step(1, 1, wo=False)
            act_e.wait_ge(s_ms, 2)
            with act_e.Fori(1, T // 2) as i:
                step(2 * i, 0)
                step(2 * i + 1, 1)
            act_e.wait_ge(s_cst2, 16 * 4)
            nc.scalar.activation(rw_h[:], rw[:], ACT.Copy).then_inc(s_rwh, 1)
            nc.scalar.activation(gw_h[:], gw[:], ACT.Copy).then_inc(s_rwh, 1)
            step(T, 0, q=False, end=True)

            def sigmoid(m, hf):
                E = moes[m]["E"]
                act_e.wait_ge(s_lg[m], hf + 1)
                nc.scalar.activation(sigT[0:E, hf * BANK:(hf + 1) * BANK], [bV, bP][hf][0:E, :],
                                     ACT.Sigmoid).then_inc(s_sig[m], 1)

            def comb_copy(m, E):
                n = 3 * E + 2 * m
                act_e.wait_ge(s_cz, 1)
                act_e.wait_ge(s_cbT[m], 1)
                nc.scalar.activation(combT[0:n, 0:BANK], qbanks[0:n, 0, :].bitcast(BF16)[:, 0:BANK],
                                     ACT.Copy).then_inc(s_cbc[m], 1)

            def split_ab(m, c, j, later):
                if later:
                    act_e.wait_ge(s_U[m], 2 * c - 2)
                    act_e.wait_ge(s_wsl[m], c - 1)
                wa_s, wb_s, _ = chunk_weights(m, c)
                nc.scalar.activation(wA_h[j][:], wa_s, ACT.Copy)
                nc.scalar.activation(wB_h[j][:], wb_s, ACT.Copy).then_inc(s_wsh[m], 1)

            def run_mixture(m):
                q_all = sum(n for _, n, _ in moes[m]["runs"]) // 2

                def split_c(c, j, later):
                    if later:
                        act_e.wait_ge(s_D[m], 2 * c - 2)
                        act_e.wait_ge(s_wcl[m], c - 1)
                    nc.scalar.activation(wC_h[j][:], chunk_weights(m, c)[2], ACT.Copy).then_inc(s_wch[m], 1)

                def high(q, n, later):
                    act_e.wait_ge(s_act[m], 4 * q + n + 1)
                    if later:
                        act_e.wait_ge(s_D[m], 4 * q + n - 3)
                    nc.scalar.activation(act_h[:, n, :], act[:, n % 2, :], ACT.Copy).then_inc(s_ah[m], 1)

                def pair(q, first, second, gated, more):
                    for n in range(4):
                        s = 4 * q + n
                        if first and n == 0 and gated:
                            sigmoid(m, 1)
                        act_e.wait_ge(s_G[m], s + 1)
                        if not (first and n == 0):
                            act_e.wait_ge(s_prd[m], s)
                        nc.scalar.activation(gate_s[:], bT[:], ACT.Silu if gated else ACT.Copy).then_inc(s_fst[m], 1)
                        if first and n == 0 and not gated:
                            sigmoid(m, 1)
                        if first and n == 1:
                            comb_copy(m, moes[m]["E"])
                        if n:
                            high(q, n - 1, not first)
                        elif not first:
                            high(q - 1, 3, not second)
                        if not gated:
                            act_e.wait_ge(s_prd[m], s + 1)
                            nc.scalar.activation(prod[:, 1, :], prod[:, 0, :], ACT.Silu).then_inc(s_sil[m], 1)
                        if n == 0:
                            split_ab(m, 2 * q + 1, 1, not first)
                        if n == 1:
                            split_c(2 * q, 0, not first)
                        if n == 2 and more:
                            split_ab(m, 2 * q + 2, 0, True)
                        elif n == 2 and m == 0:
                            act_e.wait_ge(s_w1[0], 16 * 9)
                            act_e.wait_ge(s_pad, 3)
                            act_e.wait_ge(s_U[0], 4 * q_all - 2)
                            act_e.wait_ge(s_wsl[0], 2 * q_all - 1)
                            split_ab(1, 0, 0, False)
                        if n == 3:
                            split_c(2 * q + 1, 1, not first)

                if m == 0:
                    act_e.wait_ge(moes[m]["sems"][1], 16 * 3)
                runs = [(lo // 2, (lo + n) // 2, g) for lo, n, g in moes[m]["runs"]]
                for lo, hi, gated in runs:
                    if lo == 0:
                        pair(0, True, False, gated, True)
                        pair(1, False, True, gated, True)
                        lo = 2
                    end = hi - 1 if hi == q_all else hi
                    if end > lo:
                        with act_e.Fori(lo, end) as q:
                            pair(q, False, False, gated, True)
                    if hi == q_all:
                        pair(q_all - 1, False, False, gated, False)
                high(q_all - 1, 3, True)
                for i in range(2):
                    act_e.wait_ge(s_D[m], 4 * q_all - 1 + i)
                    nc.scalar.activation(outT[:, 0, i * BANK:(i + 1) * BANK], qbanks[:, i, :],
                                         ACT.Copy).then_inc(s_mx0[m][i], 1)

            features_high(0, 4)
            features_high(0, 5)
            act_e.wait_ge(s_w0[0], 16 * 3)
            split_ab(0, 0, 0, False)
            features_high(0, T - 2)
            sigmoid(0, 0)
            act_e.wait_ge(s_x1, T)
            act_e.wait_ge(s_ssq, 2 * T - 1)
            nc.scalar.activation(junkx[:], x1[:, T - 1, :], ACT.Square,
                                 accum_out=ssq[:, T - 1:T]).then_inc(s_ssq, 1)
            features_high(0, T - 1)
            run_mixture(0)
            for t in range(T):
                features_high(1, t)
                if t == 5:
                    sigmoid(1, 0)
            run_mixture(1)

        @block.gpsimd
        def _(pool):
            nc.gpsimd.memset(mhalf[:], -0.5).then_inc(s_zero, 1)
            nc.gpsimd.memset(wbd0[:], 0.0).then_inc(s_zero, 1)
            nc.gpsimd.memset(x1[:, T, :], 0.0).then_inc(s_zero, 1)
            nc.gpsimd.memset(rms[:, T:T + 1], 0.0).then_inc(s_zero, 1)

            def gather(m, t, s):
                nc.gpsimd.indirect_dma_start(
                    crows[:, m, t, :], None, [cw0, cw1][m].rearrange("s c d -> (s c) d"),
                    bass.IndirectOffsetOnAxis(ap=cidx[:, m, t:t + 1].bitcast(U32), axis=0),
                ).then_inc(s, 16)

            pool.wait_ge(s_cidx, 1)
            gather(0, 0, s_crow[0])
            for t in range(1, 4):
                gather(0, t, s_crow[1])
            pool.wait_ge(s_ms, 1)
            nc.gpsimd.tensor_tensor(rms[:, 0:1], rms[:, 0:1], mhalf[:, 0:1], ALU.pow).then_inc(s_rms, 1)
            for t in range(4, T):
                gather(0, t, s_crow[2])
            nc.gpsimd.memset(pT_h[:].bitcast(F32), 0.0).then_inc(s_pTz, 1)
            nc.gpsimd.memset(pT_l[:].bitcast(F32), 0.0).then_inc(s_pTz, 1)

            def split_ab(m, c, j):
                pool.wait_ge(s_wsh[m], c + 1)
                wa_s, wb_s, _ = chunk_weights(m, c)
                nc.gpsimd.tensor_tensor(wA_l[j][:], wa_s, wA_h[j][:].bitcast(F32), ALU.subtract)
                nc.gpsimd.tensor_tensor(wB_l[j][:], wb_s, wB_h[j][:].bitcast(F32),
                                        ALU.subtract).then_inc(s_wsl[m], 1)

            def root(lo, hi):
                pool.wait_ge(s_ms, 3 + max(0, lo - (T - 3)))
                nc.gpsimd.tensor_tensor(rms[:, lo:hi], rms[:, lo:hi], mhalf[:, lo:hi], ALU.pow).then_inc(s_rms, 1)

            def sum_rows(lo, hi):
                pool.wait_ge(s_x1, hi)
                for t in range(lo, hi):
                    nc.gpsimd.tensor_tensor(xin[:, t, :], xin[:, t, :], x1[:, t, :], ALU.add).then_inc(s_xs, 1)

            def step(t, par, q=True, mid=True, k=True, end=False):
                if q and k:
                    pool.wait_ge(s_kms, t + 1)
                    nc.gpsimd.tensor_tensor(qkr[:, 1:2], qkr[:, 1:2], mhalf[:, 0:1], ALU.pow).then_inc(s_kr, 1)
                    pool.wait_ge(s_kpost, t + 1)
                    nc.gpsimd.tensor_tensor(qk[:, H:QK, 0:2 * HALF], qk[:, H:QK, 0:2 * HALF], rot[:, H:QK, :],
                                            ALU.add).then_inc(s_krot, 1)
                if end:
                    root(0, T - 2)
                if q:
                    pool.wait_ge(s_qms, t + 1)
                    nc.gpsimd.tensor_tensor(qkr[:, 0:1], qkr[:, 0:1], mhalf[:, 0:1], ALU.pow).then_inc(s_qr, 1)
                if q:
                    for i in range(2):
                        r = slice(i * H // 2, (i + 1) * H // 2)
                        pool.wait_ge(s_qpost, 2 * t + i + 1)
                        nc.gpsimd.tensor_tensor(qk[:, r, 0:2 * HALF], qk[:, r, 0:2 * HALF], rot[:, r, :],
                                                ALU.add).then_inc(s_qrot, 1)

            pool.wait_ge(s_kms, 1)
            nc.gpsimd.tensor_tensor(qkr[:, 1:2], qkr[:, 1:2], mhalf[:, 0:1], ALU.pow).then_inc(s_kr, 1)
            pool.wait_ge(s_kpost, 1)
            nc.gpsimd.tensor_tensor(qk[:, H:QK, 0:2 * HALF], qk[:, H:QK, 0:2 * HALF], rot[:, H:QK, :],
                                    ALU.add).then_inc(s_krot, 1)
            pool.wait_ge(s_ms, 2)
            nc.gpsimd.tensor_tensor(rms[:, 1:T], rms[:, 1:T], mhalf[:, 1:T], ALU.pow).then_inc(s_rms, 1)
            step(0, 0, mid=False, k=False)
            step(1, 1)
            with pool.Fori(1, T // 2) as i:
                step(2 * i, 0)
                step(2 * i + 1, 1)
            step(T, 0, q=False, end=True)
            root(T - 2, T - 1)
            nr = NR * P
            pool.wait_ge(s_q, 4 * T)
            nc.gpsimd.memset(w1_s[:, :, nr + HID:], 0.0).then_inc(s_pad, 1)
            nc.gpsimd.memset(wbd1[:], 0.0).then_inc(s_zero1, 1)
            sum_rows(0, T // 2)
            split_ab(0, 0, 0)
            root(T - 1, T)
            sum_rows(T // 2, T)
            pool.wait_ge(s_ssq, 2 * T)
            nc.gpsimd.memset(combT[:], 0.0).then_inc(s_cz, 1)
            nc.gpsimd.memset(w3_s[:, :, nr + HID:], 0.0).then_inc(s_pad, 1)
            nc.gpsimd.memset(w2_s[:, NR + 1, :], 0.0).then_inc(s_pad, 1)

            def run_mixture(m):
                q_all = sum(n for _, n, _ in moes[m]["runs"]) // 2

                def split_c(c, j):
                    pool.wait_ge(s_wch[m], c + 1)
                    nc.gpsimd.tensor_tensor(wC_l[j][:], chunk_weights(m, c)[2], wC_h[j][:].bitcast(F32),
                                            ALU.subtract).then_inc(s_wcl[m], 1)

                def low(q, n):
                    pool.wait_ge(s_ah[m], 4 * q + n + 1)
                    nc.gpsimd.tensor_tensor(act_l[:, n, :], act[:, n % 2, :], act_h[:, n, :].bitcast(F32),
                                            ALU.subtract).then_inc(s_al[m], 1)

                def pair(q, first, more):
                    def rows1(n):
                        if m == 0 and first:
                            gather(1, n, s_crow1)
                        elif m == 0 and not more and n < 2:
                            gather(1, T // 2 + 2 * n, s_crow1)
                            gather(1, T // 2 + 2 * n + 1, s_crow1)

                    if not first:
                        low(q - 1, 3)
                    rows1(0)
                    split_ab(m, 2 * q + 1, 1)
                    low(q, 0)
                    rows1(1)
                    split_c(2 * q, 0)
                    low(q, 1)
                    rows1(2)
                    if more:
                        split_ab(m, 2 * q + 2, 0)
                    elif m == 0:
                        split_ab(1, 0, 0)
                    low(q, 2)
                    rows1(3)
                    split_c(2 * q + 1, 1)

                pair(0, True, True)
                with pool.Fori(1, q_all - 1) as q:
                    pair(q, False, True)
                pair(q_all - 1, False, False)
                low(q_all - 1, 3)

            run_mixture(0)
            run_mixture(1)

        @block.vector
        def _(dve):
            chain = [0]

            def then(ins):
                chain[0] += 1
                ins.then_inc(s_dve, 1)
                dve.wait_ge(s_dve, chain[0])

            V = nc.vector
            dve.wait_ge(s_idx, 16 * 2)
            V.tensor_scalar(cidx[:], idx[:], float(C), rowno[:, 0:1], ALU.mult, ALU.add).then_inc(s_cidx, 1)

            def piece_low(n):
                dve.wait_ge(s_wh, n + 1)
                if n < NPIECE:
                    V.tensor_tensor(wqkv_l[:, n, :, :], wqkv[:, n, :, :], wqkv_h[:, n, :, :].bitcast(F32),
                                    ALU.subtract).then_inc(s_wl, 1)
                else:
                    r = slice(4 * (n - NPIECE), 4 * (n - NPIECE) + 4)
                    V.tensor_tensor(wo_l[:, r, :], wo_raw[:, r, :], wo_h[:, r, :].bitcast(F32),
                                    ALU.subtract).then_inc(s_wl, 1)

            def place(m, wbd, lo, hi):
                for a in range(BT):
                    r = slice(a * C, (a + 1) * C)
                    V.tensor_copy(wbd[r, lo:hi, r], crows[r, m, lo:hi, :]).then_inc(s_wbd[m], 1)

            def rows0(lo, hi):
                for t in range(lo, hi):
                    dve.wait_ge(s_c0, t + 1)
                    V.tensor_copy(x1[:, t, :], qbanks[:, t % 4, 0:D]).then_inc(s_res, 1)

            dve.wait_ge(s_zero, 4)
            dve.wait_ge(s_crow[0], 16)
            place(0, wbd0, 0, 1)
            piece_low(0)
            rows0(0, 1)
            dve.wait_ge(s_ssq, 1)
            V.tensor_scalar(rms[:, 0:1], ssq[:, 0:1], 1.0 / D, EPS, ALU.mult, ALU.add).then_inc(s_ms, 1)
            dve.wait_ge(s_rms, 1)
            V.tensor_scalar(hn[:], x1[:, 0, :], rms[:, 0:1], None, ALU.mult).then_inc(s_hn, 1)
            piece_low(1)

            def tables(h0, h1):
                for lo_d, hi_d in ((0, HALF), (HALF, 0)):
                    last = V.tensor_tensor(wb[:, h0:h1, lo_d:lo_d + HALF], wa[:, h0:h1, hi_d:hi_d + HALF],
                                           sinT[:, lo_d:lo_d + HALF].unsqueeze(1).broadcast_to([P, h1 - h0, HALF]),
                                           ALU.mult)
                then(last)
                then(V.tensor_tensor(wa[:, h0:h1, 0:2 * HALF], wa[:, h0:h1, 0:2 * HALF],
                                     cosT[:, :].unsqueeze(1).broadcast_to([P, h1 - h0, 2 * HALF]), ALU.mult))

            def straight(r, src, h0, h1):
                V.scalar_tensor_tensor(qk[:, h0:h1, :].rearrange("p h d -> p (h d)"), src, r,
                                       wa[:, h0:h1, :].rearrange("p h d -> p (h d)"), ALU.mult, ALU.mult)

            def swapped(r, src, h0, h1):
                sv = src.rearrange("p (h d) -> p h d", d=DH)
                for lo, hi in ((0, HALF), (HALF, 0)):
                    last = V.scalar_tensor_tensor(rot[:, h0:h1, lo:lo + HALF], sv[:, :, hi:hi + HALF], r,
                                                  wb[:, h0:h1, lo:lo + HALF], ALU.mult, ALU.mult)
                return last

            def heads_copy(t, n):
                dve.wait_ge(s_tr, NTR * t - 4 + n)
                V.tensor_copy(qT[:, :, n - 1, :, :].rearrange("p a r c -> p r a c"),
                              tr_bank[n][:, :].rearrange("p (r a c) -> p r a c", r=REP, a=BT)).then_inc(s_trD, 1)

            def rows_low(t):
                dve.wait_ge(s_hTh, t + 1)
                for k in range(KD):
                    last = V.scalar_tensor_tensor(hT_l[:, k, :], X2[:, k * P:(k + 1) * P], lnw[:, 0, k:k + 1],
                                                  hT_h[:, k, :].bitcast(F32), ALU.mult, ALU.subtract)
                last.then_inc(s_hTl, 1)

            def mean_squares(lo, hi):
                dve.wait_ge(s_ssq, T + hi)
                V.tensor_scalar(rms[:, lo:hi], ssq[:, lo:hi], 1.0 / D, EPS, ALU.mult, ALU.add).then_inc(s_ms, 1)

            def scaled_rows(lo, hi):
                dve.wait_ge(s_rms, 3 + max(0, lo - (T - 3)))
                for t in range(lo, hi):
                    V.tensor_scalar(hn2[:, t, :], x1[:, t, :], rms[:, t:t + 1], None, ALU.mult).then_inc(s_hn2, 1)

            def features_low(m, t):
                dve.wait_ge(s_fTh[m], t + 1)
                b = qbanks[:, t % 4, 0:KD * P].rearrange("p (k n) -> p k n", k=KD)
                r = slice(t * P, (t + 1) * P)
                if m == 0:
                    for k in range(KD):
                        last = V.scalar_tensor_tensor(featT_l[:, k, r], b[:, k, :], lnw[:, 1, k:k + 1],
                                                      featT_h[:, k, r].bitcast(F32), ALU.mult, ALU.subtract)
                    last.then_inc(s_fTl[m], 1)
                else:
                    V.tensor_tensor(featT_l[:, :, r], b, featT_h[:, :, r].bitcast(F32),
                                    ALU.subtract).then_inc(s_fTl[m], 1)

            def step(t, par, q=True, mid=True, wo=True, t0=False, end=False):
                if q:
                    dve.wait_ge(s_kss, t + 1)
                    V.tensor_scalar(qkr[:, 1:2], qkss[:, 4:5], 1.0 / (KV * DH), EPS, ALU.mult, ALU.add).then_inc(s_kms, 1)
                if mid:
                    heads_copy(t, 2)
                if q:
                    dve.wait_ge(s_kr, t + 1)
                    straight(qkr[:, 1:2], X2[:], H, QK)
                    swapped(qkr[:, 1:2], X2[:], H, QK).then_inc(s_kpost, 1)
                    dve.wait_ge(s_vh, t + 1)
                    V.tensor_tensor(v_l[par][:], X3[:], v_h[par][:].bitcast(F32), ALU.subtract).then_inc(s_vc, 1)
                if mid and not wo:
                    piece_low(NPIECE)
                if end:
                    mean_squares(0, T - 2)
                if mid:
                    heads_copy(t, 4)
                if mid and not wo:
                    piece_low(NPIECE + 1)
                if t0:
                    rows0(1, T // 2)
                    dve.wait_ge(s_crow[2], 16 * (T - T // 2))
                    place(0, wbd0, T // 2, T)
                    piece_low(2)
                    rows0(T // 2, T)
                    piece_low(3)
                    dve.wait_ge(s_ssq, T)
                    V.tensor_scalar(rms[:, 1:T], ssq[:, 1:T], 1.0 / D, EPS, ALU.mult, ALU.add).then_inc(s_ms, 1)
                    piece_low(4)
                    dve.wait_ge(s_rms, 2)
                if q:
                    dve.wait_ge(s_hT, t + 1)
                    u = bass.ds(t + 1, 1)
                    V.tensor_scalar(hn[:], x1[:, u, :].rearrange("p a d -> p (a d)"), rms[:, u], None,
                                    ALU.mult).then_inc(s_hn, 1)
                if t0:
                    piece_low(5)
                    dve.wait_ge(s_tab[1], 16)
                    tables(0, H)
                if end:
                    scaled_rows(0, T - 2)
                if mid:
                    dve.wait_ge(s_sc, t)
                    scores = X1[:, :].rearrange("p (u c) -> p u c", c=C)
                    V.tensor_reduce(smax[:], scores, AX.X, ALU.max).then_inc(s_mx, 1)
                    dve.wait_ge(s_mx, t)
                    V.tensor_tensor(sm[:], scores, smax[:].unsqueeze(2).broadcast_to([P, KV * BT, C]),
                                    ALU.subtract).then_inc(s_sub, 1)
                    if not wo:
                        piece_low(NPIECE + 2)
                    dve.wait_ge(s_exp, t)
                    V.tensor_reduce(psm[:], prob[:], AX.X, ALU.add).then_inc(s_sum2, 1)
                    dve.wait_ge(s_sum2, t)
                    V.reciprocal(psm[:], psm[:]).then_inc(s_sum, 1)
                    dve.wait_ge(s_sum, t)
                    V.tensor_tensor(prob[:], prob[:], psm[:].unsqueeze(2).broadcast_to([P, KV * BT, C]),
                                    ALU.mult).then_inc(s_p, 1)
                    if end:
                        for i in range(LOWS):
                            features_low(0, i)
                    if not wo:
                        piece_low(NPIECE + 3)
                def probs_low():
                    for a in range(BT):
                        r = slice(a * C, (a + 1) * C)
                        dve.wait_ge(s_pTh, BT * t - 3 + a)
                        last = V.tensor_tensor(pT_l[r, :, a, :], X1[r, :].rearrange("p (g n) -> p g n", g=KV),
                                               pT_h[r, :, a, :].bitcast(F32), ALU.subtract)
                    last.then_inc(s_pTl, 1)

                if mid and not wo:
                    probs_low()
                if q:
                    dve.wait_ge(s_qss, 4 * t + 4)
                    V.tensor_reduce(qkr[:, 2:3], qkss[:, 0:4], AX.X, ALU.add).then_inc(s_qsum, 1)
                    dve.wait_ge(s_qsum, t + 1)
                    V.tensor_scalar(qkr[:, 0:1], qkr[:, 2:3], 1.0 / (H * DH), EPS, ALU.mult, ALU.add).then_inc(s_qms, 1)
                    rows_low(t + 1)
                if mid and wo:
                    probs_low()
                if q:
                    dve.wait_ge(s_qr, t + 1)
                    straight(qkr[:, 0:1], qv[:, 0:2 * BANK], 0, H // 2)
                    swapped(qkr[:, 0:1], qv[:, 0:2 * BANK], 0, H // 2).then_inc(s_qpost, 1)
                if wo:
                    dve.wait_ge(s_wo, t - 1)
                    u = x1[:, bass.ds(t - 2, 1), :].rearrange("p a d -> p (a d)")
                    V.tensor_tensor(u, u, X3[:, 0:D], ALU.add).then_inc(s_x1, 1)
                if end:
                    for i in range(LOWS, 4):
                        features_low(0, i)
                if mid:
                    for g in range(KV):
                        dve.wait_ge(s_oh, KV * t - 3 + g)
                        h = slice(g * REP, (g + 1) * REP)
                        V.tensor_tensor(oT_l[:, h, :, :], o_bank[g][:, :].rearrange("p (a r c) -> p r a c", a=BT, c=C),
                                        oT_h[:, h, :, :].bitcast(F32), ALU.subtract).then_inc(s_ol, 1)
                if q:
                    straight(qkr[:, 0:1], qv[:, 2 * BANK:], H // 2, H)
                    swapped(qkr[:, 0:1], qv[:, 2 * BANK:], H // 2, H).then_inc(s_qpost, 1)

            rows_low(0)
            dve.wait_ge(s_crow[1], 16 * 3)
            place(0, wbd0, 1, T // 2)
            dve.wait_ge(s_tab[0], 16 * 3)
            tables(H, QK)
            step(0, 0, mid=False, wo=False, t0=True)
            dve.wait_ge(s_pTz, 2)
            step(1, 1, wo=False)
            with dve.Fori(1, T // 2) as i:
                step(2 * i, 0)
                step(2 * i + 1, 1)
            dve.wait_ge(s_rwh, 2)
            V.tensor_tensor(rw_l[:], rw[:], rw_h[:].bitcast(F32), ALU.subtract).then_inc(s_rwl, 1)
            V.tensor_tensor(gw_l[:], gw[:], gw_h[:].bitcast(F32), ALU.subtract).then_inc(s_rwl, 1)
            step(T, 0, q=False, end=True)

            def first_product(m):
                dve.wait_ge(s_fst[m], 1)
                dve.wait_ge(s_U[m], 1)
                V.tensor_tensor(prod[:, 0, :], gate_s[:], bK[:], ALU.mult).then_inc(s_prd[m], 1)

            def router(m, E, K, bias):
                def v3(z):
                    return z[:, 0:T * E].rearrange("p (t e) -> p t e", e=E)

                def row(z):
                    return z.unsqueeze(2).broadcast_to([P, T, E])

                if m == 1:
                    first_product(m)
                dve.wait_ge(s_sgT[m], 1)
                if m == 0:
                    V.tensor_copy(v3(sig), v3(bV))
                then(V.tensor_tensor(v3(score), v3(bV), bias[:].unsqueeze(1).broadcast_to([P, T, E]), ALU.add))
                for t in range(T):
                    last = V.max(top8[:, t, :], score[:, t * E:(t + 1) * E])
                then(last)
                then(V.memset(top8[:, :, K:8], NONE))
                for t in range(T):
                    e = slice(t * E, (t + 1) * E)
                    last = V.match_replace(rest[:, e], top8[:, t, :], score[:, e], NONE)
                then(last)
                if m == 0:
                    first_product(m)
                then(V.scalar_tensor_tensor(v3(comb), v3(rest), NONE, v3(score if m else sig),
                                            ALU.is_equal, ALU.mult))
                then(V.tensor_reduce(total[:], v3(comb), AX.X, ALU.add))
                then(V.reciprocal(total[:], total[:]))
                then(V.tensor_tensor(v3(comb), v3(comb), row(total[:]), ALU.mult))
                then(V.tensor_copy(comb3[:, :, 0:E], v3(comb)))
                then(V.tensor_tensor(v3(comb), v3(comb), comb3[:, :, 0:E], ALU.subtract))
                then(V.tensor_copy(comb3[:, :, E:2 * E], v3(comb)))
                V.tensor_tensor(comb3[:, :, 2 * E:3 * E], v3(comb), comb3[:, :, E:2 * E],
                                ALU.subtract).then_inc(s_cb3[m], 1)
                n = 3 * E + 2 * m
                dve.wait_ge(s_cz, 1)
                dve.wait_ge(s_cbT[m], 2)
                V.tensor_copy(combT[0:n, BANK:], qbanks[0:n, 1, :].bitcast(BF16)[:, 0:BANK]).then_inc(s_cbd[m], 1)

            def run_mixture(m):
                q_all = sum(n for _, n, _ in moes[m]["runs"]) // 2

                def pair(q, first, gated):
                    for n in range(4):
                        s = 4 * q + n
                        if not (first and n == 0):
                            dve.wait_ge(s_fst[m], s + 1)
                            dve.wait_ge(s_U[m], s + 1)
                            dve.wait_ge(s_act[m], s)
                            V.tensor_tensor(prod[:, 0, :], gate_s[:], bK[:], ALU.mult).then_inc(s_prd[m], 1)
                        dve.wait_ge(s_BC[m], s + 1)
                        if gated:
                            dve.wait_ge(s_prd[m], s + 1)
                        else:
                            dve.wait_ge(s_sil[m], s + 1)
                        if not (first and n < 2):
                            dve.wait_ge(s_al[m], s - 1)
                        V.tensor_tensor(act[:, n % 2, :], prod[:, 0 if gated else 1, :], [bV, bP][n % 2][:],
                                        ALU.mult).then_inc(s_act[m], 1)

                pair(0, True, moes[m]["runs"][0][2])
                for lo, n, gated in moes[m]["runs"]:
                    lo, hi = max(lo // 2, 1), (lo + n) // 2
                    if hi - lo > 1:
                        with dve.Fori(lo, hi) as q:
                            pair(q, False, gated)
                    else:
                        pair(lo, False, gated)
                if m == 0:
                    dve.wait_ge(s_zero1, 1)
                    dve.wait_ge(s_crow1, 16 * T)
                    place(1, wbd1, 0, T)
                for i in range(2):
                    dve.wait_ge(s_D[m], 4 * q_all - 1 + i)
                    V.tensor_copy(outT[:, 1, i * BANK:(i + 1) * BANK], qbanks[:, 2 + i, :]).then_inc(s_mx0[m][i], 1)

            mean_squares(T - 2, T - 1)
            scaled_rows(T - 2, T - 1)
            for t in range(4, T - 1):
                features_low(0, t)
            dve.wait_ge(s_wo, T)
            V.tensor_tensor(x1[:, T - 1, :], x1[:, T - 1, :], X3[:, 0:D], ALU.add).then_inc(s_x1, 1)
            mean_squares(T - 1, T)
            scaled_rows(T - 1, T)
            features_low(0, T - 1)
            then(V.memset(comb3[:, :, 3 * E1:3 * E1 + 2], 1.0))
            router(0, E0, TOPK0, rbias)
            run_mixture(0)
            dve.wait_ge(s_xs, T)

            def second_rows(t):
                dve.wait_ge(s_bk[0], t + 1)
                V.tensor_tensor(x1[:, t, :], xin[:, t, :], back_bank(t), ALU.add).then_inc(s_x2, 1)

            second_rows(0)
            second_rows(1)
            for t in range(T):
                if t + 2 < T:
                    second_rows(t + 2)
                features_low(1, t)
            router(1, E1, TOPK1, gbias)
            run_mixture(1)
            for t in range(T):
                dve.wait_ge(s_bk[1], t + 1)
                V.tensor_tensor(xin[:, t, :], x1[:, t, :], back_bank(t), ALU.add).then_inc(s_fin, 1)


_INS = ["x", "indices", "L0_cond_weights", "ln_w", "L0_ffn_wq",
        "L0_ffn_wk", "L0_ffn_wv", "L0_ffn_wo", "L0_ffn_qnorm_w", "L0_ffn_knorm_w", "L0_ffn_router_w",
        "L0_ffn_router_bias", "L0_ffn_wg", "L0_ffn_wu", "L0_ffn_wd", "L1_cond_weights", "L1_ffn_gate_w",
        "L1_ffn_gate_b", "L1_ffn_w1_shared", "L1_ffn_w2_shared", "L1_ffn_w3_shared", "L1_ffn_w1_routed",
        "L1_ffn_w2_routed", "L1_ffn_w3_routed"]


def shape_constants():
    import numpy as np
    one = 0x3F80
    p = np.arange(128)
    pos = (p % 32).astype(np.float32)
    inv = (1.0 / np.float32(1000000.0) ** (np.arange(0, 64, 2, dtype=np.float32) / np.float32(64))).astype(np.float32)
    ang = pos[:, None] * inv[None, :]
    cos, sin = np.cos(ang), np.sin(ang)
    mask = np.tile(np.where(np.arange(32)[None, :] <= pos[:, None], 0, 0xFF62).astype(np.uint16), (1, 16))
    sel0 = np.zeros((128, 8, 128), np.uint16)
    for e in range(8):
        sel0[[e, 8 + e, 16 + e], e, :] = one
    sel1 = np.zeros((128, 24, 128), np.uint16)
    for c in range(22):
        e = (c * 128 + p) // 176
        for part in range(3):
            sel1[16 * part + e, c, p] = one
    sel1[48, 22:24, :] = one
    return {"c_ident": np.eye(128, dtype=np.float32), "c_identb": np.eye(128, dtype=np.uint16) * np.uint16(one),
            "c_mask": mask, "c_cos": np.concatenate([cos, cos], 1).astype(np.float32),
            "c_sin": np.concatenate([-sin, sin], 1).astype(np.float32), "c_rowno": pos[:, None],
            "c_sel0": sel0, "c_sel1": sel1}


def kernel(**inputs):
    import numpy as _np
    import concourse.bacc as _bacc
    from concourse import mybir as _mybir
    from concourse.bass_utils import run_bass_kernel_spmd as _run

    nc = _bacc.Bacc("TRN2", target_bir_lowering=False, num_devices=1)
    arrays, args = {}, []
    laid = dict(inputs)
    laid["indices"] = _np.stack([_np.repeat(inputs[name].reshape(8, 4).T, 32, axis=0)
                                 for name in ("itok_B_1_198", "itok_B_0_7")], axis=1)
    laid["ln_w"] = _np.stack([inputs[name].reshape(2, 128).T for name in ("L0_ffn_ln1_w", "L0_ffn_ln2_w")], axis=1)
    laid["L1_ffn_gate_w"] = inputs["L1_ffn_gate_w"].T
    for name in _INS:
        arrays[f"in_{name}"] = _np.ascontiguousarray(laid[name])
    for name, a in shape_constants().items():
        arrays[f"in_{name}"] = a
    for name, a in arrays.items():
        args.append(nc.dram_tensor(name, a.shape, _mybir.dt.from_np(a.dtype), kind="ExternalInput").ap())
    args.append(nc.dram_tensor("out_rows", arrays["in_x"].shape, F32, kind="ExternalOutput").ap())
    adaln_moe_program(nc, *args)
    r = _run(nc, [arrays], core_ids=[0])
    return r.results[0]["out_rows"]
```
